# Optimizing a Trainium2 kernel written in Bass

```python
import numpy as np
import jax
import jax.numpy as jnp

def _softmax(x, axis=-1):
    return jax.nn.softmax(x, axis=axis)

def _gelu(x):
    return jax.nn.gelu(x, approximate=True)

def _silu(x):
    return jax.nn.silu(x)

def _sigmoid(x):
    return jax.nn.sigmoid(x)

def _layernorm(x, axis=-1, eps=1e-05):
    m = jnp.mean(x, axis=axis, keepdims=True)
    v = jnp.var(x, axis=axis, keepdims=True)
    return (x - m) / jnp.sqrt(v + eps)

def _scatter_add(tgt, idx, src, axis=0):
    return tgt.at[idx].add(src)

def _segment_sum(src, seg, n):
    return jax.ops.segment_sum(src, seg, n)
kernel_name = 'mk_conv_attn_hybrid_d2_conv_nchw256_r2_78d916'

def setup_inputs(seed: int=0):
    np.random.seed(seed)
    _w = jnp.asarray

    def _rec_inputs():
        import jax
        import jax.numpy as jnp
        _gk = jax.random.key(seed)
        x = -0.000125 + 0.9999 * jax.random.normal(jax.random.fold_in(_gk, 1), (32, 128, 32, 32), jnp.float32)
        return x
    x = _rec_inputs()

    def _L0_conv_setup():
        import jax, jax.numpy as jnp
        from jax import lax
        import numpy as np
        EPS = 1e-05
        GROUPS = 32
        key = jax.random.key(seed)
        ks = jax.random.split(key, 6)
        B, C, H, W = (32, 128, 32, 32)
        S = 32
        CD = 2 * S
        x = jax.random.normal(ks[0], (B, C, H, W), dtype=jnp.float32)
        ln_w = jnp.ones((1, C, 1, 1), dtype=jnp.float32)
        ln_b = jnp.zeros((1, C, 1, 1), dtype=jnp.float32)
        w_bcdt = jax.random.normal(ks[1], (CD, C, 1, 1), dtype=jnp.float32) / np.sqrt(C)
        w_gw = jax.random.normal(ks[2], (CD, CD // GROUPS, 3, 3), dtype=jnp.float32) / np.sqrt(9 * CD // GROUPS)
        w_out = jax.random.normal(ks[3], (C, C, 1, 1), dtype=jnp.float32) / np.sqrt(C)
        A = jax.random.uniform(ks[4], (S,), dtype=jnp.float32, minval=1.0, maxval=16.0)
        return {'x': x, 'ln_w': ln_w, 'ln_b': ln_b, 'w_bcdt': w_bcdt, 'w_gw': w_gw, 'w_out': w_out, 'A': A}
    _L0_conv_all = _L0_conv_setup()
    _L0_conv_in = {k: v for k, v in _L0_conv_all.items() if k in ('ln_w', 'ln_b', 'w_bcdt', 'w_gw', 'w_out', 'A')}
    del _L0_conv_all

    def _L1_attn_setup():
        import jax, jax.numpy as jnp
        import numpy as np
        B, S, E, U = (4, 2048, 128, 64)
        NEG_FILL = -2.0 ** 32 + 1.0

        def _lrelu(z):
            return jnp.where(z >= 0, z, 0.2 * z)
        key = jax.random.key(seed)
        ks = jax.random.split(key, 4)
        sc_in = 1.0 / np.sqrt(E)
        return {'x': jax.random.normal(ks[0], (B, S, E), dtype=jnp.float32), 'Wq': jax.random.normal(ks[1], (E, U), dtype=jnp.float32) * sc_in, 'bq': jnp.zeros((U,), dtype=jnp.float32), 'Wk': jax.random.normal(ks[2], (E, U), dtype=jnp.float32) * sc_in, 'bk': jnp.zeros((U,), dtype=jnp.float32), 'Wv': jax.random.normal(ks[3], (E, E), dtype=jnp.float32) * sc_in, 'bv': jnp.zeros((E,), dtype=jnp.float32), 'gamma': jnp.ones((E,), dtype=jnp.float32), 'beta': jnp.zeros((E,), dtype=jnp.float32)}
    _L1_attn_all = _L1_attn_setup()
    _L1_attn_in = {k: v for k, v in _L1_attn_all.items() if k in ('Wq', 'bq', 'Wk', 'bk', 'Wv', 'bv', 'gamma', 'beta')}
    del _L1_attn_all

    def _L1_ffn_setup():
        import math
        import jax, jax.numpy as jnp
        import numpy as np
        CAPACITY_FACTOR = 1.25
        key = jax.random.key(seed)
        ks = jax.random.split(key, 5)
        B, L, D, F, E = (8, 4096, 128, 512, 8)
        h = jax.random.normal(ks[0], (B, L, D), dtype=jnp.float32)
        gate_w = jax.random.normal(ks[1], (D, E), dtype=jnp.float32) * 0.02
        gate_b = jnp.zeros((E,), dtype=jnp.float32)
        w1 = jax.random.normal(ks[2], (E, D, F), dtype=jnp.float32) * (1.0 / math.sqrt(D))
        b1 = jnp.zeros((E, F), dtype=jnp.float32)
        w2 = jax.random.normal(ks[3], (E, F, D), dtype=jnp.float32) * (1.0 / math.sqrt(F))
        b2 = jnp.zeros((E, D), dtype=jnp.float32)
        return {'h': h, 'gate_w': gate_w, 'gate_b': gate_b, 'w1': w1, 'b1': b1, 'w2': w2, 'b2': b2}
    _L1_ffn_all = _L1_ffn_setup()
    _L1_ffn_in = {k: v for k, v in _L1_ffn_all.items() if k in ('gate_w', 'gate_b', 'w1', 'b1', 'w2', 'b2')}
    del _L1_ffn_all
    return {'x': x, 'L0_conv_ln_w': _L0_conv_in['ln_w'], 'L0_conv_ln_b': _L0_conv_in['ln_b'], 'L0_conv_w_bcdt': _L0_conv_in['w_bcdt'], 'L0_conv_w_gw': _L0_conv_in['w_gw'], 'L0_conv_w_out': _L0_conv_in['w_out'], 'L0_conv_A': _L0_conv_in['A'], 'L1_attn_Wq': _L1_attn_in['Wq'], 'L1_attn_bq': _L1_attn_in['bq'], 'L1_attn_Wk': _L1_attn_in['Wk'], 'L1_attn_bk': _L1_attn_in['bk'], 'L1_attn_Wv': _L1_attn_in['Wv'], 'L1_attn_bv': _L1_attn_in['bv'], 'L1_attn_gamma': _L1_attn_in['gamma'], 'L1_attn_beta': _L1_attn_in['beta'], 'L1_ffn_gate_w': _L1_ffn_in['gate_w'], 'L1_ffn_gate_b': _L1_ffn_in['gate_b'], 'L1_ffn_w1': _L1_ffn_in['w1'], 'L1_ffn_b1': _L1_ffn_in['b1'], 'L1_ffn_w2': _L1_ffn_in['w2'], 'L1_ffn_b2': _L1_ffn_in['b2']}

def reference(x, L0_conv_ln_w, L0_conv_ln_b, L0_conv_w_bcdt, L0_conv_w_gw, L0_conv_w_out, L0_conv_A, L1_attn_Wq, L1_attn_bq, L1_attn_Wk, L1_attn_bk, L1_attn_Wv, L1_attn_bv, L1_attn_gamma, L1_attn_beta, L1_ffn_gate_w, L1_ffn_gate_b, L1_ffn_w1, L1_ffn_b1, L1_ffn_w2, L1_ffn_b2):
    import jax
    import jax.numpy as jnp

    def _L0_conv_ref(x, ln_w, ln_b, w_bcdt, w_gw, w_out, A):
        import jax, jax.numpy as jnp
        from jax import lax
        import numpy as np
        EPS = 1e-05
        GROUPS = 32
        B, C, H, W = x.shape
        N = H * W
        mean = jnp.mean(x, axis=1, keepdims=True)
        var = jnp.sum((x - mean) ** 2, axis=1, keepdims=True) / (C - 1)
        xn = (x - mean) / jnp.sqrt(var + EPS) * ln_w + ln_b
        bcdt = jnp.einsum('bchw,oc->bohw', xn, w_bcdt[:, :, 0, 0])
        bcdt = lax.conv_general_dilated(bcdt, w_gw, window_strides=(1, 1), padding=[(1, 1), (1, 1)], dimension_numbers=('NCHW', 'OIHW', 'NCHW'), feature_group_count=GROUPS)
        flat = bcdt.reshape(B, -1, N)
        BC, dt = jnp.split(flat, 2, axis=1)
        Asm = jax.nn.softmax(dt + A[None, :, None], axis=-1)
        AB = Asm * BC
        xf = x.reshape(B, C, N)
        h = jnp.einsum('bcn,bsn->bcs', xf, AB)
        y = jnp.einsum('bcs,bsn->bcn', h, BC)
        y = y.reshape(B, C, H, W)
        y = jnp.einsum('bchw,oc->bohw', y, w_out[:, :, 0, 0])
        return y + x

    def _L1_attn_ref(x, Wq, bq, Wk, bk, Wv, bv, gamma, beta):
        import jax, jax.numpy as jnp
        import numpy as np
        B, S, E, U = (4, 2048, 128, 64)
        NEG_FILL = -2.0 ** 32 + 1.0

        def _lrelu(z):
            return jnp.where(z >= 0, z, 0.2 * z)
        num_units = Wq.shape[-1]
        q = _lrelu(jnp.einsum('bse,eu->bsu', x, Wq) + bq)
        k = _lrelu(jnp.einsum('bse,eu->bsu', x, Wk) + bk)
        v = _lrelu(jnp.einsum('bse,ef->bsf', x, Wv) + bv)
        scores = jnp.einsum('bqu,bku->bqk', q, k) / jnp.sqrt(jnp.asarray(num_units, dtype=x.dtype))
        key_mask = jnp.sign(jnp.sum(jnp.abs(x), axis=-1))
        masked = jnp.where(key_mask[:, None, :] == 0, jnp.asarray(NEG_FILL, dtype=x.dtype), scores)
        probs = jax.nn.softmax(masked, axis=-1)
        out = jnp.einsum('bqk,bkf->bqf', probs, v) + x
        mean = jnp.mean(out, axis=-1, keepdims=True)
        var = jnp.mean(jnp.square(out - mean), axis=-1, keepdims=True)
        normalized = (out - mean) / jnp.sqrt(var + 1e-08)
        return gamma * normalized + beta

    def _L1_ffn_ref(h, gate_w, gate_b, w1, b1, w2, b2):
        import math
        import jax, jax.numpy as jnp
        import numpy as np
        CAPACITY_FACTOR = 1.25
        B, L, D = h.shape
        E = gate_w.shape[1]
        T = B * L
        C = max(1, math.ceil(CAPACITY_FACTOR * T / E))
        x = h.reshape(T, D)
        logits = x @ gate_w + gate_b
        probs = jax.nn.softmax(logits, axis=-1)
        idx = jnp.argmax(probs, axis=-1)
        prb = jnp.take_along_axis(probs, idx[:, None], axis=1)[:, 0]
        one_hot = jax.nn.one_hot(idx, E, dtype=jnp.float32)
        pos = (jnp.cumsum(one_hot, axis=0) * one_hot).sum(-1).astype(jnp.int32) - 1
        kept = pos < C
        pos_safe = jnp.where(kept, pos, C)
        buf = jnp.zeros((E, C, D), dtype=h.dtype).at[idx, pos_safe].set(x, mode='drop')
        hmid = jax.nn.relu(jnp.einsum('ecd,edf->ecf', buf, w1) + b1[:, None, :])
        ybuf = jnp.einsum('ecf,efd->ecd', hmid, w2) + b2[:, None, :]
        pos_g = jnp.minimum(pos, C - 1)
        y_tok = ybuf[idx, pos_g] * (prb * kept)[:, None]
        y = y_tok.reshape(B, L, D)
        y = jnp.nan_to_num(y, nan=0.0, posinf=10000.0, neginf=-10000.0)
        return y

    def _gn(v, G=32, eps=1e-05):
        B_, C_, H_, W_ = v.shape
        g = v.reshape(B_, G, C_ // G, H_, W_)
        m = jnp.mean(g, axis=(2, 3, 4), keepdims=True)
        s = jnp.var(g, axis=(2, 3, 4), keepdims=True)
        return ((g - m) / jnp.sqrt(s + eps)).reshape(v.shape)

    def _ln_c(v, eps=1e-06):
        m = jnp.mean(v, axis=1, keepdims=True)
        s = jnp.var(v, axis=1, keepdims=True)
        return (v - m) / jnp.sqrt(s + eps)

    def _ln_t(v, eps=1e-05):
        m = jnp.mean(v, axis=-1, keepdims=True)
        s = jnp.var(v, axis=-1, keepdims=True)
        return (v - m) / jnp.sqrt(s + eps)

    def _to_tokens(v):
        B_, C_, H_, W_ = v.shape
        return v.reshape(B_, C_, H_ * W_).transpose(0, 2, 1)

    def _from_tokens(t, like):
        B_, C_, H_, W_ = like.shape
        return t.transpose(0, 2, 1).reshape(B_, C_, H_, W_)
    x = _L0_conv_ref(x, L0_conv_ln_w, L0_conv_ln_b, L0_conv_w_bcdt, L0_conv_w_gw, L0_conv_w_out, L0_conv_A)
    t = _to_tokens(x)
    t = t + _L1_attn_ref(_ln_t(t), L1_attn_Wq, L1_attn_bq, L1_attn_Wk, L1_attn_bk, L1_attn_Wv, L1_attn_bv, L1_attn_gamma, L1_attn_beta)
    t = t + _L1_ffn_ref(_ln_t(t), L1_ffn_gate_w, L1_ffn_gate_b, L1_ffn_w1, L1_ffn_b1, L1_ffn_w2, L1_ffn_b2)
    x = _from_tokens(t, x)
    return x

_drawn_inputs = setup_inputs


def setup_inputs(seed=0):
    import zlib

    import numpy as np

    out = dict(_drawn_inputs(seed))
    spreads = {'L0_conv_ln_w': (1.0, 0.2),
     'L0_conv_ln_b': (0.0, 0.1),
     'L1_attn_bq': (0.0, 0.8),
     'L1_attn_bk': (0.0, 0.8),
     'L1_attn_bv': (0.0, 0.1),
     'L1_attn_gamma': (1.0, 0.2),
     'L1_attn_beta': (0.0, 0.1),
     'L1_ffn_gate_b': (0.0, 0.1),
     'L1_ffn_b1': (0.0, 0.8),
     'L1_ffn_b2': (0.0, 0.8)}
    factors = {'L0_conv_A': 8.0, 'L1_attn_Wq': 3.308, 'L1_attn_Wk': 2.988}
    for name, (base, spread) in spreads.items():
        noise = np.random.default_rng([zlib.crc32(name.encode()), seed]).standard_normal(out[name].shape)
        drawn = base * np.exp(spread * noise) if base else spread * noise
        out[name] = jnp.asarray(drawn.astype(out[name].dtype))
    for name, factor in factors.items():
        out[name] = (out[name] * factor).astype(out[name].dtype)
    return out
```

```python
from contextlib import ExitStack

import concourse.bass as bass
from concourse import mybir

F32 = mybir.dt.float32
BF16 = mybir.dt.bfloat16
I32 = mybir.dt.int32
ALU = mybir.AluOpType
ACT = mybir.ActivationFunctionType
AX = mybir.AxisListType.X

P = 128
B, C, H, W = 32, 128, 32, 32
N = H * W
NT = N // P
S = 32
HP, WP = H + 2, W + 2
U = 64
KA = U + 2
VA = C + 1
HALF = 512
E, F = 8, 512
FC = F // P
T = B * N
CAP = -(-5 * T // (4 * E))
ROW = C + 2
BLK = 512
G = BLK // P
NBLK = CAP // BLK
FILL_ROWS = 10
NFILL = E * CAP // (P * FILL_ROWS)
NO_TOKEN = 1 << 24
DROP = float(1 << 20)
NEG_FILL = -2.0 ** 32 + 1.0
NAN_CLIP = 10000.0


def early(b, n):
    return isinstance(b, int) and b < n


def wait_apart(eng, sem, value, passed):
    eng.wait_ge(sem, value)
    if not isinstance(value, int):
        eng.sem_inc(passed, 1)


def token_program(nc, x, ln_w, ln_b, w_bcdt_t, w_gw, w_out_t, A, Wq, bq, Wk, bk, Wv, bv, gamma, beta,
                  gate_w, gate_b, slots, tokens, sems):
    with ExitStack() as ctx:
        def sb(name, shape, dt=F32):
            return ctx.enter_context(nc.sbuf_tensor(name, shape, dt))

        def sem(name):
            return sems.enter_context(nc.semaphore(name))

        NW = 17

        ident = sb("ident", [P, P])
        ones_bf = sb("ones_bf", [P, P], BF16)
        before_bf = sb("before_bf", [P, P], BF16)
        onecol_bf = sb("onecol_bf", [P, 2], BF16)
        lnw_c, lnb_c = sb("lnw_c", [P, 1]), sb("lnb_c", [P, 1])
        wbc = sb("wbc", [P, 2, U])
        wgr = sb("wgr", [U, 2, 9])
        gmask = sb("gmask", [U, U])
        wexp = sb("wexp", [U, 9, U])
        wtap2 = sb("wtap2", [P, 3, U])
        wtap1 = sb("wtap1", [U, 3, U])
        wot = sb("wot", [P, C])
        A_c = sb("A_c", [U, 1])
        wq_s, wk_s, wv_s = sb("wq_s", [P, U]), sb("wk_s", [P, U]), sb("wv_s", [P, C])
        bq_c, bk_c = sb("bq_c", [U, 1]), sb("bk_c", [U, 1])
        bqs_c = sb("bqs_c", [U, 1])
        bv_r, gamma_r, beta_r = sb("bv_r", [P, C]), sb("gamma_r", [P, C]), sb("beta_r", [P, C])
        gw_s, gb_r = sb("gw_s", [P, E]), sb("gb_r", [P, E])
        kscale = sb("kscale", [KA, 1])
        neghalf = sb("neghalf", [P, NT])
        rank = sb("rank", [P, NT, E])
        eoff = sb("eoff", [P, NT, E])
        iota_i = sb("iota_i", [P, NT, E], I32)
        tokid = sb("tokid", [P, NT])
        tokid_i = sb("tokid_i", [P, NT], I32)
        fill = sb("fill", [P, FILL_ROWS, ROW])

        xs = [sb(f"xs{k}", [P, N]) for k in range(2)]
        xT = sb("xT", [P, NT, C])
        bn = sb("bn", [P, NT, 6])
        mv = sb("mv", [P, NT, 2])
        negm = sb("negm", [P, NT])
        rstd = sb("rstd", [P, NT])
        tmpv = sb("tmpv", [P, NT])
        xn = sb("xn", [P, NT, C])
        xnT = sb("xnT", [P, N])
        img = sb("img", [P, HP, WP])
        cd = sb("cd", [U, N])
        dts = sb("dts", [U, 4])
        dtr = sb("dtr", [U, 1])
        cdT = sb("cdT", [P, NT, U])
        abT = sb("abT", [P, NT, S])
        hs = sb("hs", [P, S])
        gs = sb("gs", [S, C])
        t1 = [sb(f"t1_{k}", [P, NT, C]) for k in range(2)]
        u1 = [sb(f"u1_{k}", [P, NT, C]) for k in range(2)]
        u1T = sb("u1T", [P, N])
        absu = sb("absu", [P, N], BF16)
        qa = [sb(f"qa{k}", [KA, N]) for k in range(2)]
        ka = [sb(f"ka{k}", [KA, N]) for k in range(2)]
        qb = [sb(f"qb{k}", [KA, N], BF16) for k in range(2)]
        kb = [sb(f"kb{k}", [KA, N], BF16) for k in range(2)]
        vz = sb("vz", [P, NT, C])
        qz, kz = sb("qz", [U, N]), sb("kz", [U, N])
        va = [sb(f"va{k}", [P, NT, VA]) for k in range(2)]
        mxs = sb("mxs", [P, NT, 2])
        nmx = sb("nmx", [P, NT])
        pT = [sb(f"pT{k}", [P, NT, HALF]) for k in range(2)]
        prv = sb("prv", [P, NT])
        o = [sb(f"o{k}", [P, NT, C]) for k in range(2)]
        bn3 = sb("bn3", [P, NT, 6])
        mv3 = sb("mv3", [P, NT, 2])
        negm3 = sb("negm3", [P, NT])
        rstd3 = sb("rstd3", [P, NT])
        tmpv3 = sb("tmpv3", [P, NT])
        rows = [sb(f"rows{k}", [P, NT, ROW]) for k in range(2)]
        u2 = sb("u2", [P, NT, C])
        u2T = sb("u2T", [P, N])
        lg = sb("lg", [P, NT, E])
        eg = sb("eg", [P, NT, E])
        r8 = sb("r8", [P, 6, NT])
        oh = sb("oh", [P, NT, E])
        oh_bf = sb("oh_bf", [P, NT, E], BF16)
        ra = sb("ra", [P, NT, E])
        rb = sb("rb", [P, NT, E])
        rc = sb("rc", [P, NT, E])
        rd = sb("rd", [P, NT, E])
        run = sb("run", [P, 1, E])
        slot_i = [sb(f"slot_i{k}", [P, NT], I32) for k in range(2)]

        work = ctx.enter_context(nc.psum_tensor("work", [P, 2, HALF], F32))
        mxp = [ctx.enter_context(nc.psum_tensor(f"mxp{k}", [P, HALF], F32)) for k in range(2)]
        stp = [ctx.enter_context(nc.psum_tensor(f"stp{k}", [P, HALF], F32)) for k in range(2)]
        pvp = [ctx.enter_context(nc.psum_tensor(f"pvp{k}", [P, HALF], F32)) for k in range(2)]
        workf = work[:].rearrange("p a b -> p (a b)")
        workt = work[:].rearrange("p a (t c) -> p (a t) c", c=C)

        names = """w_loaded wpe_loaded const_pool const_dve const_act fill_ready fill_done mask_ready wexp_ready
        taps_psum taps_ready
        x_turned xT_ready x_stats x_mv x_rstd xn_ready xn_turned xnT_ready bcdt_done img_lo img_hi conv_done
        dt_small cd_bc cd_exp dt_sumr asm_ready cd_turned cdT_ready abT_ready h_done h_ready g_done g_ready y_done t1_ready
        t_stats t_mv t_rstd u1_ready u1_turned u1T_ready absu_ready q_done qz_ready qa_ready qb_ready k_done kz_ready ka_ready
        kmask_ready kb_ready v_done vz_ready va_ready
        mx_done mx_read negmax_ready mrow_done mrow_ready st_done exp_ready pv_done pv_rinv o_ready
        o_stats o_mv o_rstd on_ready ong_ready onb_ready t2_ready t2_stats t2_mv t2_rstd u2_ready u2_turned u2T_ready
        gate_done lg_ready eg_ready gate_chain ohb_ready pos_done slot_ready rowid_ready rowprob_ready""".split()
        s = {n: sem(n) for n in names}
        passed = {n: sem(f"passed_{n}") for n in ("sp", "pool", "dve", "pe")}
        x_loaded, scattered, tokens_stored = ([sem(f"{n}{k}") for k in range(2)]
                                              for n in ("x_loaded", "scattered", "tokens_stored"))

        def bc_last(ap2, n):
            return ap2.unsqueeze(2).to_broadcast([ap2.shape[0], ap2.shape[1], n])

        def bc_mid(ap2, n):
            return ap2.unsqueeze(1).to_broadcast([ap2.shape[0], n, ap2.shape[1]])

        steps = [("st", 0, 0), "x_turn", ("st", 0, 1), "ln2", ("st", 0, 2), "xn_turn", ("st", 0, 3), "bcdt",
                 ("st", 0, 4), "conv", ("st", 0, 5), "ln3", ("st", 0, 6), ("st", 0, 7), "cd_turn",
                 ("pv", 0, 0), "h", ("pv", 0, 1), "g", ("pv", 0, 2), "y", ("pv", 0, 3), "u2_turn",
                 ("mrow", 1), ("st", 1, 0), "gate", ("st", 1, 1), ("st", 1, 2), "pos", ("st", 1, 3), "u1_turn",
                 ("st", 1, 4), "q", ("st", 1, 5), "k", ("st", 1, 6), "v", ("st", 1, 7),
                 ("pv", 1, 0), "scatter", ("pv", 1, 1), ("pv", 1, 2), ("pv", 1, 3), ("mrow", 0)]
        ROUTE = ("ln2", "ln3", "u2_turn", "gate", "pos", "scatter")

        def batch(i, c):
            return i * 2 + c, i + c // 2, c % 2

        def one_pass(one, i, c, route=True, attend=True, more=True):
            for st in steps:
                if st == ("mrow", 0):
                    if more:
                        if not attend:
                            one("mx_first", *batch(i, c + 1))
                        one(st, *batch(i, c + 1))
                elif isinstance(st, tuple):
                    if attend:
                        one(st, *batch(i, c))
                elif st in ROUTE:
                    if route:
                        one(st, *batch(i, c - 1))
                elif more:
                    one(st, *batch(i, c + 1))

        def passes(eng, one):
            one_pass(one, 0, -1, route=False, attend=False)
            one_pass(one, 0, 0, route=False)
            one_pass(one, 0, 1)
            one_pass(one, 0, 2)
            with eng.Fori(1, (B - 4) // 2) as i:
                one_pass(one, i, 1)
                one_pass(one, i, 2)
            one_pass(one, 0, B - 3)
            one_pass(one, 0, B - 2)
            one_pass(one, 0, B - 1, more=False)
            for st in ROUTE:
                one(st, *batch(0, B - 1))

        block = ctx.enter_context(nc.Block())

        @block.sync
        def _(sp):
            def w(dst, src):
                sp.dma_start(dst, src).then_inc(s["w_loaded"], 16)

            def load_x(b, k):
                sp.dma_start(xs[k][:], x[bass.ds(b, 1)].rearrange("o c n -> (o c) n")).then_inc(x_loaded[k], 16)

            load_x(0, 0)
            w(wbc[:, 0, :], w_bcdt_t)
            w(wbc[:, 1, :], w_bcdt_t)
            w(wgr[:], w_gw)
            w(wot[:], w_out_t)
            w(lnw_c[:], ln_w)
            w(lnb_c[:], ln_b)
            w(A_c[S:U, :], A.unsqueeze(1))
            w(wq_s[:], Wq)
            w(wk_s[:], Wk)
            w(wv_s[:], Wv)
            w(bq_c[:], bq.unsqueeze(1))
            w(bk_c[:], bk.unsqueeze(1))
            w(bv_r[:], bv.partition_broadcast(P))
            w(gamma_r[:], gamma.partition_broadcast(P))
            w(beta_r[:], beta.partition_broadcast(P))
            w(gw_s[:], gate_w)
            w(gb_r[:], gate_b.partition_broadcast(P))
            load_x(1, 1)
            sp.wait_ge(s["fill_ready"], 1)
            for f in range(NFILL):
                sp.dma_start(slots[f * P * FILL_ROWS:(f + 1) * P * FILL_ROWS].rearrange("(p r) d -> p (r d)", p=P),
                             fill[:].rearrange("p r d -> p (r d)")).then_inc(s["fill_done"], 16)

            def one(st, b, m, k):
                if st == "x_turn" and not early(b, 1) and not (isinstance(b, int) and b == B - 1):
                    wait_apart(sp, s["x_turned"], b, passed["sp"])
                    load_x(b + 1, 1 - k)
                if st == "u2_turn":
                    wait_apart(sp, s["t2_ready"], b + 1, passed["sp"])
                    sp.dma_start(tokens[bass.ds(b * N, N)].rearrange("(t p) c -> p t c", p=P),
                                 rows[k][:, :, 0:C]).then_inc(tokens_stored[k], 16)

            passes(sp, one)
            for k in range(2):
                sp.wait_ge(scattered[k], (B // 2) * NT * 16)
                sp.wait_ge(tokens_stored[k], (B // 2) * 16)

        @block.gpsimd
        def _(pool):
            g = nc.gpsimd
            cp = [0]

            def chain(ins):
                cp[0] += 1
                ins.then_inc(s["const_pool"], 1)
                pool.wait_ge(s["const_pool"], cp[0])

            chain(g.memset(fill[:], 0.0))
            chain(g.memset(fill[:, :, C:C + 1].bitcast(I32), NO_TOKEN))
            g.memset(neghalf[:], -0.5).then_inc(s["fill_ready"], 1)
            chain(g.memset(ident[:], 0.0))
            chain(g.affine_select(out=ident[:], in_=ident[:], pattern=[[-1, P]], compare_op=ALU.not_equal, fill=1.0,
                                  base=0, channel_multiplier=1))
            chain(g.memset(ones_bf[:], 1.0))
            chain(g.affine_select(out=before_bf[:], in_=ones_bf[:], pattern=[[1, P]], compare_op=ALU.is_gt, fill=0.0,
                                  base=0, channel_multiplier=-1))
            chain(g.memset(onecol_bf[:, 0:1], 0.0))
            chain(g.memset(onecol_bf[:, 1:2], 1.0))
            gm = gmask[:].rearrange("o (g i) -> o g i", i=2)
            chain(g.memset(gmask[:], 1.0))
            chain(g.affine_select(out=gm, in_=gm, pattern=[[-2, S], [0, 2]], compare_op=ALU.is_ge, fill=0.0,
                                  base=0, channel_multiplier=1))
            chain(g.affine_select(out=gm, in_=gm, pattern=[[2, S], [0, 2]], compare_op=ALU.is_ge, fill=0.0,
                                  base=1, channel_multiplier=-1))
            chain(g.iota(iota_i[:], pattern=[[0, NT], [1, E]], base=0, channel_multiplier=0))
            chain(g.tensor_scalar(rank[:], iota_i[:], -1.0, float(E), ALU.mult, ALU.add))
            chain(g.tensor_scalar(eoff[:], iota_i[:], float(CAP), 0.0, ALU.mult, ALU.add))
            chain(g.iota(tokid_i[:], pattern=[[P, NT]], base=0, channel_multiplier=1))
            chain(g.tensor_copy(tokid[:], tokid_i[:]))
            chain(g.memset(run[:], 0.0))
            chain(g.memset(kscale[U:KA, :], NEG_FILL))
            chain(g.memset(kscale[U:U + 1, :], 1.0))
            chain(g.memset(img[:], 0.0))
            for k in range(2):
                chain(g.memset(qa[k][U:KA, :], 1.0))
                chain(g.memset(qb[k][U:KA, :], 1.0))
                chain(g.memset(qb[k][U:U + 1, :], 0.0))
                chain(g.memset(va[k][:, :, C:VA], 1.0))
            g.memset(tmpv[:], 0.0).then_inc(s["mask_ready"], 1)

            def rsqrt(mv_, tmp_, negm_, rstd_, scale, eps, have, done, b):
                wait_apart(pool, have, b + 1, passed["pool"])
                g.tensor_scalar(tmp_[:], mv_[:, :, 1], scale, eps, ALU.mult, ALU.add).then_inc(done, 1)
                g.tensor_scalar(negm_[:], mv_[:, :, 0], -1.0, 0.0, ALU.mult, ALU.add).then_inc(done, 1)
                wait_apart(pool, done, b * 3 + 2, passed["pool"])
                g.tensor_tensor(rstd_[:], tmp_[:], neghalf[:], ALU.pow).then_inc(done, 1)
                wait_apart(pool, done, b * 3 + 3, passed["pool"])

            def normalise(dst, src, negm_, rstd_, done):
                for t in range(NT):
                    last = g.tensor_scalar(dst[:, t, :], src[:, t, :], negm_[:, t:t + 1], rstd_[:, t:t + 1],
                                           ALU.add, ALU.mult)
                last.then_inc(done, 1)

            def one(st, b, m, k):
                first = early(b, 1)
                if st == "x_turn":
                    rsqrt(mv, tmpv, negm, rstd, C / (C - 1.0), 1e-5, s["x_mv"], s["x_rstd"], b)
                    if not first:
                        wait_apart(pool, s["xn_turned"], b, passed["pool"])
                    normalise(xn, xT, negm, rstd, s["xn_ready"])
                if st == "cd_turn":
                    wait_apart(pool, s["cdT_ready"], b + 1, passed["pool"])
                    if not first:
                        wait_apart(pool, s["h_done"], b, passed["pool"])
                    g.tensor_tensor(abT[:], cdT[:, :, 0:S], cdT[:, :, S:U], ALU.mult).then_inc(s["abT_ready"], 1)
                if st == "y":
                    rsqrt(mv, tmpv, negm, rstd, 1.0, 1e-5, s["t_mv"], s["t_rstd"], b)
                    normalise(u1[k], t1[k], negm, rstd, s["u1_ready"])
                if st == "ln2":
                    rsqrt(mv3, tmpv3, negm3, rstd3, 1.0, 1e-8, s["o_mv"], s["o_rstd"], b)
                    normalise(o[k], o[k], negm3, rstd3, s["on_ready"])
                    wait_apart(pool, s["ong_ready"], b + 1, passed["pool"])
                    g.tensor_tensor(o[k][:], o[k][:], bc_mid(beta_r[:], NT), ALU.add).then_inc(s["onb_ready"], 1)
                if st == "ln3":
                    rsqrt(mv3, tmpv3, negm3, rstd3, 1.0, 1e-5, s["t2_mv"], s["t2_rstd"], b)
                    if not first:
                        wait_apart(pool, s["u2_turned"], b, passed["pool"])
                    normalise(u2, rows[k][:, :, 0:C], negm3, rstd3, s["u2_ready"])
                    if not early(b, 2):
                        wait_apart(pool, scattered[k], m * (NT * 16), passed["pool"])
                    g.tensor_copy(rows[k][:, :, C:C + 1].bitcast(I32), tokid[:].unsqueeze(2)).then_inc(s["rowid_ready"], 1)
                    wait_apart(pool, s["rowid_ready"], b * 2 + 1, passed["pool"])
                    g.tensor_scalar(tokid[:], tokid[:], float(N), 0.0, ALU.add, ALU.add).then_inc(s["rowid_ready"], 1)
                    wait_apart(pool, s["rowid_ready"], b * 2 + 2, passed["pool"])
                if st == "scatter":
                    wait_apart(pool, s["slot_ready"], b + 1, passed["pool"])
                    wait_apart(pool, s["rowprob_ready"], b + 1, passed["pool"])
                    wait_apart(pool, s["rowid_ready"], b * 2 + 1, passed["pool"])
                    if first:
                        wait_apart(pool, s["fill_done"], 16 * NFILL, passed["pool"])
                    for t in range(NT):
                        g.indirect_dma_start(out=slots, out_offset=bass.IndirectOffsetOnAxis(ap=slot_i[k][:, t:t + 1], axis=0),
                                             in_=rows[k][:, t, :], in_offset=None, bounds_check=E * CAP - 1,
                                             oob_is_err=False).then_inc(scattered[k], 16)

            passes(pool, one)

        @block.scalar
        def _(act):
            a = nc.scalar
            act.wait_ge(s["w_loaded"], 16 * NW)
            a.mul(bqs_c[:], bq_c[:], 0.125).then_inc(s["const_act"], 1)
            act.wait_ge(s["const_act"], 1)
            act.wait_ge(s["mask_ready"], 1)

            def one(st, b, m, k):
                first = early(b, 1)
                if st == "x_turn":
                    act.wait_ge(s["x_turned"], b + 1)
                    if not first:
                        act.wait_ge(s["t1_ready"], b)
                    a.copy(xT[:].rearrange("p t c -> p (t c)"), workf).then_inc(s["xT_ready"], 1)
                if st == "xn_turn":
                    act.wait_ge(s["xn_turned"], b + 1)
                    if not first:
                        act.wait_ge(s["bcdt_done"], b)
                    a.activation(xnT[:], workf, ACT.Identity, bias=lnb_c[:], scale=lnw_c[:]).then_inc(s["xnT_ready"], 1)
                if st == "bcdt":
                    act.wait_ge(s["bcdt_done"], b + 1)
                    if not first:
                        act.wait_ge(s["conv_done"], b)
                    a.copy(img[0:U, 1:H + 1, 1:W + 1],
                           workf[0:U, :].rearrange("p (h w) -> p h w", w=W)).then_inc(s["img_lo"], 1)
                if st == "conv":
                    act.wait_ge(s["conv_done"], b + 1)
                    if not first:
                        act.wait_ge(s["y_done"], b)
                    a.copy(cd[0:S, :], workf[0:S, :]).then_inc(s["cd_bc"], 1)
                    act.wait_ge(s["dt_small"], b * 3 + 3)
                    a.activation(cd[S:U, :], workf[S:U, :], ACT.Exp, bias=dts[S:U, 2:3],
                                 accum_out=dts[S:U, 3:4]).then_inc(s["cd_exp"], 1)
                if st == "cd_turn":
                    act.wait_ge(s["cd_turned"], b + 1)
                    if not first:
                        act.wait_ge(s["abT_ready"], b)
                    a.copy(cdT[:].rearrange("p t c -> p (t c)"), work[:, 0, :]).then_inc(s["cdT_ready"], 1)
                if st == "u1_turn":
                    act.wait_ge(s["u1_turned"], b + 1)
                    if not first:
                        act.wait_ge(s["v_done"], b)
                    a.copy(u1T[:], workf).then_inc(s["u1T_ready"], 1)
                    if not first:
                        act.wait_ge(s["k_done"], b)
                    a.activation(absu[:], workf, ACT.Abs).then_inc(s["absu_ready"], 1)
                if st == "q":
                    act.wait_ge(s["q_done"], b + 1)
                    if not first:
                        act.wait_ge(s["qa_ready"], b)
                    a.activation(qz[:], workf[0:U, :], ACT.Identity, bias=bqs_c[:], scale=0.125).then_inc(s["qz_ready"], 1)
                if st == "k":
                    act.wait_ge(s["k_done"], b + 1)
                    if not first:
                        act.wait_ge(s["ka_ready"], b)
                    a.activation(kz[:], workf[0:U, :], ACT.Identity, bias=bk_c[:], scale=1.0).then_inc(s["kz_ready"], 1)
                if isinstance(st, tuple) and st[0] == "st":
                    c, kt = st[1], st[2]
                    act.wait_ge(s["st_done"], b * 16 + (c * 8 + kt + 1))
                    if kt == 0 and not first:
                        act.wait_ge(s["pv_done"], b * 8 + (4 * c - 4))
                    a.activation(pT[c][:, kt, :], stp[kt % 2][:], ACT.Exp).then_inc(s["exp_ready"], 1)
                if st == "u2_turn":
                    act.wait_ge(s["u2_turned"], b + 1)
                    if not first:
                        act.wait_ge(s["gate_done"], b)
                    a.copy(u2T[:], workf).then_inc(s["u2T_ready"], 1)
                if st == "gate":
                    act.wait_ge(s["gate_chain"], b * 13 + 2)
                    a.activation(eg[:], lg[:], ACT.Exp).then_inc(s["eg_ready"], 1)

            passes(act, one)

        @block.vector
        def _(dve):
            v = nc.vector
            dve.wait_ge(s["w_loaded"], 16 * NW)
            dve.wait_ge(s["mask_ready"], 1)
            for ii in range(2):
                for tap in range(9):
                    wi = wexp[:, tap, :].rearrange("o (g i) -> o g i", i=2)[:, :, ii]
                    mi = gmask[:].rearrange("o (g i) -> o g i", i=2)[:, :, ii]
                    last = v.tensor_tensor(wi, mi, wgr[:, ii, tap:tap + 1].to_broadcast([U, S]), ALU.mult)
            last.then_inc(s["wexp_ready"], 1)
            dve.wait_ge(s["taps_psum"], 1)
            for kh in range(3):
                v.tensor_copy(wtap2[:, kh, :], work[:, 0, kh * U:(kh + 1) * U])
                last = v.tensor_copy(wtap1[:, kh, :], work[0:U, 1, kh * U:(kh + 1) * U])
            last.then_inc(s["taps_ready"], 1)

            def stats(src, bn_, mv_, got, done, b):
                for t in range(NT):
                    last = v.bn_stats(bn_[:, t, :], src[:, t, :])
                last.then_inc(got, 1)
                wait_apart(dve, got, b + 1, passed["dve"])
                for t in range(NT):
                    last = v.bn_aggr(mv_[:, t, :], bn_[:, t, :])
                last.then_inc(done, 1)

            def lrelu(dst, zs):
                return v.scalar_tensor_tensor(out=dst, in0=zs, scalar=0.2, in1=zs, op0=ALU.mult, op1=ALU.max)

            def mx_reads(b, c, n0, n1):
                for n in range(n0, n1):
                    qt = 4 * c + n // 2
                    dve.wait_ge(s["mx_done"], b * 16 + (c * 8 + n + 1))
                    v.reduce_max(mxs[:, qt, n % 2:n % 2 + 1], mxp[n % 2][:], AX).then_inc(s["mx_read"], 1)

            def negmax(b, c):
                dve.wait_ge(s["mx_read"], b * 16 + (c * 8 + 8))
                v.tensor_reduce(nmx[:, 4 * c:4 * c + 4], mxs[:, 4 * c:4 * c + 4, :], AX, ALU.max,
                                negate=True).then_inc(s["negmax_ready"], 1)

            def one(st, b, m, k):
                first = early(b, 1)
                if st == "x_turn":
                    dve.wait_ge(s["xT_ready"], b + 1)
                    if not first:
                        dve.wait_ge(s["t_rstd"], b * 3)
                    stats(xT, bn, mv, s["x_stats"], s["x_mv"], b)
                if st == "bcdt":
                    dve.wait_ge(s["bcdt_done"], b + 1)
                    if not first:
                        dve.wait_ge(s["conv_done"], b)
                    v.tensor_copy(img[U:P, 1:H + 1, 0:W],
                                  workf[U:P, :].rearrange("p (h w) -> p h w", w=W)).then_inc(s["img_hi"], 1)
                if st == "conv":
                    dve.wait_ge(s["cd_bc"], b + 1)
                    v.reduce_max(dts[S:U, 0:1], workf[S:U, :], AX).then_inc(s["dt_small"], 1)
                    dve.wait_ge(s["dt_small"], b * 3 + 1)
                    v.tensor_tensor(dts[S:U, 1:2], dts[S:U, 0:1], A_c[S:U, :], ALU.add).then_inc(s["dt_small"], 1)
                    dve.wait_ge(s["dt_small"], b * 3 + 2)
                    v.tensor_tensor(dts[S:U, 2:3], A_c[S:U, :], dts[S:U, 1:2], ALU.subtract).then_inc(s["dt_small"], 1)
                    dve.wait_ge(s["cd_exp"], b + 1)
                    v.reciprocal(dtr[S:U, :], dts[S:U, 3:4]).then_inc(s["dt_sumr"], 1)
                    dve.wait_ge(s["dt_sumr"], b + 1)
                    v.tensor_scalar(cd[S:U, :], cd[S:U, :], dtr[S:U, :], None, ALU.mult).then_inc(s["asm_ready"], 1)
                if st == "h":
                    dve.wait_ge(s["h_done"], b + 1)
                    v.tensor_copy(hs[:], work[:, 1, 0:S]).then_inc(s["h_ready"], 1)
                if st == "g":
                    dve.wait_ge(s["g_done"], b + 1)
                    v.tensor_copy(gs[:], work[0:S, 0, 0:C]).then_inc(s["g_ready"], 1)
                if st == "y":
                    dve.wait_ge(s["y_done"], b + 1)
                    if not early(b, 2):
                        dve.wait_ge(s["t2_ready"], b - 1)
                    v.tensor_tensor(t1[k][:], workt, xT[:], ALU.add).then_inc(s["t1_ready"], 1)
                    dve.wait_ge(s["t1_ready"], b + 1)
                    dve.wait_ge(s["x_rstd"], b * 3 + 3)
                    stats(t1[k], bn, mv, s["t_stats"], s["t_mv"], b)
                if st == "q":
                    dve.wait_ge(s["qz_ready"], b + 1)
                    lrelu(qa[k][0:U, :], qz[:]).then_inc(s["qa_ready"], 1)
                    dve.wait_ge(s["qa_ready"], b + 1)
                    v.tensor_copy(qb[k][0:U, :], qa[k][0:U, :]).then_inc(s["qb_ready"], 1)
                if st == "k":
                    dve.wait_ge(s["kz_ready"], b + 1)
                    lrelu(ka[k][0:U, :], kz[:]).then_inc(s["ka_ready"], 1)
                    v.tensor_scalar(ka[k][U:KA, :], workf[U:KA, :], 0.0, kscale[U:KA, :], ALU.is_equal,
                                    ALU.mult).then_inc(s["kmask_ready"], 1)
                    dve.wait_ge(s["kmask_ready"], b + 1)
                    v.tensor_copy(kb[k][:], ka[k][:]).then_inc(s["kb_ready"], 1)
                if st == "v":
                    dve.wait_ge(s["v_done"], b + 1)
                    v.tensor_tensor(vz[:], workt, bc_mid(bv_r[:], NT), ALU.add).then_inc(s["vz_ready"], 1)
                    dve.wait_ge(s["vz_ready"], b + 1)
                    lrelu(va[k][:, :, 0:C], vz[:]).then_inc(s["va_ready"], 1)
                if isinstance(st, tuple) and st[0] == "st" and st[1] == 0:
                    mx_reads(b, 1, st[2], st[2] + 1)
                if isinstance(st, tuple) and st[0] == "pv":
                    c, n = st[1], st[2]
                    qt = 4 * c + n
                    dve.wait_ge(s["pv_done"], b * 8 + (qt + 1))
                    v.reciprocal(prv[:, qt:qt + 1], pvp[qt % 2][:, C:VA]).then_inc(s["pv_rinv"], 1)
                    dve.wait_ge(s["pv_rinv"], b * 8 + (qt + 1))
                    v.scalar_tensor_tensor(out=o[k][:, qt, :], in0=pvp[qt % 2][:, 0:C], scalar=prv[:, qt:qt + 1],
                                           in1=u1[k][:, qt, :], op0=ALU.mult, op1=ALU.add).then_inc(s["o_ready"], 1)
                    if c == 1 and not (isinstance(b, int) and b == B - 1):
                        mx_reads(b + 1, 0, 2 * n, 2 * n + 2)
                if st == "mx_first":
                    mx_reads(b, 0, 0, 8)
                if st == "ln2":
                    dve.wait_ge(s["o_ready"], b * 8 + 8)
                    if not first:
                        dve.wait_ge(s["t2_rstd"], b * 3)
                    stats(o[k], bn3, mv3, s["o_stats"], s["o_mv"], b)
                    dve.wait_ge(s["on_ready"], b + 1)
                    v.tensor_tensor(o[k][:], o[k][:], bc_mid(gamma_r[:], NT), ALU.mult).then_inc(s["ong_ready"], 1)
                if st == "ln3":
                    dve.wait_ge(s["onb_ready"], b + 1)
                    if not early(b, 2):
                        dve.wait_ge(scattered[k], m * (NT * 16))
                        dve.wait_ge(tokens_stored[k], m * 16)
                    v.tensor_tensor(rows[k][:, :, 0:C], o[k][:], t1[k][:], ALU.add).then_inc(s["t2_ready"], 1)
                    dve.wait_ge(s["t2_ready"], b + 1)
                    stats(rows[k][:, :, 0:C], bn3, mv3, s["t2_stats"], s["t2_mv"], b)
                if isinstance(st, tuple) and st[0] == "mrow":
                    c = st[1]
                    negmax(b, c)
                    dve.wait_ge(s["mrow_done"], b * 2 + (c + 1))
                    v.tensor_copy(qa[k][U:U + 1, c * HALF:(c + 1) * HALF],
                                  stp[1][U:U + 1, :]).then_inc(s["mrow_ready"], 1)
                if st == "gate":
                    gc = s["gate_chain"]
                    cnt = [0]

                    def link(ins):
                        cnt[0] += 1
                        ins.then_inc(gc, 1)
                        dve.wait_ge(gc, b * 13 + cnt[0])
                    dve.wait_ge(s["gate_done"], b + 1)
                    lgw = work[:, 0, 0:NT * E].rearrange("p (t e) -> p t e", e=E)
                    link(v.tensor_tensor(ra[:], lgw, bc_mid(gb_r[:], NT), ALU.add))
                    v.reduce_max(r8[:, 0, :], ra[:], AX).then_inc(s["lg_ready"], 1)
                    dve.wait_ge(s["lg_ready"], b + 1)
                    link(v.tensor_tensor(lg[:], ra[:], bc_last(r8[:, 0, :], E), ALU.subtract))
                    dve.wait_ge(s["eg_ready"], b + 1)
                    link(v.reduce_sum(r8[:, 1, :], eg[:], AX))
                    link(v.reduce_max(r8[:, 2, :], eg[:], AX))
                    link(v.reciprocal(r8[:, 3, :], r8[:, 1, :]))
                    if not early(b, 2):
                        dve.wait_ge(scattered[k], m * (NT * 16))
                    v.tensor_tensor(rows[k][:, :, C + 1], r8[:, 2, :], r8[:, 3, :], ALU.mult).then_inc(s["rowprob_ready"], 1)
                    link(v.tensor_tensor(ra[:], eg[:], bc_last(r8[:, 2, :], E), ALU.is_equal))
                    link(v.tensor_tensor(rb[:], ra[:], rank[:], ALU.mult))
                    link(v.reduce_max(r8[:, 4, :], rb[:], AX))
                    link(v.tensor_tensor(oh[:], rb[:], bc_last(r8[:, 4, :], E), ALU.is_equal))
                    v.tensor_copy(oh_bf[:], oh[:]).then_inc(s["ohb_ready"], 1)
                if st == "pos":
                    gc = s["gate_chain"]
                    cnt = [9]

                    def link2(ins):
                        cnt[0] += 1
                        ins.then_inc(gc, 1)
                        dve.wait_ge(gc, b * 13 + cnt[0])
                    dve.wait_ge(s["pos_done"], b + 1)
                    pw = work[:, 1, 0:(NT + 1) * E].rearrange("p (t e) -> p t e", e=E)
                    link2(v.tensor_tensor(ra[:], pw[:, 0:NT, :], run[:].to_broadcast([P, NT, E]), ALU.add))
                    v.tensor_tensor(run[:], pw[:, NT:NT + 1, :], run[:], ALU.add)
                    v.tensor_tensor(rb[:], ra[:], oh[:], ALU.mult)
                    link2(v.tensor_tensor(rc[:], ra[:], eoff[:], ALU.add))
                    v.reduce_sum(r8[:, 4, :], rb[:], AX)
                    link2(v.tensor_tensor(rd[:], rc[:], oh[:], ALU.mult))
                    v.tensor_scalar(r8[:, 4, :], r8[:, 4, :], float(CAP), DROP, ALU.is_ge, ALU.mult)
                    link2(v.reduce_sum(r8[:, 5, :], rd[:], AX))
                    v.tensor_tensor(slot_i[k][:], r8[:, 4, :], r8[:, 5, :], ALU.add).then_inc(s["slot_ready"], 1)

            passes(dve, one)

        @block.tensor
        def _(pe):
            mm = nc.tensor.matmul
            pe.wait_ge(s["w_loaded"], 16 * NW)
            pe.wait_ge(s["mask_ready"], 1)
            pe.wait_ge(s["wexp_ready"], 1)
            for kh in range(3):
                nc.tensor.transpose(work[:, 0, kh * U:(kh + 1) * U],
                                    wexp[:, 3 * kh:3 * kh + 2, :].rearrange("o a i -> o (a i)"), ident[0:U, 0:U])
                last = nc.tensor.transpose(work[0:U, 1, kh * U:(kh + 1) * U], wexp[:, 3 * kh + 2, :], ident[0:U, 0:U])
            last.then_inc(s["taps_psum"], 1)
            pe.wait_ge(s["taps_ready"], 1)

            def turn(src, done):
                for t in range(NT):
                    last = nc.tensor.transpose(workt[:, t, :], src(t), ident[:])
                last.then_inc(done, 1)

            def mx_items(b, k, c, n0, n1):
                for n in range(n0, n1):
                    qt = 4 * c + n // 2
                    if not (isinstance(b, int) and b == 0 and c == 0 and n < 2):
                        pe.wait_ge(s["mx_read"], b * 16 + (c * 8 + n - 1))
                    mm(mxp[n % 2][:], qb[k][:, qt * P:(qt + 1) * P], kb[k][:, (n % 2) * HALF:(n % 2 + 1) * HALF],
                       start=True, stop=True).then_inc(s["mx_done"], 1)

            def one(st, b, m, k):
                first = early(b, 1)
                if st == "x_turn":
                    pe.wait_ge(x_loaded[k], m * 16 + 16)
                    if not first:
                        pe.wait_ge(s["vz_ready"], b)
                    turn(lambda t: xs[k][:, t * P:(t + 1) * P], s["x_turned"])
                if st == "xn_turn":
                    pe.wait_ge(s["xn_ready"], b + 1)
                    turn(lambda t: xn[:, t, :], s["xn_turned"])
                if st == "bcdt":
                    pe.wait_ge(s["xnT_ready"], b + 1)
                    for h in range(2):
                        last = mm(work[:, h, :], wbc[:].rearrange("p a u -> p (a u)"), xnT[:, h * HALF:(h + 1) * HALF],
                                  start=True, stop=True)
                    last.then_inc(s["bcdt_done"], 1)
                if st == "conv":
                    pe.wait_ge(s["img_lo"], b + 1)
                    pe.wait_ge(s["img_hi"], b + 1)
                    for h in range(2):
                        r0 = h * (H // 2)
                        for kh in range(3):
                            mm(work[0:U, h, :], wtap2[:, kh, :], img[:, r0 + kh:r0 + kh + H // 2, 0:W],
                               start=(kh == 0), stop=False)
                            last = mm(work[0:U, h, :], wtap1[:, kh, :], img[0:U, r0 + kh:r0 + kh + H // 2, 2:2 + W],
                                      start=False, stop=(kh == 2))
                    last.then_inc(s["conv_done"], 1)
                if st == "cd_turn":
                    wait_apart(pe, s["asm_ready"], b + 1, passed["pe"])
                    for t in range(NT):
                        last = nc.tensor.transpose(work[:, 0, t * U:(t + 1) * U], cd[:, t * P:(t + 1) * P],
                                                   ident[0:U, 0:U])
                    last.then_inc(s["cd_turned"], 1)
                if st == "h":
                    pe.wait_ge(s["abT_ready"], b + 1)
                    for t in range(NT):
                        last = mm(work[:, 1, 0:S], xT[:, t, :], abT[:, t, :], start=(t == 0), stop=(t == NT - 1))
                    last.then_inc(s["h_done"], 1)
                if st == "g":
                    pe.wait_ge(s["h_ready"], b + 1)
                    mm(work[0:S, 0, 0:C], hs[:], wot[:], start=True, stop=True).then_inc(s["g_done"], 1)
                if st == "y":
                    pe.wait_ge(s["g_ready"], b + 1)
                    for t in range(NT):
                        last = mm(workt[:, t, :], cd[0:S, t * P:(t + 1) * P], gs[:], start=True, stop=True)
                    last.then_inc(s["y_done"], 1)
                if st == "u1_turn":
                    pe.wait_ge(s["u1_ready"], b + 1)
                    if not early(b, 2):
                        pe.wait_ge(s["gate_chain"], b * 13 - 15)
                    turn(lambda t: u1[k][:, t, :], s["u1_turned"])
                if st == "q":
                    pe.wait_ge(s["absu_ready"], b + 1)
                    for h in range(2):
                        last = mm(work[0:U, h, :], wq_s[:], u1T[:, h * HALF:(h + 1) * HALF], start=True, stop=True)
                    last.then_inc(s["q_done"], 1)
                if st == "k":
                    pe.wait_ge(s["qz_ready"], b + 1)
                    for h in range(2):
                        mm(work[0:U, h, :], wk_s[:], u1T[:, h * HALF:(h + 1) * HALF], start=True, stop=True)
                        last = mm(work[U:KA, h, :], onecol_bf[:], absu[:, h * HALF:(h + 1) * HALF], start=True, stop=True)
                    last.then_inc(s["k_done"], 1)
                if st == "v":
                    pe.wait_ge(s["kmask_ready"], b + 1)
                    for t in range(NT):
                        last = mm(workt[:, t, :], u1T[:, t * P:(t + 1) * P], wv_s[:], start=True, stop=True)
                    last.then_inc(s["v_done"], 1)
                if isinstance(st, tuple) and st[0] == "st":
                    c, kt = st[1], st[2]
                    if kt == 0:
                        pe.wait_ge(s["mrow_ready"], b * 2 + (c + 1))
                    if not (first and c == 0 and kt < 2):
                        pe.wait_ge(s["exp_ready"], b * 16 + (c * 8 + kt - 1))
                    mm(stp[kt % 2][:], ka[k][:, kt * P:(kt + 1) * P], qa[k][:, c * HALF:(c + 1) * HALF],
                       start=True, stop=True).then_inc(s["st_done"], 1)
                    if c == 0:
                        mx_items(b, k, 1, kt, kt + 1)
                if isinstance(st, tuple) and st[0] == "mrow":
                    c = st[1]
                    pe.wait_ge(s["negmax_ready"], b * 2 + (c + 1))
                    if not (first and c == 0):
                        pe.wait_ge(s["exp_ready"], b * 16 + c * 8)
                    for n in range(4):
                        qt = 4 * c + n
                        last = mm(stp[1][U:U + 1, n * P:(n + 1) * P], nmx[:, qt:qt + 1], ident[:], start=True, stop=True)
                    last.then_inc(s["mrow_done"], 1)
                if isinstance(st, tuple) and st[0] == "pv":
                    c, n = st[1], st[2]
                    qt = 4 * c + n
                    if n == 0:
                        pe.wait_ge(s["exp_ready"], b * 16 + (c * 8 + 8))
                    if n == 0 and c == 0:
                        pe.wait_ge(s["va_ready"], b + 1)
                    if not (first and qt < 2):
                        pe.wait_ge(s["o_ready"], b * 8 + (qt - 1))
                    for kt in range(NT):
                        last = mm(pvp[qt % 2][:, 0:VA], pT[c][:, kt, n * P:(n + 1) * P], va[k][:, kt, :],
                                  start=(kt == 0), stop=(kt == NT - 1))
                    last.then_inc(s["pv_done"], 1)
                    if c == 1 and not (isinstance(b, int) and b == B - 1):
                        if n == 0:
                            pe.wait_ge(s["kb_ready"], b + 2)
                            pe.wait_ge(s["qb_ready"], b + 2)
                        mx_items(b + 1, 1 - k, 0, 2 * n, 2 * n + 2)
                if st == "mx_first":
                    pe.wait_ge(s["kb_ready"], 1)
                    pe.wait_ge(s["qb_ready"], 1)
                    mx_items(b, k, 0, 0, 8)
                if st == "u2_turn":
                    pe.wait_ge(s["u2_ready"], b + 1)
                    if not (isinstance(b, int) and b >= B - 2):
                        pe.wait_ge(s["t1_ready"], b + 3)
                    turn(lambda t: u2[:, t, :], s["u2_turned"])
                if st == "gate":
                    pe.wait_ge(s["u2T_ready"], b + 1)
                    for t in range(NT):
                        last = mm(work[:, 0, t * E:(t + 1) * E], u2T[:, t * P:(t + 1) * P], gw_s[:], start=True, stop=True)
                    last.then_inc(s["gate_done"], 1)
                if st == "pos":
                    pe.wait_ge(s["ohb_ready"], b + 1)
                    ohf = oh_bf[:].rearrange("p t e -> p (t e)")
                    mm(work[:, 1, 0:NT * E], before_bf[:], ohf, start=True, stop=False, skip_group_check=True)
                    for d in range(NT):
                        last = mm(work[:, 1, (d + 1) * E:(NT + 1) * E], ones_bf[:], ohf[:, 0:(NT - d) * E],
                                  start=False, stop=(d == NT - 1), skip_group_check=True)
                    last.then_inc(s["pos_done"], 1)

            passes(pe, one)



def expert_program(nc, slots, tokens, w1, b1, w2, b2, sems):
    with ExitStack() as ctx:
        def sb(name, shape, dt=F32):
            return ctx.enter_context(nc.sbuf_tensor(name, shape, dt))

        def sem(name):
            return sems.enter_context(nc.semaphore(name))

        ident = sb("e_ident", [P, P])
        neghalf = sb("e_neghalf", [P, G])
        w1s = [sb(f"w1s{k}", [P, F]) for k in range(2)]
        w2s = [sb(f"w2s{k}", [P, FC, C]) for k in range(2)]
        b1c = [sb(f"b1c{k}", [P, FC]) for k in range(2)]
        b2r = [sb(f"b2r{k}", [P, C]) for k in range(2)]
        rows = [sb(f"e_rows{k}", [P, G, ROW]) for k in range(2)]
        kept = [sb(f"kept{k}", [P, G, ROW]) for k in range(2)]
        bn = sb("e_bn", [P, G, 6])
        mv = sb("e_mv", [P, G, 2])
        tmpv, negm, rstd = sb("e_tmpv", [P, G]), sb("e_negm", [P, G]), sb("e_rstd", [P, G])
        u = sb("e_u", [P, G, C])
        uT = [sb(f"e_uT{k}", [P, BLK]) for k in range(2)]
        hid = [sb(f"hid{k}", [P, BLK]) for k in range(4)]
        yb = sb("yb", [P, G, C])
        z = sb("z", [P, G, C])
        clip = sb("clip", [P, G, C])
        isnum = sb("isnum", [P, G, C], I32)
        isfin = sb("isfin", [P, G, C], I32)
        ysafe = sb("ysafe", [P, G, C])
        res = [sb(f"res{k}", [P, G, C]) for k in range(2)]
        tp = [ctx.enter_context(nc.psum_tensor(f"e_tp{k}", [P, BLK], F32)) for k in range(2)]
        hp = [ctx.enter_context(nc.psum_tensor(f"e_hp{k}", [P, BLK], F32)) for k in range(2)]
        yp = [ctx.enter_context(nc.psum_tensor(f"e_yp{k}", [P, G, C], F32)) for k in range(2)]

        names = """e_const e_ident_ready e_stats e_mv_ready e_rstd_ready e_u_ready e_turned e_uT_ready e_kept
        e_hid_done e_hid_ready e_y_done e_yb_ready e_guard e_zero e_res_ready""".split()
        s = {n: sem(n) for n in names}
        passed = {n: sem(f"e_passed_{n}") for n in ("sp", "pool", "dve", "pe")}
        w_loaded, rows_loaded, stored = ([sem(f"e_{n}{k}") for k in range(2)] for n in ("w_loaded", "rows_loaded", "stored"))
        NBLKS = E * NBLK

        def blocks(eng, one, before=None):
            def expert(e, par, first=False, last=False):
                if before:
                    before(e, par, last)
                lo, hi = (2 if first else 1), (NBLK // 2 - 1 if last else NBLK // 2)
                one(e * NBLK, 0, par, True, first, False)
                one(e * NBLK + 1, 1, par, False, False, False)
                if first:
                    one(e * NBLK + 2, 0, par, False, False, False)
                    one(e * NBLK + 3, 1, par, False, False, False)
                with eng.Fori(lo, hi) as j:
                    one(e * NBLK + j * 2, 0, par, False, False, False)
                    one(e * NBLK + j * 2 + 1, 1, par, False, False, False)
                if last:
                    one(e * NBLK + NBLK - 2, 0, par, False, False, False)
                    one(e * NBLK + NBLK - 1, 1, par, False, False, True)
            expert(0, 0, first=True)
            expert(1, 1)
            with eng.Fori(1, E // 2 - 1) as i:
                expert(i * 2, 0)
                expert(i * 2 + 1, 1)
            expert(E - 2, 0)
            expert(E - 1, 1, last=True)

        def wait_rows(eng, n, half):
            eng.wait_ge(rows_loaded[half], n * 8 + (16 if half == 0 else 8))

        block = ctx.enter_context(nc.Block())

        @block.sync
        def _(sp):
            def load_w(e, par):
                for dst, src in ((w1s[par][:], w1[bass.ds(e, 1)].rearrange("o d f -> (o d) f")),
                                 (w2s[par][:], w2[bass.ds(e, 1)].rearrange("o (c p) d -> p (o c) d", p=P)),
                                 (b1c[par][:], b1[bass.ds(e, 1)].rearrange("o p c -> (o p) c")),
                                 (b2r[par][:], b2[bass.ds(e, 1)].rearrange("o d -> (o d)").partition_broadcast(P))):
                    sp.dma_start(dst, src).then_inc(w_loaded[par], 16)

            def load_rows(n, half):
                sp.dma_start(rows[half][:].rearrange("p g d -> p (g d)"),
                             slots[bass.ds(n * BLK, BLK)].rearrange("(p g) d -> p (g d)", p=P)).then_inc(rows_loaded[half], 16)

            load_rows(0, 0)
            load_w(0, 0)
            state = {}

            def before(e, par, last):
                state["e"] = None if last else e

            def one(n, half, par, j0, first, last):
                if not last:
                    if not first:
                        wait_apart(sp, s["e_u_ready"], n, passed["sp"])
                        wait_apart(sp, s["e_kept"], n, passed["sp"])
                    load_rows(n + 1, 1 - half)
                if j0 and state["e"] is not None:
                    if not first:
                        wait_apart(sp, s["e_y_done"], n, passed["sp"])
                        wait_apart(sp, s["e_yb_ready"], n * 2, passed["sp"])
                    load_w(state["e"] + 1, 1 - par)

            blocks(sp, one, before)

        @block.gpsimd
        def _(pool):
            g = nc.gpsimd
            g.memset(ident[:], 0.0).then_inc(s["e_const"], 1)
            pool.wait_ge(s["e_const"], 1)
            g.memset(neghalf[:], -0.5).then_inc(s["e_const"], 1)
            pool.wait_ge(s["e_const"], 2)
            g.affine_select(out=ident[:], in_=ident[:], pattern=[[-1, P]], compare_op=ALU.not_equal, fill=1.0,
                            base=0, channel_multiplier=1).then_inc(s["e_ident_ready"], 1)

            def prep(n):
                wait_apart(pool, s["e_mv_ready"], n + 1, passed["pool"])
                if not early(n, 1):
                    wait_apart(pool, s["e_u_ready"], n, passed["pool"])
                r = s["e_rstd_ready"]
                g.tensor_scalar(tmpv[:], mv[:, :, 1], 1.0, 1e-5, ALU.mult, ALU.add).then_inc(r, 1)
                g.tensor_scalar(negm[:], mv[:, :, 0], -1.0, 0.0, ALU.mult, ALU.add).then_inc(r, 1)
                wait_apart(pool, r, n * 3 + 2, passed["pool"])
                g.tensor_tensor(rstd[:], tmpv[:], neghalf[:], ALU.pow).then_inc(r, 1)
                wait_apart(pool, r, n * 3 + 3, passed["pool"])
                if not (isinstance(n, int) and n == 0):
                    wait_apart(pool, s["e_turned"], n, passed["pool"])
                return r

            def normalise(half):
                for q in range(G):
                    last = g.tensor_scalar(u[:, q, :], rows[half][:, q, 0:C], negm[:, q:q + 1], rstd[:, q:q + 1],
                                           ALU.add, ALU.mult)
                last.then_inc(s["e_u_ready"], 1)

            def store(n, half):
                wait_apart(pool, s["e_res_ready"], n + 1, passed["pool"])
                for q in range(G):
                    g.indirect_dma_start(out=tokens, out_offset=bass.IndirectOffsetOnAxis(
                        ap=kept[half][:, q, C:C + 1].bitcast(I32), axis=0), in_=res[half][:, q, :], in_offset=None,
                        bounds_check=T - 1, oob_is_err=False).then_inc(stored[half], 16)

            def zero(n):
                if not (isinstance(n, int) and n == 0):
                    wait_apart(pool, s["e_res_ready"], n, passed["pool"])
                g.memset(ysafe[:], 0.0).then_inc(s["e_zero"], 1)

            prep(0)
            normalise(0)

            def one(n, half, par, j0, first, last):
                if not last:
                    prep(n + 1)
                    normalise(1 - half)
                if not first:
                    zero(n - 1)
                    store(n - 1, 1 - half)

            blocks(pool, one)
            zero(NBLKS - 1)
            store(NBLKS - 1, 1)

        @block.scalar
        def _(act):
            a = nc.scalar

            def prep(n, half):
                if not (isinstance(n, int) and n < 2):
                    act.wait_ge(stored[half], (n - half) * 32)
                wait_rows(act, n, half)
                a.copy(kept[half][:], rows[half][:]).then_inc(s["e_kept"], 1)
                act.wait_ge(s["e_turned"], n + 1)
                a.copy(uT[half][:], tp[half][:]).then_inc(s["e_uT_ready"], 1)

            def relu(n, f, par):
                act.wait_ge(s["e_hid_done"], n * FC + (f + 1))
                a.activation(hid[f][:], hp[f % 2][:], ACT.Relu, bias=b1c[par][:, f:f + 1], scale=1.0)\
                    .then_inc(s["e_hid_ready"], 1)

            def one(n, half, par, j0, first, last):
                for f in range(3):
                    relu(n, f, par)
                if not last:
                    prep(n + 1, 1 - half)
                relu(n, 3, par)
            prep(0, 0)
            blocks(act, one)

        @block.vector
        def _(dve):
            v = nc.vector

            def prep(n, half):
                if not (isinstance(n, int) and n == 0):
                    dve.wait_ge(s["e_rstd_ready"], n * 3)
                for q in range(G):
                    last = v.bn_stats(bn[:, q, :], rows[half][:, q, 0:C])
                last.then_inc(s["e_stats"], 1)
                wait_apart(dve, s["e_stats"], n + 1, passed["dve"])
                for q in range(G):
                    last = v.bn_aggr(mv[:, q, :], bn[:, q, :])
                last.then_inc(s["e_mv_ready"], 1)

            def result(n, half, par, early2):
                dve.wait_ge(s["e_y_done"], n + 1)
                v.tensor_tensor(yb[:], yp[half][:], b2r[par][:].unsqueeze(1).to_broadcast([P, G, C]), ALU.add)\
                    .then_inc(s["e_yb_ready"], 1)
                dve.wait_ge(s["e_yb_ready"], n * 2 + 1)
                v.tensor_tensor(z[:], yb[:], kept[half][:, :, C + 1:C + 2].to_broadcast([P, G, C]), ALU.mult)\
                    .then_inc(s["e_yb_ready"], 1)
                dve.wait_ge(s["e_yb_ready"], n * 2 + 2)
                v.tensor_scalar(clip[:], z[:], -NAN_CLIP, NAN_CLIP, ALU.max, ALU.min)
                v.tensor_tensor(isnum[:], z[:], z[:], ALU.is_equal)
                v.tensor_scalar(isfin[:], z[:], 0.0, 0.0, ALU.mult, ALU.is_equal).then_inc(s["e_guard"], 1)
                dve.wait_ge(s["e_guard"], n * 3 + 1)
                wait_apart(dve, s["e_zero"], n + 1, passed["dve"])
                v.copy_predicated(ysafe[:], isnum[:], clip[:]).then_inc(s["e_guard"], 1)
                wait_apart(dve, s["e_guard"], n * 3 + 2, passed["dve"])
                v.copy_predicated(ysafe[:], isfin[:], z[:]).then_inc(s["e_guard"], 1)
                dve.wait_ge(s["e_guard"], n * 3 + 3)
                if not early2:
                    dve.wait_ge(stored[half], (n - half) * 32)
                v.tensor_tensor(res[half][:], ysafe[:], kept[half][:, :, 0:C], ALU.add).then_inc(s["e_res_ready"], 1)

            def one(n, half, par, j0, first, last):
                if not last:
                    wait_rows(dve, n + 1, 1 - half)
                    prep(n + 1, 1 - half)
                if not first:
                    result(n - 1, 1 - half, 1 - par if j0 else par, isinstance(n, int) and n - 1 < 2)

            wait_rows(dve, 0, 0)
            prep(0, 0)
            blocks(dve, one)
            result(NBLKS - 1, 1, 1, False)

        @block.tensor
        def _(pe):
            mm = nc.tensor.matmul
            pe.wait_ge(s["e_ident_ready"], 1)

            def turn(n, half):
                pe.wait_ge(s["e_u_ready"], n + 1)
                for q in range(G):
                    last = nc.tensor.transpose(tp[half][:, q * P:(q + 1) * P], u[:, q, :], ident[:])
                last.then_inc(s["e_turned"], 1)

            def layer1(n, half, par, f):
                if not (isinstance(n, int) and n == 0 and f < 2):
                    pe.wait_ge(s["e_hid_ready"], n * FC + (f - 1))
                mm(hp[f % 2][:], w1s[par][:, f * P:(f + 1) * P], uT[half][:], start=True, stop=True)\
                    .then_inc(s["e_hid_done"], 1)

            def layer2(n, half, par, f):
                pe.wait_ge(s["e_hid_ready"], n * FC + (f + 1))
                for q in range(G):
                    last = mm(yp[half][:, q, :], hid[f][:, q * P:(q + 1) * P], w2s[par][:, f, :],
                              start=(f == 0 and q == 0), stop=(f == FC - 1), skip_group_check=True)
                if f == FC - 1:
                    last.then_inc(s["e_y_done"], 1)

            turn(0, 0)

            def before(e, par, last):
                pe.wait_ge(w_loaded[par], (e * 32 + 64) if par == 0 else (e * 32 + 32))

            def one(n, half, par, j0, first, last):
                pe.wait_ge(s["e_uT_ready"], n + 1)
                layer1(n, half, par, 0)
                layer1(n, half, par, 1)
                if not (isinstance(n, int) and n < 2):
                    pe.wait_ge(s["e_yb_ready"], n * 2 - 3)
                layer2(n, half, par, 0)
                layer1(n, half, par, 2)
                if not last:
                    turn(n + 1, 1 - half)
                layer2(n, half, par, 1)
                layer1(n, half, par, 3)
                layer2(n, half, par, 2)
                layer2(n, half, par, 3)

            blocks(pe, one, before)

        @block.sync
        def _(sp):
            for k in range(2):
                sp.wait_ge(stored[k], NBLKS // 2 * G * 16)


def output_program(nc, tokens, out, sems):
    with ExitStack() as ctx:
        def sem(name):
            return sems.enter_context(nc.semaphore(name))

        ident = ctx.enter_context(nc.sbuf_tensor("f_ident", [P, P], F32))
        rows = [ctx.enter_context(nc.sbuf_tensor(f"f_rows{k}", [P, NT, C], F32)) for k in range(4)]
        cols = [ctx.enter_context(nc.sbuf_tensor(f"f_cols{k}", [P, N], F32)) for k in range(2)]
        ps = [ctx.enter_context(nc.psum_tensor(f"f_ps{k}", [P, 2, HALF], F32)) for k in range(2)]
        ident_set, ident_ready, turned, lo_ready, hi_ready = (sem(f"f_{n}") for n in
                                                              ("ident_set", "ident_ready", "turned", "lo_ready", "hi_ready"))
        loaded = [sem(f"f_loaded{k}") for k in range(4)]
        stored = [sem(f"f_stored{k}") for k in range(2)]
        passed = {"sp": sem("f_passed_sp")}
        R = 4
        block = ctx.enter_context(nc.Block())

        @block.sync
        def _(sp):
            def load(b, r):
                sp.dma_start(rows[r][:], tokens[bass.ds(b * N, N)].rearrange("(t p) c -> p t c", p=P)).then_inc(loaded[r], 16)
            for r in range(R):
                load(r, r)
            with sp.Fori(1, B // R) as i:
                for r in range(R):
                    wait_apart(sp, turned, i * R + (r + 1 - R), passed["sp"])
                    load(i * R + r, r)

        @block.gpsimd
        def _(pool):
            nc.gpsimd.memset(ident[:], 0.0).then_inc(ident_set, 1)
            pool.wait_ge(ident_set, 1)
            nc.gpsimd.affine_select(out=ident[:], in_=ident[:], pattern=[[-1, P]], compare_op=ALU.not_equal, fill=1.0,
                                    base=0, channel_multiplier=1).then_inc(ident_ready, 1)

        @block.tensor
        def _(pe):
            pe.wait_ge(ident_ready, 1)

            def one(i, r):
                pe.wait_ge(loaded[r], i * 16 + 16)
                if not (isinstance(i, int) and r < 2):
                    pe.wait_ge(lo_ready, i * R + (r - 1))
                    pe.wait_ge(hi_ready, i * R + (r - 1))
                for t in range(NT):
                    last = nc.tensor.transpose(ps[r % 2][:, t // 4, (t % 4) * P:(t % 4 + 1) * P], rows[r][:, t, :], ident[:])
                last.then_inc(turned, 1)
            for r in range(R):
                one(0, r)
            with pe.Fori(1, B // R) as i:
                for r in range(R):
                    one(i, r)

        @block.scalar
        def _(act):
            def one(i, r):
                act.wait_ge(turned, i * R + (r + 1))
                if not (isinstance(i, int) and r < 2):
                    act.wait_ge(stored[r % 2], i * 32 + (r // 2) * 16)
                nc.scalar.copy(cols[r % 2][:, 0:HALF], ps[r % 2][:, 0, :]).then_inc(lo_ready, 1)
                act.wait_ge(lo_ready, i * R + (r + 1))
                act.wait_ge(hi_ready, i * R + (r + 1))
                act.dma_start(out[bass.ds(i * R + r, 1)].rearrange("o c n -> (o c) n"), cols[r % 2][:]).then_inc(stored[r % 2], 16)
            for r in range(R):
                one(0, r)
            with act.Fori(1, B // R) as i:
                for r in range(R):
                    one(i, r)
            for k in range(2):
                act.wait_ge(stored[k], B // 2 * 16)

        @block.vector
        def _(dve):
            def one(i, r):
                dve.wait_ge(turned, i * R + (r + 1))
                if not (isinstance(i, int) and r < 2):
                    dve.wait_ge(stored[r % 2], i * 32 + (r // 2) * 16)
                nc.vector.tensor_copy(cols[r % 2][:, HALF:N], ps[r % 2][:, 1, :]).then_inc(hi_ready, 1)
            for r in range(R):
                one(0, r)
            with dve.Fori(1, B // R) as i:
                for r in range(R):
                    one(i, r)


def program(nc, a, out):
    slots = nc.dram_tensor("expert_slots", [E * CAP, ROW], F32, kind="Internal").ap()
    tokens = nc.dram_tensor("token_rows", [T, C], F32, kind="Internal").ap()
    with ExitStack() as sems:
        token_program(nc, a["x"], a["ln_w"], a["ln_b"], a["w_bcdt_t"], a["w_gw"], a["w_out_t"], a["A"], a["Wq"], a["bq"],
                      a["Wk"], a["bk"], a["Wv"], a["bv"], a["gamma"], a["beta"], a["gate_w"], a["gate_b"],
                      slots, tokens, sems)
        expert_program(nc, slots, tokens, a["w1"], a["b1"], a["w2"], a["b2"], sems)
        output_program(nc, tokens, out, sems)


def kernel(**inputs):
    import numpy as np
    import concourse.bacc as bacc
    from concourse.bass_utils import run_bass_kernel_spmd

    def get(name):
        return np.asarray(inputs[name])

    lay = {
        "x": get("x").reshape(B, C, N),
        "ln_w": get("L0_conv_ln_w").reshape(C, 1), "ln_b": get("L0_conv_ln_b").reshape(C, 1),
        "w_bcdt_t": get("L0_conv_w_bcdt").reshape(U, C).T, "w_gw": get("L0_conv_w_gw").reshape(U, 2, 9),
        "w_out_t": get("L0_conv_w_out").reshape(C, C).T, "A": get("L0_conv_A"),
        "Wq": get("L1_attn_Wq"), "bq": get("L1_attn_bq"), "Wk": get("L1_attn_Wk"), "bk": get("L1_attn_bk"),
        "Wv": get("L1_attn_Wv"), "bv": get("L1_attn_bv"), "gamma": get("L1_attn_gamma"), "beta": get("L1_attn_beta"),
        "gate_w": get("L1_ffn_gate_w"), "gate_b": get("L1_ffn_gate_b"), "w1": get("L1_ffn_w1"),
        "b1": get("L1_ffn_b1").reshape(E, FC, P).transpose(0, 2, 1),
        "w2": get("L1_ffn_w2"), "b2": get("L1_ffn_b2"),
    }
    nc = bacc.Bacc("TRN2", target_bir_lowering=False, num_devices=1)
    arrays = {f"in_{n}": np.ascontiguousarray(v) for n, v in lay.items()}
    args = {n: nc.dram_tensor(f"in_{n}", arrays[f"in_{n}"].shape, mybir.dt.from_np(arrays[f"in_{n}"].dtype),
                              kind="ExternalInput").ap() for n in lay}
    out = nc.dram_tensor("out", [B, C, N], F32, kind="ExternalOutput").ap()
    program(nc, args, out)
    r = run_bass_kernel_spmd(nc, [arrays], core_ids=[0])
    return r.results[0]["out"].reshape(B, C, H, W)
```

```python
from contextlib import ExitStack

import concourse.bass as bass
from concourse import mybir

F32 = mybir.dt.float32
BF16 = mybir.dt.bfloat16
I32 = mybir.dt.int32
ALU = mybir.AluOpType
ACT = mybir.ActivationFunctionType
AX = mybir.AxisListType.X

P = 128
B, C, H, W = 32, 128, 32, 32
N = H * W
NT = N // P
S = 32
HP, WP = H + 2, W + 2
U = 64
KA = U + 2
VA = C + 1
HALF = 512
E, F = 8, 512
FC = F // P
T = B * N
CAP = -(-5 * T // (4 * E))
ROW = C + 4
TOKEN, PROB, RSTD, SHIFT = range(C, ROW)
BLK = 512
G = BLK // P
NBLK = CAP // BLK
FILL_ROWS = 10
NFILL = E * CAP // (P * FILL_ROWS)
NO_TOKEN = 1 << 24
DROP = float(1 << 20)
NEG_FILL = -2.0 ** 32 + 1.0
NAN_CLIP = 10000.0


def early(b, n):
    return isinstance(b, int) and b < n


def wait_apart(eng, sem, value, passed):
    eng.wait_ge(sem, value)
    if not isinstance(value, int):
        eng.sem_inc(passed, 1)


def token_program(nc, x, ln_w, ln_b, w_bcdt_t, w_gw, w_out_t, A, Wq, bq, Wk, bk, Wv, bv, gamma, beta,
                  gate_w, gate_b, slots, tokens, sems):
    with ExitStack() as ctx:
        def sb(name, shape, dt=F32):
            return ctx.enter_context(nc.sbuf_tensor(name, shape, dt))

        def sem(name):
            return sems.enter_context(nc.semaphore(name))

        NW = 17

        ident = sb("ident", [P, P])
        ones_bf = sb("ones_bf", [P, P], BF16)
        before_bf = sb("before_bf", [P, P], BF16)
        onecol_bf = sb("onecol_bf", [P, 2], BF16)
        lnw_c, lnb_c = sb("lnw_c", [P, 1]), sb("lnb_c", [P, 1])
        wbc = sb("wbc", [P, 2, U])
        wgr = sb("wgr", [U, 2, 9])
        gmask = sb("gmask", [U, U])
        wexp = sb("wexp", [U, 9, U])
        wtap2 = sb("wtap2", [P, 3, U])
        wtap1 = sb("wtap1", [U, 3, U])
        wot = sb("wot", [P, C])
        A_c = sb("A_c", [U, 1])
        wq_s, wk_s, wv_s = sb("wq_s", [P, U]), sb("wk_s", [P, U]), sb("wv_s", [P, C])
        bq_c, bk_c = sb("bq_c", [U, 1]), sb("bk_c", [U, 1])
        bqs_c = sb("bqs_c", [U, 1])
        bv_r, gamma_r, beta_r = sb("bv_r", [P, C]), sb("gamma_r", [P, C]), sb("beta_r", [P, C])
        gw_s, gb_r = sb("gw_s", [P, E]), sb("gb_r", [P, E])
        kscale = sb("kscale", [KA, 1])
        neghalf = sb("neghalf", [P, NT])
        rank = sb("rank", [P, NT, E])
        eoff = sb("eoff", [P, NT, E])
        iota_i = sb("iota_i", [P, NT, E], I32)
        tokid = sb("tokid", [P, NT])
        tokid_i = sb("tokid_i", [P, NT], I32)
        fill = sb("fill", [P, FILL_ROWS, ROW])

        xs = [sb(f"xs{k}", [P, N]) for k in range(2)]
        xT = sb("xT", [P, NT, C])
        bn = sb("bn", [P, NT, 6])
        mv = sb("mv", [P, NT, 2])
        tmpv, negm, rstd, shift = (sb(f"{n}_x", [P, NT]) for n in ("tmpv", "negm", "rstd", "shift"))
        mvt = sb("mvt", [P, NT, 2])
        tmpvt, negmt, rstdt, shiftt = (sb(f"{n}_t", [P, NT]) for n in ("tmpv", "negm", "rstd", "shift"))
        xn = sb("xn", [P, NT, C])
        xnT = sb("xnT", [P, N])
        img = sb("img", [P, HP, WP])
        cd = sb("cd", [U, N])
        dts = sb("dts", [U, 4])
        dtr = sb("dtr", [U, 1])
        cdT = sb("cdT", [P, NT, U])
        abT = sb("abT", [P, NT, S])
        hs = sb("hs", [P, S])
        gs = sb("gs", [S, C])
        t1 = [sb(f"t1_{k}", [P, NT, C]) for k in range(2)]
        u1 = [sb(f"u1_{k}", [P, NT, C]) for k in range(2)]
        u1T = sb("u1T", [P, N])
        absu = sb("absu", [P, N], BF16)
        qa = [sb(f"qa{k}", [KA, N]) for k in range(2)]
        ka = [sb(f"ka{k}", [KA, N]) for k in range(2)]
        qb = [sb(f"qb{k}", [KA, N], BF16) for k in range(2)]
        kb = [sb(f"kb{k}", [KA, N], BF16) for k in range(2)]
        vz = sb("vz", [P, NT, C])
        qz, kz = sb("qz", [U, N]), sb("kz", [U, N])
        va = [sb(f"va{k}", [P, NT, VA]) for k in range(2)]
        mxs = sb("mxs", [P, NT, 2])
        nmx = sb("nmx", [P, NT])
        pT = [sb(f"pT{k}", [P, NT, HALF]) for k in range(2)]
        prv = sb("prv", [P, NT])
        o = [sb(f"o{k}", [P, NT, C]) for k in range(2)]
        bn3 = sb("bn3", [P, NT, 6])
        mv3 = sb("mv3", [P, NT, 2])
        tmpv3, negm3, rstd3, shift3 = (sb(f"{n}_3", [P, NT]) for n in ("tmpv", "negm", "rstd", "shift"))
        rows = [sb(f"rows{k}", [P, NT, ROW]) for k in range(2)]
        u2 = sb("u2", [P, NT, C])
        u2T = sb("u2T", [P, N])
        lg = sb("lg", [P, NT, E])
        eg = sb("eg", [P, NT, E])
        r8 = sb("r8", [P, 6, NT])
        oh = sb("oh", [P, NT, E])
        oh_bf = sb("oh_bf", [P, NT, E], BF16)
        ra = sb("ra", [P, NT, E])
        rb = sb("rb", [P, NT, E])
        rc = sb("rc", [P, NT, E])
        rd = sb("rd", [P, NT, E])
        run = sb("run", [P, 1, E])
        slot_i = [sb(f"slot_i{k}", [P, NT], I32) for k in range(2)]

        work = ctx.enter_context(nc.psum_tensor("work", [P, 2, HALF], F32))
        mxp = [ctx.enter_context(nc.psum_tensor(f"mxp{k}", [P, HALF], F32)) for k in range(2)]
        stp = [ctx.enter_context(nc.psum_tensor(f"stp{k}", [P, HALF], F32)) for k in range(2)]
        pvp = [ctx.enter_context(nc.psum_tensor(f"pvp{k}", [P, HALF], F32)) for k in range(2)]
        workf = work[:].rearrange("p a b -> p (a b)")
        workt = work[:].rearrange("p a (t c) -> p (a t) c", c=C)

        names = """w_loaded wpe_loaded const_pool const_dve const_act fill_ready fill_done mask_ready wexp_ready
        taps_psum taps_ready
        x_turned xT_ready x_stats x_mv x_rstd xn_ready xn_turned xnT_ready bcdt_done img_ready conv_done
        dt_small cd_exp dt_sumr asm_ready cd_turned cdT_ready abT_ready h_done h_ready g_done g_ready y_done t1_ready
        t1b_ready t_stats t_mv t_rstd u1_ready u1_turned u1T_ready absu_ready q_done qz_ready qa_ready qb_ready k_done kz_ready kmask_ready ka_ready kb_ready v_done vz_ready va_ready
        mx_done mx_read negmax_ready mrow_done mrow_ready st_done exp_ready pv_done pv_rinv o_ready
        o_stats o_mv o_rstd on_ready ong_ready t2_ready t2_stats t2_mv t2_rstd u2_ready u2_turned u2T_ready
        gate_done lg_ready eg_ready gate_chain ohb_ready pos_done slot_ready rowid_ready rowprob_ready""".split()
        s = {n: sem(n) for n in names}
        passed = {n: sem(f"passed_{n}") for n in ("sp", "pool", "dve", "pe")}
        x_loaded, scattered, tokens_stored = ([sem(f"{n}{k}") for k in range(2)]
                                              for n in ("x_loaded", "scattered", "tokens_stored"))

        def bc_last(ap2, n):
            return ap2.unsqueeze(2).to_broadcast([ap2.shape[0], ap2.shape[1], n])

        def bc_mid(ap2, n):
            return ap2.unsqueeze(1).to_broadcast([ap2.shape[0], n, ap2.shape[1]])

        steps = ["t1b", ("st", 0, 0), ("ln2s", 0), ("u1n", 0), ("st", 0, 1), ("ln2s", 1), ("u1n", 1), ("st", 0, 2),
                 "x_turn", ("u1n", 2), ("st", 0, 3), ("u1n", 3), ("st", 0, 4), "u1_turn", ("xs", 0), ("ln2n", 0),
                 ("st", 0, 5), ("xs", 1), ("ln2n", 1), ("st", 0, 6), "q", ("ln2n", 2), ("st", 0, 7), ("ln2n", 3), "k",
                 ("negmax", 1), ("pv", 0, 0), ("xn", 0), ("xn", 1), ("pv", 0, 1), "ln2g", "v", ("xn", 2), ("xn", 3),
                 ("mrow", 1), "xn_turn", ("ln3s", 0), ("pv", 0, 2), ("ln3s", 1), "bcdt", ("pv", 0, 3),
                 ("st", 1, 0), ("conv", 0), ("ln3n", 0), ("st", 1, 1), ("conv", 1), "dt", ("st", 1, 2), ("ln3n", 1),
                 ("st", 1, 3), ("ln3n", 2), ("st", 1, 4), ("ln3n", 3), ("st", 1, 5), "asm", ("st", 1, 6), "u2_turn",
                 ("st", 1, 7), "gate", ("pv", 1, 0), "cd_turn", ("pv", 1, 1), "pos", ("pv", 1, 2), "h", ("pv", 1, 3),
                 ("negmax", 0), "g", ("mrow", 0), "scatter", "y", "ts"]
        ROUTE = ("ln2s", "ln2n", "ln2g", "ln3s", "ln3n", "u2_turn", "gate", "pos", "scatter")
        PROJ = ("u1n", "u1_turn", "q", "k", "v")
        ATT = ("t1b", "st", "pv", "negmax", "mrow")

        def batch(i, c):
            return i * 2 + c, i + c // 2, c % 2

        def one_pass(one, i, c, attend=True, last=False):
            for st in steps:
                what = st[0] if isinstance(st, tuple) else st
                if st in (("negmax", 0), ("mrow", 0)):
                    if c == -1 and what == "negmax":
                        one("mx_first", *batch(i, c + 1))
                    if c != -2 and not (last and c == B - 1):
                        one(st, *batch(i, c + 1))
                elif what in ATT:
                    if attend:
                        one(st, *batch(i, c))
                elif what in ROUTE:
                    if attend and c != 0:
                        one(st, *batch(i, c - 1))
                elif what in PROJ:
                    if c != -2 and not (last and c == B - 1):
                        one(st, *batch(i, c + 1))
                elif not last:
                    one(st, *batch(i, c + 2))

        def passes(eng, one):
            one_pass(one, 0, -2, attend=False)
            one_pass(one, 0, -1, attend=False)
            one_pass(one, 0, 0)
            one_pass(one, 0, 1)
            one_pass(one, 0, 2)
            with eng.Fori(1, (B - 4) // 2) as i:
                one_pass(one, i, 1)
                one_pass(one, i, 2)
            one_pass(one, 0, B - 3)
            one_pass(one, 0, B - 2, last=True)
            one_pass(one, 0, B - 1, last=True)
            for st in steps:
                if (st[0] if isinstance(st, tuple) else st) in ROUTE:
                    one(st, *batch(0, B - 1))

        block = ctx.enter_context(nc.Block())

        @block.sync
        def _(sp):
            def w(dst, src):
                sp.dma_start(dst, src).then_inc(s["w_loaded"], 16)

            def load_x(b, k):
                sp.dma_start(xs[k][:], x[bass.ds(b, 1)].rearrange("o c n -> (o c) n")).then_inc(x_loaded[k], 16)

            load_x(0, 0)
            w(wbc[:, 0, :], w_bcdt_t)
            w(wbc[:, 1, :], w_bcdt_t)
            w(wgr[:], w_gw)
            w(wot[:], w_out_t)
            w(lnw_c[:], ln_w)
            w(lnb_c[:], ln_b)
            w(A_c[S:U, :], A.unsqueeze(1))
            w(wq_s[:], Wq)
            w(wk_s[:], Wk)
            w(wv_s[:], Wv)
            w(bq_c[:], bq.unsqueeze(1))
            w(bk_c[:], bk.unsqueeze(1))
            w(bv_r[:], bv.partition_broadcast(P))
            w(gamma_r[:], gamma.partition_broadcast(P))
            w(beta_r[:], beta.partition_broadcast(P))
            w(gw_s[:], gate_w)
            w(gb_r[:], gate_b.partition_broadcast(P))
            load_x(1, 1)
            sp.wait_ge(s["fill_ready"], 1)
            for f in range(NFILL):
                sp.dma_start(slots[f * P * FILL_ROWS:(f + 1) * P * FILL_ROWS].rearrange("(p r) d -> p (r d)", p=P),
                             fill[:].rearrange("p r d -> p (r d)")).then_inc(s["fill_done"], 16)

            def one(st, b, m, k):
                if st == "x_turn" and not early(b, 1) and not (isinstance(b, int) and b == B - 1):
                    wait_apart(sp, s["x_turned"], b, passed["sp"])
                    load_x(b + 1, 1 - k)
                if st == ("ln3s", 0):
                    wait_apart(sp, s["t2_ready"], b + 1, passed["sp"])
                    sp.dma_start(tokens[bass.ds(b * N, N)].rearrange("(t p) c -> p t c", p=P),
                                 rows[k][:, :, 0:C]).then_inc(tokens_stored[k], 16)

            passes(sp, one)
            for k in range(2):
                sp.wait_ge(scattered[k], (B // 2) * NT * 16)
                sp.wait_ge(tokens_stored[k], (B // 2) * 16)

        @block.gpsimd
        def _(pool):
            g = nc.gpsimd
            cp = [0]

            def chain(ins):
                cp[0] += 1
                ins.then_inc(s["const_pool"], 1)
                pool.wait_ge(s["const_pool"], cp[0])

            chain(g.memset(fill[:], 0.0))
            chain(g.memset(fill[:, :, TOKEN:TOKEN + 1].bitcast(I32), NO_TOKEN))
            g.memset(neghalf[:], -0.5).then_inc(s["fill_ready"], 1)
            chain(g.memset(ident[:], 0.0))
            chain(g.affine_select(out=ident[:], in_=ident[:], pattern=[[-1, P]], compare_op=ALU.not_equal, fill=1.0,
                                  base=0, channel_multiplier=1))
            chain(g.memset(ones_bf[:], 1.0))
            chain(g.affine_select(out=before_bf[:], in_=ones_bf[:], pattern=[[1, P]], compare_op=ALU.is_gt, fill=0.0,
                                  base=0, channel_multiplier=-1))
            chain(g.memset(onecol_bf[:, 0:1], 0.0))
            chain(g.memset(onecol_bf[:, 1:2], 1.0))
            gm = gmask[:].rearrange("o (g i) -> o g i", i=2)
            chain(g.memset(gmask[:], 1.0))
            chain(g.affine_select(out=gm, in_=gm, pattern=[[-2, S], [0, 2]], compare_op=ALU.is_ge, fill=0.0,
                                  base=0, channel_multiplier=1))
            chain(g.affine_select(out=gm, in_=gm, pattern=[[2, S], [0, 2]], compare_op=ALU.is_ge, fill=0.0,
                                  base=1, channel_multiplier=-1))
            chain(g.iota(iota_i[:], pattern=[[0, NT], [1, E]], base=0, channel_multiplier=0))
            chain(g.tensor_scalar(rank[:], iota_i[:], -1.0, float(E), ALU.mult, ALU.add))
            chain(g.tensor_scalar(eoff[:], iota_i[:], float(CAP), 0.0, ALU.mult, ALU.add))
            chain(g.iota(tokid_i[:], pattern=[[P, NT]], base=0, channel_multiplier=1))
            chain(g.tensor_copy(tokid[:], tokid_i[:]))
            chain(g.memset(run[:], 0.0))
            chain(g.memset(kscale[U:KA, :], NEG_FILL))
            chain(g.memset(kscale[U:U + 1, :], 1.0))
            chain(g.memset(img[:], 0.0))
            for k in range(2):
                chain(g.memset(qa[k][U:KA, :], 1.0))
                chain(g.memset(qb[k][U:KA, :], 1.0))
                chain(g.memset(qb[k][U:U + 1, :], 0.0))
                chain(g.memset(va[k][:, :, C:VA], 1.0))
            g.memset(tmpv[:], 0.0).then_inc(s["mask_ready"], 1)

            def rsqrt(mv_, tmp_, negm_, rstd_, shift_, scale, eps, have, done, b):
                wait_apart(pool, have, b + 1, passed["pool"])
                g.tensor_scalar(tmp_[:], mv_[:, :, 1], scale, eps, ALU.mult, ALU.add).then_inc(done, 1)
                g.tensor_scalar(negm_[:], mv_[:, :, 0], -1.0, 0.0, ALU.mult, ALU.add).then_inc(done, 1)
                wait_apart(pool, done, b * 4 + 2, passed["pool"])
                g.tensor_tensor(rstd_[:], tmp_[:], neghalf[:], ALU.pow).then_inc(done, 1)
                wait_apart(pool, done, b * 4 + 3, passed["pool"])
                g.tensor_tensor(shift_[:], negm_[:], rstd_[:], ALU.mult).then_inc(done, 1)

            def one(st, b, m, k):
                first = early(b, 1)
                if st == "t1b":
                    if not early(b, 2):
                        wait_apart(pool, scattered[k], m * (NT * 16), passed["pool"])
                        wait_apart(pool, tokens_stored[k], m * 16, passed["pool"])
                    wait_apart(pool, s["t1_ready"], b + 1, passed["pool"])
                    g.tensor_tensor(rows[k][:, :, 0:C], t1[k][:], bc_mid(beta_r[:], NT), ALU.add)\
                        .then_inc(s["t1b_ready"], 1)
                if st == ("xs", 1):
                    rsqrt(mv, tmpv, negm, rstd, shift, C / (C - 1.0), 1e-5, s["x_mv"], s["x_rstd"], b)
                if st == "q":
                    wait_apart(pool, s["qa_ready"], b + 1, passed["pool"])
                    g.tensor_copy(qb[k][0:U, :], qa[k][0:U, :]).then_inc(s["qb_ready"], 1)
                if st == "k":
                    wait_apart(pool, s["ka_ready"], b + 1, passed["pool"])
                    g.tensor_copy(kb[k][:], ka[k][:]).then_inc(s["kb_ready"], 1)
                if st == "cd_turn":
                    wait_apart(pool, s["cdT_ready"], b + 1, passed["pool"])
                    if not first:
                        wait_apart(pool, s["h_done"], b, passed["pool"])
                    g.tensor_tensor(abT[:], cdT[:, :, 0:S], cdT[:, :, S:U], ALU.mult).then_inc(s["abT_ready"], 1)
                if st == "ts":
                    rsqrt(mvt, tmpvt, negmt, rstdt, shiftt, 1.0, 1e-5, s["t_mv"], s["t_rstd"], b)
                if st == ("ln2s", 1):
                    rsqrt(mv3, tmpv3, negm3, rstd3, shift3, 1.0, 1e-8, s["o_mv"], s["o_rstd"], b)
                if st == ("ln3s", 1):
                    rsqrt(mv3, tmpv3, negm3, rstd3, shift3, 1.0, 1e-5, s["t2_mv"], s["t2_rstd"], b)
                    g.tensor_copy(rows[k][:, :, TOKEN:TOKEN + 1].bitcast(I32), tokid[:].unsqueeze(2))\
                        .then_inc(s["rowid_ready"], 1)
                    wait_apart(pool, s["rowid_ready"], b * 3 + 1, passed["pool"])
                    g.tensor_scalar(tokid[:], tokid[:], float(N), 0.0, ALU.add, ALU.add).then_inc(s["rowid_ready"], 1)
                    wait_apart(pool, s["t2_rstd"], b * 4 + 4, passed["pool"])
                    g.tensor_copy(rows[k][:, :, RSTD], rstd3[:])
                    g.tensor_copy(rows[k][:, :, SHIFT], shift3[:]).then_inc(s["rowid_ready"], 1)
                if st == "scatter":
                    wait_apart(pool, s["slot_ready"], b + 1, passed["pool"])
                    wait_apart(pool, s["rowprob_ready"], b + 1, passed["pool"])
                    wait_apart(pool, s["rowid_ready"], b * 3 + 3, passed["pool"])
                    if first:
                        pool.wait_ge(s["fill_done"], 16 * NFILL)
                    for t in range(NT):
                        g.indirect_dma_start(out=slots, out_offset=bass.IndirectOffsetOnAxis(ap=slot_i[k][:, t:t + 1], axis=0),
                                             in_=rows[k][:, t, :], in_offset=None, bounds_check=E * CAP - 1,
                                             oob_is_err=False).then_inc(scattered[k], 16)

            passes(pool, one)

        @block.scalar
        def _(act):
            a = nc.scalar
            act.wait_ge(s["w_loaded"], 16 * NW)
            a.mul(bqs_c[:], bq_c[:], 0.125).then_inc(s["const_act"], 1)
            act.wait_ge(s["const_act"], 1)
            act.wait_ge(s["mask_ready"], 1)

            def normalise(dst, src, rstd_, shift_, j, done):
                for t in range(2 * j, 2 * j + 2):
                    last = a.activation(dst[:, t, :], src[:, t, 0:C], ACT.Identity, bias=shift_[:, t:t + 1],
                                        scale=rstd_[:, t:t + 1])
                if j == 3:
                    last.then_inc(done, 1)

            def one(st, b, m, k):
                first = early(b, 1)
                what, j = (st[0], st[1]) if isinstance(st, tuple) else (st, 0)
                if st == "x_turn":
                    act.wait_ge(s["x_turned"], b + 1)
                    if not first:
                        act.wait_ge(s["t1_ready"], b)
                    a.copy(xT[:].rearrange("p t c -> p (t c)"), workf).then_inc(s["xT_ready"], 1)
                if what == "xn":
                    if j == 0:
                        act.wait_ge(s["x_rstd"], b * 4 + 4)
                        act.wait_ge(s["xT_ready"], b + 1)
                    normalise(xn, xT, rstd, shift, j, s["xn_ready"])
                if what == "u1n":
                    if j == 0:
                        act.wait_ge(s["t_rstd"], b * 4 + 4)
                        if not early(b, 2):
                            act.wait_ge(s["o_ready"], b * 8 - 8)
                    normalise(u1[k], t1[k], rstdt, shiftt, j, s["u1_ready"])
                if what == "ln2n":
                    if j == 0:
                        act.wait_ge(s["o_rstd"], b * 4 + 4)
                    normalise(o[k], o[k], rstd3, shift3, j, s["on_ready"])
                if what == "ln3n":
                    if j == 0:
                        act.wait_ge(s["t2_rstd"], b * 4 + 4)
                    normalise(u2, rows[k], rstd3, shift3, j, s["u2_ready"])
                if st == "xn_turn":
                    act.wait_ge(s["xn_turned"], b + 1)
                    if not first:
                        act.wait_ge(s["bcdt_done"], b)
                    a.activation(xnT[:], workf, ACT.Identity, bias=lnb_c[:], scale=lnw_c[:]).then_inc(s["xnT_ready"], 1)
                if st == "bcdt":
                    act.wait_ge(s["bcdt_done"], b + 1)
                    if not first:
                        act.wait_ge(s["conv_done"], b * 2)
                    a.copy(img[0:U, 1:H + 1, 1:W + 1], workf[0:U, :].rearrange("p (h w) -> p h w", w=W))
                    a.copy(img[U:P, 1:H + 1, 0:W],
                           workf[U:P, :].rearrange("p (h w) -> p h w", w=W)).then_inc(s["img_ready"], 1)
                if st == "dt":
                    act.wait_ge(s["conv_done"], b * 2 + 2)
                    if not first:
                        act.wait_ge(s["y_done"], b)
                    a.copy(cd[0:S, :], workf[0:S, :])
                    act.wait_ge(s["dt_small"], b * 3 + 3)
                    a.activation(cd[S:U, :], workf[S:U, :], ACT.Exp, bias=dts[S:U, 2:3],
                                 accum_out=dts[S:U, 3:4]).then_inc(s["cd_exp"], 1)
                if st == "cd_turn":
                    act.wait_ge(s["cd_turned"], b + 1)
                    if not first:
                        act.wait_ge(s["abT_ready"], b)
                    a.copy(cdT[:].rearrange("p t c -> p (t c)"), work[:, 0, :]).then_inc(s["cdT_ready"], 1)
                if st == "u1_turn":
                    act.wait_ge(s["u1_turned"], b + 1)
                    if not first:
                        act.wait_ge(s["v_done"], b)
                    a.copy(u1T[:], workf).then_inc(s["u1T_ready"], 1)
                    a.activation(absu[:], workf, ACT.Abs).then_inc(s["absu_ready"], 1)
                if st == "q":
                    act.wait_ge(s["q_done"], b + 1)
                    if not first:
                        act.wait_ge(s["qa_ready"], b)
                    a.activation(qz[:], workf[0:U, :], ACT.Identity, bias=bqs_c[:], scale=0.125).then_inc(s["qz_ready"], 1)
                if st == "k":
                    act.wait_ge(s["k_done"], b + 1)
                    if not first:
                        act.wait_ge(s["ka_ready"], b)
                    a.activation(kz[:], workf[0:U, :], ACT.Identity, bias=bk_c[:], scale=1.0).then_inc(s["kz_ready"], 1)
                if what == "mrow":
                    act.wait_ge(s["mrow_done"], b * 2 + (j + 1))
                    a.copy(qa[k][U:U + 1, j * HALF:(j + 1) * HALF], stp[1][U:U + 1, :]).then_inc(s["mrow_ready"], 1)
                if what == "st":
                    kt = st[2]
                    act.wait_ge(s["st_done"], b * 16 + (j * 8 + kt + 1))
                    if kt == 0 and not first:
                        act.wait_ge(s["pv_done"], b * 8 + (4 * j - 4))
                    a.activation(pT[j][:, kt, :], stp[kt % 2][:], ACT.Exp).then_inc(s["exp_ready"], 1)
                if st == "u2_turn":
                    act.wait_ge(s["u2_turned"], b + 1)
                    if not first:
                        act.wait_ge(s["gate_done"], b)
                    a.copy(u2T[:], workf).then_inc(s["u2T_ready"], 1)
                if st == "gate":
                    act.wait_ge(s["gate_chain"], b * 13 + 2)
                    a.activation(eg[:], lg[:], ACT.Exp).then_inc(s["eg_ready"], 1)

            passes(act, one)

        @block.vector
        def _(dve):
            v = nc.vector
            dve.wait_ge(s["w_loaded"], 16 * NW)
            dve.wait_ge(s["mask_ready"], 1)
            for ii in range(2):
                for tap in range(9):
                    wi = wexp[:, tap, :].rearrange("o (g i) -> o g i", i=2)[:, :, ii]
                    mi = gmask[:].rearrange("o (g i) -> o g i", i=2)[:, :, ii]
                    last = v.tensor_tensor(wi, mi, wgr[:, ii, tap:tap + 1].to_broadcast([U, S]), ALU.mult)
            last.then_inc(s["wexp_ready"], 1)
            dve.wait_ge(s["taps_psum"], 1)
            for kh in range(3):
                v.tensor_copy(wtap2[:, kh, :], work[:, 0, kh * U:(kh + 1) * U])
                last = v.tensor_copy(wtap1[:, kh, :], work[0:U, 1, kh * U:(kh + 1) * U])
            last.then_inc(s["taps_ready"], 1)

            def stats(src, bn_, mv_, j, got, done, b):
                for t in range(4 * j, 4 * j + 4):
                    last = v.bn_stats(bn_[:, t, :], src[:, t, :])
                last.then_inc(got, 1)
                wait_apart(dve, got, b * 2 + (j + 1), passed["dve"])
                for t in range(4 * j, 4 * j + 4):
                    last = v.bn_aggr(mv_[:, t, :], bn_[:, t, :])
                if j == 1:
                    last.then_inc(done, 1)

            def lrelu(dst, zs):
                return v.scalar_tensor_tensor(out=dst, in0=zs, scalar=0.2, in1=zs, op0=ALU.mult, op1=ALU.max)

            def mx_reads(b, c, n0, n1):
                for n in range(n0, n1):
                    qt = 4 * c + n // 2
                    dve.wait_ge(s["mx_done"], b * 16 + (c * 8 + n + 1))
                    v.reduce_max(mxs[:, qt, n % 2:n % 2 + 1], mxp[n % 2][:], AX).then_inc(s["mx_read"], 1)

            def negmax(b, c):
                dve.wait_ge(s["mx_read"], b * 16 + (c * 8 + 8))
                v.tensor_reduce(nmx[:, 4 * c:4 * c + 4], mxs[:, 4 * c:4 * c + 4, :], AX, ALU.max,
                                negate=True).then_inc(s["negmax_ready"], 1)

            def one(st, b, m, k):
                first = early(b, 1)
                what, j = (st[0], st[1]) if isinstance(st, tuple) else (st, 0)
                if what == "xs":
                    dve.wait_ge(s["xT_ready"], b + 1)
                    stats(xT, bn, mv, j, s["x_stats"], s["x_mv"], b)
                if st == "dt":
                    dve.wait_ge(s["conv_done"], b * 2 + 2)
                    if not first:
                        dve.wait_ge(s["cd_exp"], b)
                    v.reduce_max(dts[S:U, 0:1], workf[S:U, :], AX).then_inc(s["dt_small"], 1)
                    dve.wait_ge(s["dt_small"], b * 3 + 1)
                    v.tensor_tensor(dts[S:U, 1:2], dts[S:U, 0:1], A_c[S:U, :], ALU.add).then_inc(s["dt_small"], 1)
                    dve.wait_ge(s["dt_small"], b * 3 + 2)
                    v.tensor_tensor(dts[S:U, 2:3], A_c[S:U, :], dts[S:U, 1:2], ALU.subtract).then_inc(s["dt_small"], 1)
                if st == "asm":
                    dve.wait_ge(s["cd_exp"], b + 1)
                    v.reciprocal(dtr[S:U, :], dts[S:U, 3:4]).then_inc(s["dt_sumr"], 1)
                    dve.wait_ge(s["dt_sumr"], b + 1)
                    v.tensor_scalar(cd[S:U, :], cd[S:U, :], dtr[S:U, :], None, ALU.mult).then_inc(s["asm_ready"], 1)
                if st == "h":
                    dve.wait_ge(s["h_done"], b + 1)
                    v.tensor_copy(hs[:], work[:, 1, 0:S]).then_inc(s["h_ready"], 1)
                if st == "g":
                    dve.wait_ge(s["g_done"], b + 1)
                    v.tensor_copy(gs[:], work[0:S, 0, 0:C]).then_inc(s["g_ready"], 1)
                if st == "y":
                    dve.wait_ge(s["y_done"], b + 1)
                    if not early(b, 2):
                        dve.wait_ge(s["t1b_ready"], b - 1)
                    v.tensor_tensor(t1[k][:], workt, xT[:], ALU.add).then_inc(s["t1_ready"], 1)
                if st == "ts":
                    dve.wait_ge(s["t1_ready"], b + 1)
                    for h in range(2):
                        stats(t1[k], bn, mvt, h, s["t_stats"], s["t_mv"], b)
                if st == "q":
                    dve.wait_ge(s["qz_ready"], b + 1)
                    lrelu(qa[k][0:U, :], qz[:]).then_inc(s["qa_ready"], 1)
                if st == "k":
                    dve.wait_ge(s["k_done"], b + 1)
                    v.tensor_scalar(ka[k][U:KA, :], workf[U:KA, :], 0.0, kscale[U:KA, :], ALU.is_equal, ALU.mult)\
                        .then_inc(s["kmask_ready"], 1)
                    dve.wait_ge(s["kz_ready"], b + 1)
                    lrelu(ka[k][0:U, :], kz[:]).then_inc(s["ka_ready"], 1)
                if st == "v":
                    dve.wait_ge(s["v_done"], b + 1)
                    v.tensor_tensor(vz[:], workt, bc_mid(bv_r[:], NT), ALU.add).then_inc(s["vz_ready"], 1)
                    dve.wait_ge(s["vz_ready"], b + 1)
                    lrelu(va[k][:, :, 0:C], vz[:]).then_inc(s["va_ready"], 1)
                if what == "st" and j == 0:
                    mx_reads(b, 1, st[2], st[2] + 1)
                if what == "pv":
                    n = st[2]
                    qt = 4 * j + n
                    dve.wait_ge(s["pv_done"], b * 8 + (qt + 1))
                    v.reciprocal(prv[:, qt:qt + 1], pvp[qt % 2][:, C:VA]).then_inc(s["pv_rinv"], 1)
                    dve.wait_ge(s["pv_rinv"], b * 8 + (qt + 1))
                    v.scalar_tensor_tensor(out=o[k][:, qt, :], in0=pvp[qt % 2][:, 0:C], scalar=prv[:, qt:qt + 1],
                                           in1=u1[k][:, qt, :], op0=ALU.mult, op1=ALU.add).then_inc(s["o_ready"], 1)
                    if j == 1 and not (isinstance(b, int) and b == B - 1):
                        mx_reads(b + 1, 0, 2 * n, 2 * n + 2)
                if st == "mx_first":
                    mx_reads(b, 0, 0, 8)
                if what == "ln2s":
                    if j == 0:
                        dve.wait_ge(s["o_ready"], b * 8 + 8)
                    stats(o[k], bn3, mv3, j, s["o_stats"], s["o_mv"], b)
                if st == "ln2g":
                    dve.wait_ge(s["on_ready"], b + 1)
                    v.tensor_tensor(o[k][:], o[k][:], bc_mid(gamma_r[:], NT), ALU.mult).then_inc(s["ong_ready"], 1)
                    dve.wait_ge(s["ong_ready"], b + 1)
                    v.tensor_tensor(rows[k][:, :, 0:C], rows[k][:, :, 0:C], o[k][:], ALU.add).then_inc(s["t2_ready"], 1)
                if what == "ln3s":
                    dve.wait_ge(s["t2_ready"], b + 1)
                    stats(rows[k][:, :, 0:C], bn3, mv3, j, s["t2_stats"], s["t2_mv"], b)
                if what == "negmax":
                    negmax(b, j)
                if st == "gate":
                    gc = s["gate_chain"]
                    cnt = [0]

                    def link(ins):
                        cnt[0] += 1
                        ins.then_inc(gc, 1)
                        dve.wait_ge(gc, b * 13 + cnt[0])
                    dve.wait_ge(s["gate_done"], b + 1)
                    lgw = work[:, 0, 0:NT * E].rearrange("p (t e) -> p t e", e=E)
                    link(v.tensor_tensor(ra[:], lgw, bc_mid(gb_r[:], NT), ALU.add))
                    v.reduce_max(r8[:, 0, :], ra[:], AX).then_inc(s["lg_ready"], 1)
                    dve.wait_ge(s["lg_ready"], b + 1)
                    link(v.tensor_tensor(lg[:], ra[:], bc_last(r8[:, 0, :], E), ALU.subtract))
                    dve.wait_ge(s["eg_ready"], b + 1)
                    link(v.reduce_sum(r8[:, 1, :], eg[:], AX))
                    link(v.reduce_max(r8[:, 2, :], eg[:], AX))
                    link(v.reciprocal(r8[:, 3, :], r8[:, 1, :]))
                    v.tensor_tensor(rows[k][:, :, PROB], r8[:, 2, :], r8[:, 3, :], ALU.mult).then_inc(s["rowprob_ready"], 1)
                    link(v.tensor_tensor(ra[:], eg[:], bc_last(r8[:, 2, :], E), ALU.is_equal))
                    link(v.tensor_tensor(rb[:], ra[:], rank[:], ALU.mult))
                    link(v.reduce_max(r8[:, 4, :], rb[:], AX))
                    link(v.tensor_tensor(oh[:], rb[:], bc_last(r8[:, 4, :], E), ALU.is_equal))
                    v.tensor_copy(oh_bf[:], oh[:]).then_inc(s["ohb_ready"], 1)
                if st == "pos":
                    gc = s["gate_chain"]
                    cnt = [9]

                    def link2(ins):
                        cnt[0] += 1
                        ins.then_inc(gc, 1)
                        dve.wait_ge(gc, b * 13 + cnt[0])
                    dve.wait_ge(s["pos_done"], b + 1)
                    pw = work[:, 1, 0:(NT + 1) * E].rearrange("p (t e) -> p t e", e=E)
                    link2(v.tensor_tensor(ra[:], pw[:, 0:NT, :], run[:].to_broadcast([P, NT, E]), ALU.add))
                    v.tensor_tensor(run[:], pw[:, NT:NT + 1, :], run[:], ALU.add)
                    v.tensor_tensor(rb[:], ra[:], oh[:], ALU.mult)
                    link2(v.tensor_tensor(rc[:], ra[:], eoff[:], ALU.add))
                    v.reduce_sum(r8[:, 4, :], rb[:], AX)
                    link2(v.tensor_tensor(rd[:], rc[:], oh[:], ALU.mult))
                    v.tensor_scalar(r8[:, 4, :], r8[:, 4, :], float(CAP), DROP, ALU.is_ge, ALU.mult)
                    link2(v.reduce_sum(r8[:, 5, :], rd[:], AX))
                    v.tensor_tensor(slot_i[k][:], r8[:, 4, :], r8[:, 5, :], ALU.add).then_inc(s["slot_ready"], 1)

            passes(dve, one)

        @block.tensor
        def _(pe):
            mm = nc.tensor.matmul
            pe.wait_ge(s["w_loaded"], 16 * NW)
            pe.wait_ge(s["mask_ready"], 1)
            pe.wait_ge(s["wexp_ready"], 1)
            for kh in range(3):
                nc.tensor.transpose(work[:, 0, kh * U:(kh + 1) * U],
                                    wexp[:, 3 * kh:3 * kh + 2, :].rearrange("o a i -> o (a i)"), ident[0:U, 0:U])
                last = nc.tensor.transpose(work[0:U, 1, kh * U:(kh + 1) * U], wexp[:, 3 * kh + 2, :], ident[0:U, 0:U])
            last.then_inc(s["taps_psum"], 1)
            pe.wait_ge(s["taps_ready"], 1)

            def turn(src, done):
                for t in range(NT):
                    last = nc.tensor.transpose(workt[:, t, :], src(t), ident[:])
                last.then_inc(done, 1)

            def mx_items(b, k, c, n0, n1):
                for n in range(n0, n1):
                    qt = 4 * c + n // 2
                    if not (isinstance(b, int) and b == 0 and c == 0 and n < 2):
                        pe.wait_ge(s["mx_read"], b * 16 + (c * 8 + n - 1))
                    mm(mxp[n % 2][:], qb[k][:, qt * P:(qt + 1) * P], kb[k][:, (n % 2) * HALF:(n % 2 + 1) * HALF],
                       start=True, stop=True).then_inc(s["mx_done"], 1)

            def one(st, b, m, k):
                first = early(b, 1)
                if st == "x_turn":
                    pe.wait_ge(x_loaded[k], m * 16 + 16)
                    if not first:
                        pe.wait_ge(s["t1_ready"], b)
                    turn(lambda t: xs[k][:, t * P:(t + 1) * P], s["x_turned"])
                if st == "xn_turn":
                    pe.wait_ge(s["xn_ready"], b + 1)
                    if not first:
                        pe.wait_ge(s["vz_ready"], b)
                    turn(lambda t: xn[:, t, :], s["xn_turned"])
                if st == "bcdt":
                    pe.wait_ge(s["xnT_ready"], b + 1)
                    for h in range(2):
                        last = mm(work[:, h, :], wbc[:].rearrange("p a u -> p (a u)"), xnT[:, h * HALF:(h + 1) * HALF],
                                  start=True, stop=True)
                    last.then_inc(s["bcdt_done"], 1)
                if isinstance(st, tuple) and st[0] == "conv":
                    h = st[1]
                    pe.wait_ge(s["img_ready"], b + 1)
                    r0 = h * (H // 2)
                    for kh in range(3):
                        mm(work[0:U, h, :], wtap2[:, kh, :], img[:, r0 + kh:r0 + kh + H // 2, 0:W],
                           start=(kh == 0), stop=False)
                        last = mm(work[0:U, h, :], wtap1[:, kh, :], img[0:U, r0 + kh:r0 + kh + H // 2, 2:2 + W],
                                  start=False, stop=(kh == 2))
                    last.then_inc(s["conv_done"], 1)
                if st == "cd_turn":
                    wait_apart(pe, s["asm_ready"], b + 1, passed["pe"])
                    if not early(b, 3):
                        wait_apart(pe, s["gate_chain"], b * 13 - 38, passed["pe"])
                    for t in range(NT):
                        last = nc.tensor.transpose(work[:, 0, t * U:(t + 1) * U], cd[:, t * P:(t + 1) * P],
                                                   ident[0:U, 0:U])
                    last.then_inc(s["cd_turned"], 1)
                if st == "h":
                    pe.wait_ge(s["abT_ready"], b + 1)
                    if not early(b, 3):
                        pe.wait_ge(s["gate_chain"], b * 13 - 28)
                    for t in range(NT):
                        last = mm(work[:, 1, 0:S], xT[:, t, :], abT[:, t, :], start=(t == 0), stop=(t == NT - 1))
                    last.then_inc(s["h_done"], 1)
                if st == "g":
                    pe.wait_ge(s["h_ready"], b + 1)
                    mm(work[0:S, 0, 0:C], hs[:], wot[:], start=True, stop=True).then_inc(s["g_done"], 1)
                if st == "y":
                    pe.wait_ge(s["g_ready"], b + 1)
                    for t in range(NT):
                        last = mm(workt[:, t, :], cd[0:S, t * P:(t + 1) * P], gs[:], start=True, stop=True)
                    last.then_inc(s["y_done"], 1)
                if st == "u1_turn":
                    pe.wait_ge(s["u1_ready"], b + 1)
                    if not (isinstance(b, int) and b >= B - 1):
                        pe.wait_ge(s["xT_ready"], b + 2)
                    turn(lambda t: u1[k][:, t, :], s["u1_turned"])
                if st == "q":
                    pe.wait_ge(s["absu_ready"], b + 1)
                    for h in range(2):
                        last = mm(work[0:U, h, :], wq_s[:], u1T[:, h * HALF:(h + 1) * HALF], start=True, stop=True)
                    last.then_inc(s["q_done"], 1)
                if st == "k":
                    pe.wait_ge(s["qz_ready"], b + 1)
                    for h in range(2):
                        mm(work[0:U, h, :], wk_s[:], u1T[:, h * HALF:(h + 1) * HALF], start=True, stop=True)
                        last = mm(work[U:KA, h, :], onecol_bf[:], absu[:, h * HALF:(h + 1) * HALF], start=True, stop=True)
                    last.then_inc(s["k_done"], 1)
                if st == "v":
                    pe.wait_ge(s["kz_ready"], b + 1)
                    pe.wait_ge(s["kmask_ready"], b + 1)
                    for t in range(NT):
                        last = mm(workt[:, t, :], u1T[:, t * P:(t + 1) * P], wv_s[:], start=True, stop=True)
                    last.then_inc(s["v_done"], 1)
                if isinstance(st, tuple) and st[0] == "st":
                    c, kt = st[1], st[2]
                    if kt == 0:
                        pe.wait_ge(s["mrow_ready"], b * 2 + (c + 1))
                    if not (first and c == 0 and kt < 2):
                        pe.wait_ge(s["exp_ready"], b * 16 + (c * 8 + kt - 1))
                    mm(stp[kt % 2][:], ka[k][:, kt * P:(kt + 1) * P], qa[k][:, c * HALF:(c + 1) * HALF],
                       start=True, stop=True).then_inc(s["st_done"], 1)
                    if c == 0:
                        mx_items(b, k, 1, kt, kt + 1)
                if isinstance(st, tuple) and st[0] == "mrow":
                    c = st[1]
                    pe.wait_ge(s["negmax_ready"], b * 2 + (c + 1))
                    if not (first and c == 0):
                        pe.wait_ge(s["exp_ready"], b * 16 + c * 8)
                    for n in range(4):
                        qt = 4 * c + n
                        last = mm(stp[1][U:U + 1, n * P:(n + 1) * P], nmx[:, qt:qt + 1], ident[:], start=True, stop=True)
                    last.then_inc(s["mrow_done"], 1)
                if isinstance(st, tuple) and st[0] == "pv":
                    c, n = st[1], st[2]
                    qt = 4 * c + n
                    if n == 0:
                        pe.wait_ge(s["exp_ready"], b * 16 + (c * 8 + 8))
                    if n == 0 and c == 0:
                        pe.wait_ge(s["va_ready"], b + 1)
                    if not (first and qt < 2):
                        pe.wait_ge(s["o_ready"], b * 8 + (qt - 1))
                    for kt in range(NT):
                        last = mm(pvp[qt % 2][:, 0:VA], pT[c][:, kt, n * P:(n + 1) * P], va[k][:, kt, :],
                                  start=(kt == 0), stop=(kt == NT - 1))
                    last.then_inc(s["pv_done"], 1)
                    if c == 1 and not (isinstance(b, int) and b == B - 1):
                        if n == 0:
                            pe.wait_ge(s["kb_ready"], b + 2)
                            pe.wait_ge(s["qb_ready"], b + 2)
                        mx_items(b + 1, 1 - k, 0, 2 * n, 2 * n + 2)
                if st == "mx_first":
                    pe.wait_ge(s["kb_ready"], 1)
                    pe.wait_ge(s["qb_ready"], 1)
                    mx_items(b, k, 0, 0, 8)
                if st == "u2_turn":
                    pe.wait_ge(s["u2_ready"], b + 1)
                    if not (isinstance(b, int) and b >= B - 3):
                        pe.wait_ge(s["cd_exp"], b + 4)
                    turn(lambda t: u2[:, t, :], s["u2_turned"])
                if st == "gate":
                    pe.wait_ge(s["u2T_ready"], b + 1)
                    for t in range(NT):
                        last = mm(work[:, 0, t * E:(t + 1) * E], u2T[:, t * P:(t + 1) * P], gw_s[:], start=True, stop=True)
                    last.then_inc(s["gate_done"], 1)
                if st == "pos":
                    pe.wait_ge(s["ohb_ready"], b + 1)
                    ohf = oh_bf[:].rearrange("p t e -> p (t e)")
                    mm(work[:, 1, 0:NT * E], before_bf[:], ohf, start=True, stop=False, skip_group_check=True)
                    for d in range(NT):
                        last = mm(work[:, 1, (d + 1) * E:(NT + 1) * E], ones_bf[:], ohf[:, 0:(NT - d) * E],
                                  start=False, stop=(d == NT - 1), skip_group_check=True)
                    last.then_inc(s["pos_done"], 1)

            passes(pe, one)



def expert_program(nc, slots, tokens, w1, b1, w2, b2, sems):
    with ExitStack() as ctx:
        def sb(name, shape, dt=F32):
            return ctx.enter_context(nc.sbuf_tensor(name, shape, dt))

        def sem(name):
            return sems.enter_context(nc.semaphore(name))

        ident = sb("e_ident", [P, P])
        zeros = sb("e_zeros", [P, G, C])
        w1s = [sb(f"w1s{k}", [P, F]) for k in range(2)]
        w2s = [sb(f"w2s{k}", [P, FC, C]) for k in range(2)]
        b1c = [sb(f"b1c{k}", [P, FC]) for k in range(2)]
        b2r = [sb(f"b2r{k}", [P, C]) for k in range(2)]
        rows = [sb(f"e_rows{k}", [P, G, ROW]) for k in range(2)]
        kept = [sb(f"kept{k}", [P, G, ROW]) for k in range(2)]
        u = sb("e_u", [P, G, C])
        uT = [sb(f"e_uT{k}", [P, BLK]) for k in range(2)]
        hid = [sb(f"hid{k}", [P, BLK]) for k in range(4)]
        yb = sb("yb", [P, G, C])
        z = sb("z", [P, G, C])
        isnan = sb("isnan", [P, G, C], I32)
        isfin = sb("isfin", [P, G, C], I32)
        ysafe = sb("ysafe", [P, G, C])
        res = [sb(f"res{k}", [P, G, C]) for k in range(2)]
        tp = [ctx.enter_context(nc.psum_tensor(f"e_tp{k}", [P, BLK], F32)) for k in range(2)]
        hp = [ctx.enter_context(nc.psum_tensor(f"e_hp{k}", [P, BLK], F32)) for k in range(2)]
        yp = [ctx.enter_context(nc.psum_tensor(f"e_yp{k}", [P, G, C], F32)) for k in range(2)]

        names = """e_const e_ident_ready e_u_ready e_turned e_uT_ready e_kept
        e_hid_done e_hid_ready e_y_done e_yb_ready e_guard e_res_ready""".split()
        s = {n: sem(n) for n in names}
        passed = {n: sem(f"e_passed_{n}") for n in ("sp", "pool", "dve", "pe")}
        w_loaded, rows_loaded, stored = ([sem(f"e_{n}{k}") for k in range(2)] for n in ("w_loaded", "rows_loaded", "stored"))
        NBLKS = E * NBLK

        def blocks(eng, one, before=None):
            def expert(e, par, first=False, last=False):
                if before:
                    before(e, par, last)
                lo, hi = (2 if first else 1), (NBLK // 2 - 1 if last else NBLK // 2)
                one(e * NBLK, 0, par, True, first, False)
                one(e * NBLK + 1, 1, par, False, False, False)
                if first:
                    one(e * NBLK + 2, 0, par, False, False, False)
                    one(e * NBLK + 3, 1, par, False, False, False)
                with eng.Fori(lo, hi) as j:
                    one(e * NBLK + j * 2, 0, par, False, False, False)
                    one(e * NBLK + j * 2 + 1, 1, par, False, False, False)
                if last:
                    one(e * NBLK + NBLK - 2, 0, par, False, False, False)
                    one(e * NBLK + NBLK - 1, 1, par, False, False, True)
            expert(0, 0, first=True)
            expert(1, 1)
            with eng.Fori(1, E // 2 - 1) as i:
                expert(i * 2, 0)
                expert(i * 2 + 1, 1)
            expert(E - 2, 0)
            expert(E - 1, 1, last=True)

        def wait_rows(eng, n, half):
            eng.wait_ge(rows_loaded[half], n * 8 + (16 if half == 0 else 8))

        block = ctx.enter_context(nc.Block())

        @block.sync
        def _(sp):
            def load_w(e, par):
                for dst, src in ((w1s[par][:], w1[bass.ds(e, 1)].rearrange("o d f -> (o d) f")),
                                 (w2s[par][:], w2[bass.ds(e, 1)].rearrange("o (c p) d -> p (o c) d", p=P)),
                                 (b1c[par][:], b1[bass.ds(e, 1)].rearrange("o p c -> (o p) c")),
                                 (b2r[par][:], b2[bass.ds(e, 1)].rearrange("o d -> (o d)").partition_broadcast(P))):
                    sp.dma_start(dst, src).then_inc(w_loaded[par], 16)

            def load_rows(n, half):
                sp.dma_start(rows[half][:].rearrange("p g d -> p (g d)"),
                             slots[bass.ds(n * BLK, BLK)].rearrange("(p g) d -> p (g d)", p=P)).then_inc(rows_loaded[half], 16)

            load_rows(0, 0)
            load_w(0, 0)
            state = {}

            def before(e, par, last):
                state["e"] = None if last else e

            def one(n, half, par, j0, first, last):
                if not last:
                    if not first:
                        wait_apart(sp, s["e_kept"], n, passed["sp"])
                    load_rows(n + 1, 1 - half)
                if j0 and state["e"] is not None:
                    if not first:
                        wait_apart(sp, s["e_y_done"], n, passed["sp"])
                        wait_apart(sp, s["e_yb_ready"], n * 2, passed["sp"])
                    load_w(state["e"] + 1, 1 - par)

            blocks(sp, one, before)

        @block.gpsimd
        def _(pool):
            g = nc.gpsimd
            g.memset(ident[:], 0.0).then_inc(s["e_const"], 1)
            pool.wait_ge(s["e_const"], 1)
            g.memset(zeros[:], 0.0).then_inc(s["e_const"], 1)
            g.affine_select(out=ident[:], in_=ident[:], pattern=[[-1, P]], compare_op=ALU.not_equal, fill=1.0,
                            base=0, channel_multiplier=1).then_inc(s["e_ident_ready"], 1)

            def store(n, half):
                wait_apart(pool, s["e_res_ready"], n + 1, passed["pool"])
                for q in range(G):
                    g.indirect_dma_start(out=tokens, out_offset=bass.IndirectOffsetOnAxis(
                        ap=kept[half][:, q, TOKEN:TOKEN + 1].bitcast(I32), axis=0), in_=res[half][:, q, :], in_offset=None,
                        bounds_check=T - 1, oob_is_err=False).then_inc(stored[half], 16)

            def one(n, half, par, j0, first, last):
                if not first:
                    store(n - 1, 1 - half)

            blocks(pool, one)
            store(NBLKS - 1, 1)

        @block.scalar
        def _(act):
            a = nc.scalar

            def prep(n, half):
                wait_rows(act, n, half)
                if not (isinstance(n, int) and n == 0):
                    act.wait_ge(s["e_turned"], n)
                for q in range(G):
                    last = a.activation(u[:, q, :], rows[half][:, q, 0:C], ACT.Identity,
                                        bias=rows[half][:, q, SHIFT:SHIFT + 1], scale=rows[half][:, q, RSTD:RSTD + 1])
                last.then_inc(s["e_u_ready"], 1)

            def keep(n, half):
                if not (isinstance(n, int) and n < 2):
                    act.wait_ge(stored[half], (n - half) * 32)
                wait_rows(act, n, half)
                a.copy(kept[half][:], rows[half][:]).then_inc(s["e_kept"], 1)

            def turned(n, half):
                act.wait_ge(s["e_turned"], n + 1)
                if not (isinstance(n, int) and n < 2):
                    act.wait_ge(s["e_hid_done"], n * FC - FC)
                a.copy(uT[half][:], tp[half][:]).then_inc(s["e_uT_ready"], 1)

            def relu(n, f, par):
                act.wait_ge(s["e_hid_done"], n * FC + (f + 1))
                a.activation(hid[f][:], hp[f % 2][:], ACT.Relu, bias=b1c[par][:, f:f + 1], scale=1.0)\
                    .then_inc(s["e_hid_ready"], 1)

            def one(n, half, par, j0, first, last):
                relu(n, 0, par)
                if not last:
                    prep(n + 1, 1 - half)
                relu(n, 1, par)
                relu(n, 2, par)
                if not last:
                    turned(n + 1, 1 - half)
                relu(n, 3, par)
                if not last:
                    keep(n + 1, 1 - half)
            prep(0, 0)
            turned(0, 0)
            keep(0, 0)
            blocks(act, one)

        @block.vector
        def _(dve):
            v = nc.vector

            def result(n, half, par, early2):
                dve.wait_ge(s["e_kept"], n + 1)
                dve.wait_ge(s["e_y_done"], n + 1)
                v.tensor_tensor(yb[:], yp[half][:], b2r[par][:].unsqueeze(1).to_broadcast([P, G, C]), ALU.add)\
                    .then_inc(s["e_yb_ready"], 1)
                dve.wait_ge(s["e_yb_ready"], n * 2 + 1)
                v.tensor_tensor(z[:], yb[:], kept[half][:, :, PROB:PROB + 1].to_broadcast([P, G, C]), ALU.mult)\
                    .then_inc(s["e_yb_ready"], 1)
                dve.wait_ge(s["e_yb_ready"], n * 2 + 2)
                v.tensor_scalar(ysafe[:], z[:], -NAN_CLIP, NAN_CLIP, ALU.max, ALU.min)
                v.tensor_tensor(isnan[:], z[:], z[:], ALU.not_equal)
                v.tensor_scalar(isfin[:], z[:], 0.0, 0.0, ALU.mult, ALU.is_equal).then_inc(s["e_guard"], 1)
                wait_apart(dve, s["e_guard"], n * 3 + 1, passed["dve"])
                v.copy_predicated(ysafe[:], isnan[:], zeros[:]).then_inc(s["e_guard"], 1)
                wait_apart(dve, s["e_guard"], n * 3 + 2, passed["dve"])
                v.copy_predicated(ysafe[:], isfin[:], z[:]).then_inc(s["e_guard"], 1)
                dve.wait_ge(s["e_guard"], n * 3 + 3)
                if not early2:
                    dve.wait_ge(stored[half], (n - half) * 32)
                v.tensor_tensor(res[half][:], ysafe[:], kept[half][:, :, 0:C], ALU.add).then_inc(s["e_res_ready"], 1)

            def one(n, half, par, j0, first, last):
                if not first:
                    result(n - 1, 1 - half, 1 - par if j0 else par, isinstance(n, int) and n - 1 < 2)

            dve.wait_ge(s["e_ident_ready"], 1)
            blocks(dve, one)
            result(NBLKS - 1, 1, 1, False)

        @block.tensor
        def _(pe):
            mm = nc.tensor.matmul
            pe.wait_ge(s["e_ident_ready"], 1)

            def turn(n, half):
                pe.wait_ge(s["e_u_ready"], n + 1)
                for q in range(G):
                    last = nc.tensor.transpose(tp[half][:, q * P:(q + 1) * P], u[:, q, :], ident[:])
                last.then_inc(s["e_turned"], 1)

            def layer1(n, half, par, f):
                if not (isinstance(n, int) and n == 0 and f < 2):
                    pe.wait_ge(s["e_hid_ready"], n * FC + (f - 1))
                mm(hp[f % 2][:], w1s[par][:, f * P:(f + 1) * P], uT[half][:], start=True, stop=True)\
                    .then_inc(s["e_hid_done"], 1)

            def layer2(n, half, par, f):
                pe.wait_ge(s["e_hid_ready"], n * FC + (f + 1))
                for q in range(G):
                    last = mm(yp[half][:, q, :], hid[f][:, q * P:(q + 1) * P], w2s[par][:, f, :],
                              start=(f == 0 and q == 0), stop=(f == FC - 1), skip_group_check=True)
                if f == FC - 1:
                    last.then_inc(s["e_y_done"], 1)

            turn(0, 0)

            def before(e, par, last):
                pe.wait_ge(w_loaded[par], (e * 32 + 64) if par == 0 else (e * 32 + 32))

            def one(n, half, par, j0, first, last):
                pe.wait_ge(s["e_uT_ready"], n + 1)
                layer1(n, half, par, 0)
                layer1(n, half, par, 1)
                if not (isinstance(n, int) and n < 2):
                    pe.wait_ge(s["e_yb_ready"], n * 2 - 3)
                layer2(n, half, par, 0)
                layer1(n, half, par, 2)
                if not last:
                    turn(n + 1, 1 - half)
                layer2(n, half, par, 1)
                layer1(n, half, par, 3)
                layer2(n, half, par, 2)
                layer2(n, half, par, 3)

            blocks(pe, one, before)

        @block.sync
        def _(sp):
            for k in range(2):
                sp.wait_ge(stored[k], NBLKS // 2 * G * 16)


def output_program(nc, tokens, out, sems):
    with ExitStack() as ctx:
        def sem(name):
            return sems.enter_context(nc.semaphore(name))

        ident = ctx.enter_context(nc.sbuf_tensor("f_ident", [P, P], F32))
        rows = [ctx.enter_context(nc.sbuf_tensor(f"f_rows{k}", [P, NT, C], F32)) for k in range(4)]
        cols = [ctx.enter_context(nc.sbuf_tensor(f"f_cols{k}", [P, N], F32)) for k in range(2)]
        ps = [ctx.enter_context(nc.psum_tensor(f"f_ps{k}", [P, 2, HALF], F32)) for k in range(2)]
        ident_set, ident_ready, turned, lo_ready, hi_ready = (sem(f"f_{n}") for n in
                                                              ("ident_set", "ident_ready", "turned", "lo_ready", "hi_ready"))
        loaded = [sem(f"f_loaded{k}") for k in range(4)]
        stored = [sem(f"f_stored{k}") for k in range(2)]
        passed = {"sp": sem("f_passed_sp")}
        R = 4
        block = ctx.enter_context(nc.Block())

        @block.sync
        def _(sp):
            def load(b, r):
                sp.dma_start(rows[r][:], tokens[bass.ds(b * N, N)].rearrange("(t p) c -> p t c", p=P)).then_inc(loaded[r], 16)
            for r in range(R):
                load(r, r)
            with sp.Fori(1, B // R) as i:
                for r in range(R):
                    wait_apart(sp, turned, i * R + (r + 1 - R), passed["sp"])
                    load(i * R + r, r)

        @block.gpsimd
        def _(pool):
            nc.gpsimd.memset(ident[:], 0.0).then_inc(ident_set, 1)
            pool.wait_ge(ident_set, 1)
            nc.gpsimd.affine_select(out=ident[:], in_=ident[:], pattern=[[-1, P]], compare_op=ALU.not_equal, fill=1.0,
                                    base=0, channel_multiplier=1).then_inc(ident_ready, 1)

        @block.tensor
        def _(pe):
            pe.wait_ge(ident_ready, 1)

            def one(i, r):
                pe.wait_ge(loaded[r], i * 16 + 16)
                if not (isinstance(i, int) and r < 2):
                    pe.wait_ge(lo_ready, i * R + (r - 1))
                    pe.wait_ge(hi_ready, i * R + (r - 1))
                for t in range(NT):
                    last = nc.tensor.transpose(ps[r % 2][:, t // 4, (t % 4) * P:(t % 4 + 1) * P], rows[r][:, t, :], ident[:])
                last.then_inc(turned, 1)
            for r in range(R):
                one(0, r)
            with pe.Fori(1, B // R) as i:
                for r in range(R):
                    one(i, r)

        @block.scalar
        def _(act):
            def one(i, r):
                act.wait_ge(turned, i * R + (r + 1))
                if not (isinstance(i, int) and r < 2):
                    act.wait_ge(stored[r % 2], i * 32 + (r // 2) * 16)
                nc.scalar.copy(cols[r % 2][:, 0:HALF], ps[r % 2][:, 0, :]).then_inc(lo_ready, 1)
                act.wait_ge(lo_ready, i * R + (r + 1))
                act.wait_ge(hi_ready, i * R + (r + 1))
                act.dma_start(out[bass.ds(i * R + r, 1)].rearrange("o c n -> (o c) n"), cols[r % 2][:]).then_inc(stored[r % 2], 16)
            for r in range(R):
                one(0, r)
            with act.Fori(1, B // R) as i:
                for r in range(R):
                    one(i, r)
            for k in range(2):
                act.wait_ge(stored[k], B // 2 * 16)

        @block.vector
        def _(dve):
            def one(i, r):
                dve.wait_ge(turned, i * R + (r + 1))
                if not (isinstance(i, int) and r < 2):
                    dve.wait_ge(stored[r % 2], i * 32 + (r // 2) * 16)
                nc.vector.tensor_copy(cols[r % 2][:, HALF:N], ps[r % 2][:, 1, :]).then_inc(hi_ready, 1)
            for r in range(R):
                one(0, r)
            with dve.Fori(1, B // R) as i:
                for r in range(R):
                    one(i, r)


def program(nc, a, out):
    slots = nc.dram_tensor("expert_slots", [E * CAP, ROW], F32, kind="Internal").ap()
    tokens = nc.dram_tensor("token_rows", [T, C], F32, kind="Internal").ap()
    with ExitStack() as sems:
        token_program(nc, a["x"], a["ln_w"], a["ln_b"], a["w_bcdt_t"], a["w_gw"], a["w_out_t"], a["A"], a["Wq"], a["bq"],
                      a["Wk"], a["bk"], a["Wv"], a["bv"], a["gamma"], a["beta"], a["gate_w"], a["gate_b"],
                      slots, tokens, sems)
        expert_program(nc, slots, tokens, a["w1"], a["b1"], a["w2"], a["b2"], sems)
        output_program(nc, tokens, out, sems)


def kernel(**inputs):
    import numpy as np
    import concourse.bacc as bacc
    from concourse.bass_utils import run_bass_kernel_spmd

    def get(name):
        return np.asarray(inputs[name])

    lay = {
        "x": get("x").reshape(B, C, N),
        "ln_w": get("L0_conv_ln_w").reshape(C, 1), "ln_b": get("L0_conv_ln_b").reshape(C, 1),
        "w_bcdt_t": get("L0_conv_w_bcdt").reshape(U, C).T, "w_gw": get("L0_conv_w_gw").reshape(U, 2, 9),
        "w_out_t": get("L0_conv_w_out").reshape(C, C).T, "A": get("L0_conv_A"),
        "Wq": get("L1_attn_Wq"), "bq": get("L1_attn_bq"), "Wk": get("L1_attn_Wk"), "bk": get("L1_attn_bk"),
        "Wv": get("L1_attn_Wv"), "bv": get("L1_attn_bv"), "gamma": get("L1_attn_gamma"), "beta": get("L1_attn_beta"),
        "gate_w": get("L1_ffn_gate_w"), "gate_b": get("L1_ffn_gate_b"), "w1": get("L1_ffn_w1"),
        "b1": get("L1_ffn_b1").reshape(E, FC, P).transpose(0, 2, 1),
        "w2": get("L1_ffn_w2"), "b2": get("L1_ffn_b2"),
    }
    nc = bacc.Bacc("TRN2", target_bir_lowering=False, num_devices=1)
    arrays = {f"in_{n}": np.ascontiguousarray(v) for n, v in lay.items()}
    args = {n: nc.dram_tensor(f"in_{n}", arrays[f"in_{n}"].shape, mybir.dt.from_np(arrays[f"in_{n}"].dtype),
                              kind="ExternalInput").ap() for n in lay}
    out = nc.dram_tensor("out", [B, C, N], F32, kind="ExternalOutput").ap()
    program(nc, args, out)
    r = run_bass_kernel_spmd(nc, [arrays], core_ids=[0])
    return r.results[0]["out"].reshape(B, C, H, W)
```

```python
from contextlib import ExitStack

import concourse.bass as bass
from concourse import mybir

F32 = mybir.dt.float32
BF16 = mybir.dt.bfloat16
I32 = mybir.dt.int32
F32R = mybir.dt.float32r
ALU = mybir.AluOpType
ACT = mybir.ActivationFunctionType
AX = mybir.AxisListType.X

P = 128
B, C, H, W = 32, 128, 32, 32
N = H * W
NT = N // P
S = 32
HP, WP = H + 2, W + 2
U = 64
KA = U + 2
VA = C + 1
HALF = 512
E, F = 8, 512
FC = F // P
T = B * N
CAP = -(-5 * T // (4 * E))
ROW = C + 4
TOKEN, PROB, RSTD, SHIFT = range(C, ROW)
BLK = 512
G = BLK // P
NBLK = CAP // BLK
FILL_ROWS = 10
NFILL = E * CAP // (P * FILL_ROWS)
NO_TOKEN = 1 << 24
DROP = float(1 << 20)
NEG_FILL = -2.0 ** 32 + 1.0
NAN_CLIP = 10000.0
HIGH_BITS = -(1 << 12)


def early(b, n):
    return isinstance(b, int) and b < n


def wait_apart(eng, sem, value, passed):
    eng.wait_ge(sem, value)
    if not isinstance(value, int):
        eng.sem_inc(passed, 1)


def token_program(nc, x, ln_w, ln_b, w_bcdt_t, w_gw, w_out_t, A, Wq, bq, Wk, bk, Wv, bv, gamma, beta,
                  gate_w, gate_b, slots, tokens, sems):
    with ExitStack() as ctx:
        def sb(name, shape, dt=F32):
            return ctx.enter_context(nc.sbuf_tensor(name, shape, dt))

        def sem(name):
            return sems.enter_context(nc.semaphore(name))

        NW = 17

        ident = sb("ident", [P, P])
        ones_bf = sb("ones_bf", [P, P], BF16)
        before_bf = sb("before_bf", [P, P], BF16)
        onecol_bf = sb("onecol_bf", [P, 2], BF16)
        lnw_c, lnb_c = sb("lnw_c", [P, 1]), sb("lnb_c", [P, 1])
        wbc = sb("wbc", [P, 2, U])
        wgr = sb("wgr", [U, 2, 9])
        gmask = sb("gmask", [U, U])
        wexp = sb("wexp", [U, 9, U])
        wtap2 = sb("wtap2", [P, 3, U])
        wtap1 = sb("wtap1", [U, 3, U])
        wot = sb("wot", [P, C])
        A_c = sb("A_c", [U, 1])
        wqk_s, wv_s = sb("wqk_s", [P, 2 * U]), sb("wv_s", [P, C])
        bqk_c, bqks_c = sb("bqk_c", [P, 1]), sb("bqks_c", [P, 1])
        qkscale = sb("qkscale", [P, 1])
        bv_r, gamma_r, beta_r = sb("bv_r", [P, C]), sb("gamma_r", [P, C]), sb("beta_r", [P, C])
        gw_s, gb_r = sb("gw_s", [P, E]), sb("gb_r", [P, E])
        kscale = sb("kscale", [KA, 1])
        rank = sb("rank", [P, NT, E])
        eoff = sb("eoff", [P, NT, E])
        iota_i = sb("iota_i", [P, NT, E], I32)
        tokid = sb("tokid", [P, NT])
        tokid_i = sb("tokid_i", [P, NT], I32)
        fill = sb("fill", [P, FILL_ROWS, ROW])

        xs = [sb(f"xs{k}", [P, N]) for k in range(2)]
        xT = sb("xT", [P, NT, C])
        bn = sb("bn", [P, NT, 6])
        mv = sb("mv", [P, NT, 2])
        var, negm, rstd, shift = (sb(f"{n}_x", [P, NT]) for n in ("var", "negm", "rstd", "shift"))
        mvt = sb("mvt", [P, NT, 2])
        vart, negmt, rstdt, shiftt = (sb(f"{n}_t", [P, NT]) for n in ("var", "negm", "rstd", "shift"))
        xn = sb("xn", [P, NT, C])
        xnT = sb("xnT", [P, N])
        img = sb("img", [P, HP, WP])
        cd = sb("cd", [U, N])
        dts = sb("dts", [U, 4])
        dtr, dtr0 = sb("dtr", [U, 1]), sb("dtr0", [S, 1])
        cdT = sb("cdT", [P, NT, U])
        abT = sb("abT", [P, NT, S])
        hs = sb("hs", [P, S])
        gs = sb("gs", [S, C])
        t1 = [sb(f"t1_{k}", [P, NT, C]) for k in range(2)]
        u1 = [sb(f"u1_{k}", [P, NT, C]) for k in range(2)]
        u1T = sb("u1T", [P, N])
        absu = sb("absu", [P, N], BF16)
        qhi = [sb(f"qhi{k}", [KA, N], F32R) for k in range(2)]
        khi = [sb(f"khi{k}", [KA, N], F32R) for k in range(2)]
        qhl = [sb(f"qhl{k}", [P, N], F32R) for k in range(2)]
        klh = [sb(f"klh{k}", [P, N], F32R) for k in range(2)]
        vz = sb("vz", [P, NT, C])
        qkz = sb("qkz", [P, N])
        qk = sb("qk", [P, N])
        qkh = sb("qkh", [P, N])
        va = [sb(f"va{k}", [P, NT, VA]) for k in range(2)]
        mxs = sb("mxs", [P, NT, 2])
        nmx = sb("nmx", [P, NT, 2])
        pT = [sb(f"pT{k}", [P, NT, HALF]) for k in range(2)]
        prv = sb("prv", [P, NT])
        o = [sb(f"o{k}", [P, NT, C]) for k in range(2)]
        bn3 = sb("bn3", [P, NT, 6])
        mv3 = sb("mv3", [P, NT, 2])
        var3, negm3, rstd3, shift3 = (sb(f"{n}_3", [P, NT]) for n in ("var", "negm", "rstd", "shift"))
        neghalf = sb("neghalf", [P, NT])
        rows = [sb(f"rows{k}", [P, NT, ROW]) for k in range(2)]
        u2 = sb("u2", [P, NT, C])
        u2T = sb("u2T", [P, N])
        lg = sb("lg", [P, NT, E])
        eg = sb("eg", [P, NT, E])
        r8 = sb("r8", [P, 6, NT])
        oh = sb("oh", [P, NT, E])
        oh_bf = sb("oh_bf", [P, NT, E], BF16)
        ra = sb("ra", [P, NT, E])
        rb = sb("rb", [P, NT, E])
        rc = sb("rc", [P, NT, E])
        rd = sb("rd", [P, NT, E])
        run = sb("run", [P, 1, E])
        slot_i = [sb(f"slot_i{k}", [P, NT], I32) for k in range(2)]

        work = ctx.enter_context(nc.psum_tensor("work", [P, 2, HALF], F32))
        mxp = [ctx.enter_context(nc.psum_tensor(f"mxp{k}", [P, HALF], F32)) for k in range(2)]
        stp = [ctx.enter_context(nc.psum_tensor(f"stp{k}", [P, HALF], F32)) for k in range(2)]
        pvp = [ctx.enter_context(nc.psum_tensor(f"pvp{k}", [P, HALF], F32)) for k in range(2)]
        workf = work[:].rearrange("p a b -> p (a b)")
        workt = work[:].rearrange("p a (t c) -> p (a t) c", c=C)

        GATE, PLACE = 256, 384

        names = """w_loaded const_pool const_act fill_ready fill_done mask_ready wexp_ready
        taps_psum taps_ready
        x_turned xT_ready x_stats x_rstd xn_ready xn_turned xnT_ready bcdt_done img_ready conv_done
        dt_small cd_exp dt_sumr cd_turned cdT_ready abT_ready h_done h_ready g_done g_ready y_done t1_ready
        t1b_ready t_stats t_rstd u1_ready u1_turned u1T_ready absu_ready qk_done qkz_ready qk_ready qkh_ready
        qhi_ready khi_ready parts_high parts_low mask_done kmask_ready v_done vz_ready va_ready
        mx_done mx_read negmax_ready mrow_done mrow_ready st_done exp_ready pv_done pv_rinv o_ready
        o_stats o_rstd on_ready ong_ready t2_ready t2_stats t2_rstd u2_ready u2_turned u2T_ready
        gate_done lg_ready eg_ready gate_chain ohb_ready pos_done slot_ready rowid_ready rowprob_ready""".split()
        s = {n: sem(n) for n in names}
        passed = {n: sem(f"passed_{n}") for n in ("sp", "pool", "dve", "pe")}
        x_loaded, scattered, tokens_stored = ([sem(f"{n}{k}") for k in range(2)]
                                              for n in ("x_loaded", "scattered", "tokens_stored"))

        def bc_last(ap2, n):
            return ap2.unsqueeze(2).to_broadcast([ap2.shape[0], ap2.shape[1], n])

        def bc_mid(ap2, n):
            return ap2.unsqueeze(1).to_broadcast([ap2.shape[0], n, ap2.shape[1]])

        steps = [("st", 0, 0), ("st", 0, 1), "x_turn", ("mx", 1, 0), ("u1n", 3), ("st", 0, 2), ("mx", 1, 1),
                 ("st", 0, 3), ("xs", 0), "u1_turn", ("st", 0, 4), ("mx", 1, 2), "pos", "absu", ("st", 0, 5), "qk",
                 ("mx", 1, 3), ("st", 0, 6), ("mx", 1, 4), ("xs", 1), ("st", 0, 7), "mask", "v", ("xn", 0), ("xn", 1),
                 ("pv", 0, 0), ("xn", 2), ("xn", 3), ("mx", 1, 5), ("pv", 0, 1), ("mx", 1, 6), "qk_lrelu", ("mx", 1, 7),
                 ("negmax", 1), "xn_turn", ("pv", 0, 2), ("mrow", 1), "bcdt", "qk_high", "scatter", "t1b", ("st", 1, 0),
                 ("pv", 0, 3), ("st", 1, 1), ("ln2s", 0), ("ln2s", 1), "qk_low", ("conv", 0), ("ln2n", 0), ("ln2n", 1),
                 ("ln2n", 2), ("ln2n", 3), "ln2g", ("ln3s", 0), ("conv", 1), "dt", ("mx", 0, 0), ("st", 1, 2),
                 ("mx", 0, 1), ("st", 1, 3), "dt_exp", ("ln3s", 1), ("st", 1, 4), ("st", 1, 5), "asm", "cd_turn",
                 ("mx", 0, 2), ("st", 1, 6), ("mx", 0, 3), ("st", 1, 7), ("ln3n", 0), "h", ("mx", 0, 4), ("ln3n", 1),
                 "g", ("mx", 0, 5), "y", ("mx", 0, 6), ("ts", 0), ("pv", 1, 0), ("mx", 0, 7), ("ts", 1), ("negmax", 0),
                 ("ln3n", 2), ("ln3n", 3), ("pv", 1, 1), ("u1n", 0), "u2_turn", ("u1n", 1), ("pv", 1, 2), ("mrow", 0),
                 ("u1n", 2), ("pv", 1, 3), "gate"]
        ROUTE = ("ln2s", "ln2n", "ln2g", "ln3s", "ln3n", "u2_turn", "gate")
        LATE = ("pos", "scatter")
        PROJ = (("u1n", 3), "u1_turn", "absu", "qk", "mask", "qk_lrelu", "qk_high", "qk_low", "v",
                ("mx", 0), ("negmax", 0), ("mrow", 0))
        ATT = ("t1b", "st", "pv", ("mx", 1), ("negmax", 1), ("mrow", 1))

        def batch(i, c):
            return i * 2 + c, i + c // 2, c % 2

        def one_pass(one, i, c, attend=True, last=False):
            for st in steps:
                names = (st, st[0], st[:2]) if isinstance(st, tuple) else (st,)
                if any(n in ATT for n in names):
                    if attend:
                        one(st, *batch(i, c))
                elif any(n in ROUTE for n in names):
                    if attend and c != 0:
                        one(st, *batch(i, c - 1))
                elif any(n in LATE for n in names):
                    if attend and not early(i * 2 + c, 2):
                        one(st, *batch(i, c - 2))
                elif any(n in PROJ for n in names):
                    if c != -2 and not (last and c == B - 1):
                        one(st, *batch(i, c + 1))
                elif not last:
                    one(st, *batch(i, c + 2))

        def passes(eng, one):
            one_pass(one, 0, -2, attend=False)
            one_pass(one, 0, -1, attend=False)
            one_pass(one, 0, 0)
            one_pass(one, 0, 1)
            one_pass(one, 0, 2)
            with eng.Fori(1, (B - 4) // 2) as i:
                one_pass(one, i, 1)
                one_pass(one, i, 2)
            one_pass(one, 0, B - 3)
            one_pass(one, 0, B - 2, last=True)
            one_pass(one, 0, B - 1, last=True)
            for st in steps:
                if st in LATE:
                    one(st, *batch(0, B - 2))
                elif (st[0] if isinstance(st, tuple) else st) in ROUTE:
                    one(st, *batch(0, B - 1))
            for st in LATE:
                one(st, *batch(0, B - 1))

        block = ctx.enter_context(nc.Block())

        @block.sync
        def _(sp):
            def w(dst, src):
                sp.dma_start(dst, src).then_inc(s["w_loaded"], 16)

            def load_x(b, k):
                sp.dma_start(xs[k][:], x[bass.ds(b, 1)].rearrange("o c n -> (o c) n")).then_inc(x_loaded[k], 16)

            load_x(0, 0)
            w(wbc[:, 0, :], w_bcdt_t)
            w(wbc[:, 1, :], w_bcdt_t)
            w(wgr[:], w_gw)
            w(wot[:], w_out_t)
            w(lnw_c[:], ln_w)
            w(lnb_c[:], ln_b)
            w(A_c[S:U, :], A.unsqueeze(1))
            w(wqk_s[:, 0:U], Wq)
            w(wqk_s[:, U:P], Wk)
            w(wv_s[:], Wv)
            w(bqk_c[0:U, :], bq.unsqueeze(1))
            w(bqk_c[U:P, :], bk.unsqueeze(1))
            w(bv_r[:], bv.partition_broadcast(P))
            w(gamma_r[:], gamma.partition_broadcast(P))
            w(beta_r[:], beta.partition_broadcast(P))
            w(gw_s[:], gate_w)
            w(gb_r[:], gate_b.partition_broadcast(P))
            load_x(1, 1)
            sp.wait_ge(s["fill_ready"], 1)
            for f in range(NFILL):
                sp.dma_start(slots[f * P * FILL_ROWS:(f + 1) * P * FILL_ROWS].rearrange("(p r) d -> p (r d)", p=P),
                             fill[:].rearrange("p r d -> p (r d)")).then_inc(s["fill_done"], 16)

            def one(st, b, m, k):
                if st == "x_turn" and not early(b, 1) and not (isinstance(b, int) and b == B - 1):
                    wait_apart(sp, s["x_turned"], b, passed["sp"])
                    load_x(b + 1, 1 - k)
                if st == ("ln3s", 0):
                    wait_apart(sp, s["t2_ready"], b + 1, passed["sp"])
                    sp.dma_start(tokens[bass.ds(b * N, N)].rearrange("(t p) c -> p t c", p=P),
                                 rows[k][:, :, 0:C]).then_inc(tokens_stored[k], 16)

            passes(sp, one)
            for k in range(2):
                sp.wait_ge(scattered[k], (B // 2) * NT * 16)
                sp.wait_ge(tokens_stored[k], (B // 2) * 16)

        @block.gpsimd
        def _(pool):
            g = nc.gpsimd
            cp = [0]

            def chain(ins):
                cp[0] += 1
                ins.then_inc(s["const_pool"], 1)
                pool.wait_ge(s["const_pool"], cp[0])

            chain(g.memset(fill[:], 0.0))
            g.memset(fill[:, :, TOKEN:TOKEN + 1].bitcast(I32), NO_TOKEN).then_inc(s["fill_ready"], 1)
            chain(g.memset(ident[:], 0.0))
            chain(g.affine_select(out=ident[:], in_=ident[:], pattern=[[-1, P]], compare_op=ALU.not_equal, fill=1.0,
                                  base=0, channel_multiplier=1))
            chain(g.memset(ones_bf[:], 1.0))
            chain(g.affine_select(out=before_bf[:], in_=ones_bf[:], pattern=[[1, P]], compare_op=ALU.is_gt, fill=0.0,
                                  base=0, channel_multiplier=-1))
            chain(g.memset(onecol_bf[:, 0:1], 1.0))
            chain(g.memset(onecol_bf[:, 1:2], 0.0))
            gm = gmask[:].rearrange("o (g i) -> o g i", i=2)
            chain(g.memset(gmask[:], 1.0))
            chain(g.affine_select(out=gm, in_=gm, pattern=[[-2, S], [0, 2]], compare_op=ALU.is_ge, fill=0.0,
                                  base=0, channel_multiplier=1))
            chain(g.affine_select(out=gm, in_=gm, pattern=[[2, S], [0, 2]], compare_op=ALU.is_ge, fill=0.0,
                                  base=1, channel_multiplier=-1))
            chain(g.iota(iota_i[:], pattern=[[0, NT], [1, E]], base=0, channel_multiplier=0))
            chain(g.tensor_scalar(rank[:], iota_i[:], -1.0, float(E), ALU.mult, ALU.add))
            chain(g.tensor_scalar(eoff[:], iota_i[:], float(CAP), 0.0, ALU.mult, ALU.add))
            chain(g.iota(tokid_i[:], pattern=[[P, NT]], base=0, channel_multiplier=1))
            chain(g.tensor_copy(tokid[:], tokid_i[:]))
            chain(g.memset(run[:], 0.0))
            chain(g.memset(neghalf[:], -0.5))
            chain(g.memset(kscale[U:KA, :], 1.0))
            chain(g.memset(nmx[:], 1.0))
            chain(g.memset(qkscale[0:U, :], 0.125))
            chain(g.memset(qkscale[U:P, :], 1.0))
            chain(g.memset(img[:], 0.0))
            for k in range(2):
                chain(g.memset(qhi[k][U:KA, :].bitcast(F32), 1.0))
                chain(g.memset(va[k][:, :, C:VA], 1.0))
            g.memset(kscale[U:U + 1, :], NEG_FILL).then_inc(s["mask_ready"], 1)

            def rsqrt(var, negm, rstd, shift, j, have, done, b):
                own = slice(4 * j, 4 * j + 4)
                wait_apart(pool, have, b * 8 + (4 * j + 4), passed["pool"])
                g.tensor_tensor(rstd[:, own], var[:, own], neghalf[:, own], ALU.pow).then_inc(done, 1)
                wait_apart(pool, done, b * 4 + (2 * j + 1), passed["pool"])
                g.tensor_tensor(shift[:, own], negm[:, own], rstd[:, own], ALU.mult).then_inc(done, 1)

            def one(st, b, m, k):
                first = early(b, 1)
                what, j = (st[0], st[1]) if isinstance(st, tuple) else (st, 0)
                if what == "xs":
                    rsqrt(var, negm, rstd, shift, j, s["x_stats"], s["x_rstd"], b)
                if what == "ts":
                    rsqrt(vart, negmt, rstdt, shiftt, j, s["t_stats"], s["t_rstd"], b)
                if what == "ln2s":
                    if j == 0 and not first:
                        wait_apart(pool, s["rowid_ready"], b * 3, passed["pool"])
                    rsqrt(var3, negm3, rstd3, shift3, j, s["o_stats"], s["o_rstd"], b)
                if what == "ln3s":
                    rsqrt(var3, negm3, rstd3, shift3, j, s["t2_stats"], s["t2_rstd"], b)
                if st == "t1b":
                    if not early(b, 2):
                        wait_apart(pool, scattered[k], m * (NT * 16), passed["pool"])
                        wait_apart(pool, tokens_stored[k], m * 16, passed["pool"])
                    wait_apart(pool, s["t1_ready"], b + 1, passed["pool"])
                    g.tensor_tensor(rows[k][:, :, 0:C], t1[k][:], bc_mid(beta_r[:], NT), ALU.add)\
                        .then_inc(s["t1b_ready"], 1)
                if st == ("ln3s", 1):
                    g.tensor_copy(rows[k][:, :, TOKEN:TOKEN + 1].bitcast(I32), tokid[:].unsqueeze(2))\
                        .then_inc(s["rowid_ready"], 1)
                    wait_apart(pool, s["rowid_ready"], b * 3 + 1, passed["pool"])
                    g.tensor_scalar(tokid[:], tokid[:], float(N), 0.0, ALU.add, ALU.add).then_inc(s["rowid_ready"], 1)
                    wait_apart(pool, s["t2_rstd"], b * 4 + 4, passed["pool"])
                    g.tensor_copy(rows[k][:, :, RSTD], rstd3[:])
                    g.tensor_copy(rows[k][:, :, SHIFT], shift3[:]).then_inc(s["rowid_ready"], 1)
                if st == "scatter":
                    wait_apart(pool, s["slot_ready"], b + 1, passed["pool"])
                    wait_apart(pool, s["rowprob_ready"], b + 1, passed["pool"])
                    wait_apart(pool, s["rowid_ready"], b * 3 + 3, passed["pool"])
                    if first:
                        pool.wait_ge(s["fill_done"], 16 * NFILL)
                    for t in range(NT):
                        g.indirect_dma_start(out=slots, out_offset=bass.IndirectOffsetOnAxis(ap=slot_i[k][:, t:t + 1], axis=0),
                                             in_=rows[k][:, t, :], in_offset=None, bounds_check=E * CAP - 1,
                                             oob_is_err=False).then_inc(scattered[k], 16)

            passes(pool, one)

        @block.scalar
        def _(act):
            a = nc.scalar
            act.wait_ge(s["w_loaded"], 16 * NW)
            act.wait_ge(s["mask_ready"], 1)
            a.activation(bqks_c[:], bqk_c[:], ACT.Identity, scale=qkscale[:]).then_inc(s["const_act"], 1)
            act.wait_ge(s["const_act"], 1)

            def normalise(dst, src, rstd_, shift_, j, have, b, done):
                if j % 2 == 0:
                    act.wait_ge(have, b * 4 + (j + 2))
                for t in range(2 * j, 2 * j + 2):
                    last = a.activation(dst[:, t, :], src[:, t, 0:C], ACT.Identity, bias=shift_[:, t:t + 1],
                                        scale=rstd_[:, t:t + 1])
                if j == 3:
                    last.then_inc(done, 1)

            def one(st, b, m, k):
                first = early(b, 1)
                what, j = (st[0], st[1]) if isinstance(st, tuple) else (st, 0)
                if st == "x_turn":
                    act.wait_ge(s["x_turned"], b + 1)
                    if not first:
                        act.wait_ge(s["t1_ready"], b)
                    a.copy(xT[:].rearrange("p t c -> p (t c)"), workf).then_inc(s["xT_ready"], 1)
                if what == "xn":
                    if j == 0:
                        act.wait_ge(s["xT_ready"], b + 1)
                    normalise(xn, xT, rstd, shift, j, s["x_rstd"], b, s["xn_ready"])
                if what == "u1n":
                    if not early(b, 2):
                        act.wait_ge(s["o_ready"], b * 8 + (2 * j - 14))
                    normalise(u1[k], t1[k], rstdt, shiftt, j, s["t_rstd"], b, s["u1_ready"])
                if what == "ln2n":
                    normalise(o[k], o[k], rstd3, shift3, j, s["o_rstd"], b, s["on_ready"])
                if what == "ln3n":
                    normalise(u2, rows[k], rstd3, shift3, j, s["t2_rstd"], b, s["u2_ready"])
                if st == "xn_turn":
                    act.wait_ge(s["xn_turned"], b + 1)
                    if not first:
                        act.wait_ge(s["bcdt_done"], b)
                    a.activation(xnT[:], workf, ACT.Identity, bias=lnb_c[:], scale=lnw_c[:]).then_inc(s["xnT_ready"], 1)
                if st == "bcdt":
                    act.wait_ge(s["bcdt_done"], b + 1)
                    if not first:
                        act.wait_ge(s["conv_done"], b * 2)
                    a.copy(img[0:U, 1:H + 1, 1:W + 1], workf[0:U, :].rearrange("p (h w) -> p h w", w=W))
                    a.copy(img[U:P, 1:H + 1, 0:W],
                           workf[U:P, :].rearrange("p (h w) -> p h w", w=W)).then_inc(s["img_ready"], 1)
                if st == "dt":
                    act.wait_ge(s["conv_done"], b * 2 + 2)
                    if not first:
                        act.wait_ge(s["y_done"], b)
                    a.copy(cd[0:S, :], workf[0:S, :])
                if st == "dt_exp":
                    act.wait_ge(s["dt_small"], b * 3 + 3)
                    a.activation(cd[S:U, :], workf[S:U, :], ACT.Exp, bias=dts[S:U, 2:3],
                                 accum_out=dts[S:U, 3:4]).then_inc(s["cd_exp"], 1)
                if st == "cd_turn":
                    act.wait_ge(s["cd_turned"], b + 1)
                    if not first:
                        act.wait_ge(s["abT_ready"], b)
                    a.copy(cdT[:].rearrange("p t c -> p (t c)"), work[:, 0, :]).then_inc(s["cdT_ready"], 1)
                if st == "u1_turn":
                    act.wait_ge(s["u1_turned"], b + 1)
                    if not first:
                        act.wait_ge(s["v_done"], b)
                    a.copy(u1T[:], workf).then_inc(s["u1T_ready"], 1)
                if st == "absu":
                    act.wait_ge(s["u1T_ready"], b + 1)
                    if not first:
                        act.wait_ge(s["mask_done"], b)
                    a.activation(absu[:], u1T[:], ACT.Abs).then_inc(s["absu_ready"], 1)
                if st == "qk":
                    act.wait_ge(s["qk_done"], b + 1)
                    if not first:
                        act.wait_ge(s["qk_ready"], b)
                    a.activation(qkz[:], workf, ACT.Identity, bias=bqks_c[:], scale=qkscale[:]).then_inc(s["qkz_ready"], 1)
                if st == "qk_high":
                    act.wait_ge(s["qkh_ready"], b + 1)
                    a.copy(qhi[k][0:U, :], qkh[0:U, :]).then_inc(s["qhi_ready"], 1)
                    a.copy(khi[k][0:U, :], qkh[U:P, :]).then_inc(s["khi_ready"], 1)
                if what == "mrow":
                    act.wait_ge(s["mrow_done"], b * 2 + (j + 1))
                    a.copy(qhi[k][U:KA, j * HALF:(j + 1) * HALF], stp[1][U:KA, :]).then_inc(s["mrow_ready"], 1)
                if what == "st":
                    kt = st[2]
                    act.wait_ge(s["st_done"], b * 16 + (j * 8 + kt + 1))
                    if kt == 0 and not first:
                        act.wait_ge(s["pv_done"], b * 8 + (4 * j - 4))
                    a.activation(pT[j][:, kt, :], stp[kt % 2][:], ACT.Exp).then_inc(s["exp_ready"], 1)
                if st == "u2_turn":
                    act.wait_ge(s["u2_turned"], b + 1)
                    if not first:
                        act.wait_ge(s["gate_done"], b)
                    a.copy(u2T[:], workf).then_inc(s["u2T_ready"], 1)
                if st == "gate":
                    act.wait_ge(s["gate_chain"], b * 13 + 2)
                    a.activation(eg[:], lg[:], ACT.Exp).then_inc(s["eg_ready"], 1)

            passes(act, one)

        @block.vector
        def _(dve):
            v = nc.vector
            dve.wait_ge(s["w_loaded"], 16 * NW)
            dve.wait_ge(s["mask_ready"], 1)
            for ii in range(2):
                for tap in range(9):
                    wi = wexp[:, tap, :].rearrange("o (g i) -> o g i", i=2)[:, :, ii]
                    mi = gmask[:].rearrange("o (g i) -> o g i", i=2)[:, :, ii]
                    last = v.tensor_tensor(wi, mi, wgr[:, ii, tap:tap + 1].to_broadcast([U, S]), ALU.mult)
            last.then_inc(s["wexp_ready"], 1)
            dve.wait_ge(s["taps_psum"], 1)
            for kh in range(3):
                v.tensor_copy(wtap2[:, kh, :], work[:, 0, kh * U:(kh + 1) * U])
                last = v.tensor_copy(wtap1[:, kh, :], work[0:U, 1, kh * U:(kh + 1) * U])
            last.then_inc(s["taps_ready"], 1)

            def stats(src, bn_, mv_, var, negm, j, got, b, eps, scale=1.0):
                own = slice(4 * j, 4 * j + 4)
                for t in range(4 * j, 4 * j + 4):
                    last = v.bn_stats(bn_[:, t, :], src[:, t, :])
                last.then_inc(got, 1)
                wait_apart(dve, got, b * 8 + (4 * j + 1), passed["dve"])
                for t in range(4 * j, 4 * j + 4):
                    last = v.bn_aggr(mv_[:, t, :], bn_[:, t, :])
                last.then_inc(got, 1)
                wait_apart(dve, got, b * 8 + (4 * j + 2), passed["dve"])
                v.tensor_scalar(var[:, own], mv_[:, own, 1], scale, eps, ALU.mult, ALU.add).then_inc(got, 1)
                v.tensor_scalar(negm[:, own], mv_[:, own, 0], -1.0, None, ALU.mult).then_inc(got, 1)

            def lrelu(dst, zs):
                return v.scalar_tensor_tensor(out=dst, in0=zs, scalar=0.2, in1=zs, op0=ALU.mult, op1=ALU.max)

            def mx_read(b, c, n):
                qt = 4 * c + n // 2
                dve.wait_ge(s["mx_done"], b * 16 + (c * 8 + n + 1))
                v.reduce_max(mxs[:, qt, n % 2:n % 2 + 1], mxp[n % 2][:], AX).then_inc(s["mx_read"], 1)

            def negmax(b, c):
                dve.wait_ge(s["mx_read"], b * 16 + (c * 8 + 8))
                v.tensor_reduce(nmx[:, 4 * c:4 * c + 4, 1], mxs[:, 4 * c:4 * c + 4, :], AX, ALU.max,
                                negate=True).then_inc(s["negmax_ready"], 1)

            def one(st, b, m, k):
                first = early(b, 1)
                what, j = (st[0], st[1]) if isinstance(st, tuple) else (st, 0)
                if what == "xs":
                    dve.wait_ge(s["xT_ready"], b + 1)
                    stats(xT, bn, mv, var, negm, j, s["x_stats"], b, 1e-5, C / (C - 1.0))
                if st == "dt":
                    dve.wait_ge(s["conv_done"], b * 2 + 2)
                    if not first:
                        dve.wait_ge(s["cd_exp"], b)
                    v.reduce_max(dts[S:U, 0:1], workf[S:U, :], AX).then_inc(s["dt_small"], 1)
                    dve.wait_ge(s["dt_small"], b * 3 + 1)
                    v.tensor_tensor(dts[S:U, 1:2], dts[S:U, 0:1], A_c[S:U, :], ALU.add).then_inc(s["dt_small"], 1)
                    dve.wait_ge(s["dt_small"], b * 3 + 2)
                    v.tensor_tensor(dts[S:U, 2:3], A_c[S:U, :], dts[S:U, 1:2], ALU.subtract).then_inc(s["dt_small"], 1)
                if st == "asm":
                    dve.wait_ge(s["cd_exp"], b + 1)
                    v.reciprocal(dtr[S:U, :], dts[S:U, 3:4]).then_inc(s["dt_sumr"], 1)
                    dve.wait_ge(s["dt_sumr"], b * 2 + 1)
                    v.tensor_copy(dtr0[:], dtr[S:U, :]).then_inc(s["dt_sumr"], 1)
                if st == "cd_turn":
                    dve.wait_ge(s["cdT_ready"], b + 1)
                    if not first:
                        dve.wait_ge(s["h_done"], b)
                    v.tensor_tensor(abT[:], cdT[:, :, 0:S], cdT[:, :, S:U], ALU.mult).then_inc(s["abT_ready"], 1)
                if st == "h":
                    dve.wait_ge(s["h_done"], b + 1)
                    v.tensor_copy(hs[:], work[:, 1, 0:S]).then_inc(s["h_ready"], 1)
                if st == "g":
                    dve.wait_ge(s["g_done"], b + 1)
                    dve.wait_ge(s["dt_sumr"], b * 2 + 2)
                    v.tensor_scalar(gs[:], work[0:S, 0, 0:C], dtr0[:], None, ALU.mult).then_inc(s["g_ready"], 1)
                if st == "y":
                    dve.wait_ge(s["y_done"], b + 1)
                    if not early(b, 2):
                        dve.wait_ge(s["t1b_ready"], b - 1)
                    v.tensor_tensor(t1[k][:], workt, xT[:], ALU.add).then_inc(s["t1_ready"], 1)
                if what == "ts":
                    dve.wait_ge(s["t1_ready"], b + 1)
                    stats(t1[k], bn, mvt, vart, negmt, j, s["t_stats"], b, 1e-5)
                if st == "qk_lrelu":
                    dve.wait_ge(s["qkz_ready"], b + 1)
                    if not first:
                        dve.wait_ge(s["parts_low"], b * 2)
                    lrelu(qk[:], qkz[:]).then_inc(s["qk_ready"], 1)
                if st == "mask":
                    dve.wait_ge(s["mask_done"], b + 1)
                    for h in range(2):
                        last = v.tensor_scalar(khi[k][U:KA, h * HALF:(h + 1) * HALF], mxp[h][U:KA, :], 0.0,
                                               kscale[U:KA, :], ALU.is_equal, ALU.mult)
                    last.then_inc(s["kmask_ready"], 1)
                if st == "qk_high":
                    dve.wait_ge(s["qk_ready"], b + 1)
                    if not first:
                        dve.wait_ge(s["khi_ready"], b)
                    v.tensor_scalar(qkh[:].bitcast(I32), qk[:].bitcast(I32), HIGH_BITS, None, ALU.bitwise_and)\
                        .then_inc(s["qkh_ready"], 1)
                if st == "qk_low":
                    dve.wait_ge(s["qkh_ready"], b + 1)
                    v.tensor_copy(qhl[k][0:U, :], qkh[0:U, :])
                    v.tensor_copy(klh[k][U:P, :], qkh[U:P, :]).then_inc(s["parts_high"], 1)
                    v.tensor_tensor(qhl[k][U:P, :], qk[0:U, :], qkh[0:U, :], ALU.subtract).then_inc(s["parts_low"], 1)
                    v.tensor_tensor(klh[k][0:U, :], qk[U:P, :], qkh[U:P, :], ALU.subtract).then_inc(s["parts_low"], 1)
                if st == "v":
                    dve.wait_ge(s["v_done"], b + 1)
                    v.tensor_tensor(vz[:], workt, bc_mid(bv_r[:], NT), ALU.add).then_inc(s["vz_ready"], 1)
                    dve.wait_ge(s["vz_ready"], b + 1)
                    lrelu(va[k][:, :, 0:C], vz[:]).then_inc(s["va_ready"], 1)
                if what == "mx":
                    mx_read(b, j, st[2])
                if what == "pv":
                    n = st[2]
                    qt = 4 * j + n
                    dve.wait_ge(s["pv_done"], b * 8 + (qt + 1))
                    v.reciprocal(prv[:, qt:qt + 1], pvp[qt % 2][:, C:VA]).then_inc(s["pv_rinv"], 1)
                    dve.wait_ge(s["pv_rinv"], b * 8 + (qt + 1))
                    v.scalar_tensor_tensor(out=o[k][:, qt, :], in0=pvp[qt % 2][:, 0:C], scalar=prv[:, qt:qt + 1],
                                           in1=u1[k][:, qt, :], op0=ALU.mult, op1=ALU.add).then_inc(s["o_ready"], 1)
                if what == "ln2s":
                    if j == 0:
                        dve.wait_ge(s["o_ready"], b * 8 + 8)
                    stats(o[k], bn3, mv3, var3, negm3, j, s["o_stats"], b, 1e-8)
                if st == "ln2g":
                    dve.wait_ge(s["on_ready"], b + 1)
                    v.tensor_tensor(o[k][:], o[k][:], bc_mid(gamma_r[:], NT), ALU.mult).then_inc(s["ong_ready"], 1)
                    dve.wait_ge(s["ong_ready"], b + 1)
                    dve.wait_ge(s["t1b_ready"], b + 1)
                    v.tensor_tensor(rows[k][:, :, 0:C], rows[k][:, :, 0:C], o[k][:], ALU.add).then_inc(s["t2_ready"], 1)
                if what == "ln3s":
                    dve.wait_ge(s["t2_ready"], b + 1)
                    stats(rows[k][:, :, 0:C], bn3, mv3, var3, negm3, j, s["t2_stats"], b, 1e-5)
                if what == "negmax":
                    negmax(b, j)
                if st == "gate":
                    gc = s["gate_chain"]
                    cnt = [0]

                    def link(ins):
                        cnt[0] += 1
                        ins.then_inc(gc, 1)
                        dve.wait_ge(gc, b * 13 + cnt[0])
                    dve.wait_ge(s["gate_done"], b + 1)
                    lgw = pvp[0][:, GATE:GATE + NT * E].rearrange("p (t e) -> p t e", e=E)
                    link(v.tensor_tensor(ra[:], lgw, bc_mid(gb_r[:], NT), ALU.add))
                    v.reduce_max(r8[:, 0, :], ra[:], AX).then_inc(s["lg_ready"], 1)
                    dve.wait_ge(s["lg_ready"], b + 1)
                    link(v.tensor_tensor(lg[:], ra[:], bc_last(r8[:, 0, :], E), ALU.subtract))
                    dve.wait_ge(s["eg_ready"], b + 1)
                    link(v.reduce_sum(r8[:, 1, :], eg[:], AX))
                    link(v.reduce_max(r8[:, 2, :], eg[:], AX))
                    link(v.reciprocal(r8[:, 3, :], r8[:, 1, :]))
                    v.tensor_tensor(rows[k][:, :, PROB], r8[:, 2, :], r8[:, 3, :], ALU.mult).then_inc(s["rowprob_ready"], 1)
                    link(v.tensor_tensor(ra[:], eg[:], bc_last(r8[:, 2, :], E), ALU.is_equal))
                    link(v.tensor_tensor(rb[:], ra[:], rank[:], ALU.mult))
                    link(v.reduce_max(r8[:, 4, :], rb[:], AX))
                    link(v.tensor_tensor(oh[:], rb[:], bc_last(r8[:, 4, :], E), ALU.is_equal))
                    v.tensor_copy(oh_bf[:], oh[:]).then_inc(s["ohb_ready"], 1)
                if st == "pos":
                    gc = s["gate_chain"]
                    cnt = [9]

                    def link2(ins):
                        cnt[0] += 1
                        ins.then_inc(gc, 1)
                        dve.wait_ge(gc, b * 13 + cnt[0])
                    dve.wait_ge(s["pos_done"], b + 1)
                    pw = pvp[0][:, PLACE:PLACE + (NT + 1) * E].rearrange("p (t e) -> p t e", e=E)
                    link2(v.tensor_tensor(ra[:], pw[:, 0:NT, :], run[:].to_broadcast([P, NT, E]), ALU.add))
                    v.tensor_tensor(run[:], pw[:, NT:NT + 1, :], run[:], ALU.add)
                    v.tensor_tensor(rb[:], ra[:], oh[:], ALU.mult)
                    link2(v.tensor_tensor(rc[:], ra[:], eoff[:], ALU.add))
                    v.reduce_sum(r8[:, 4, :], rb[:], AX)
                    link2(v.tensor_tensor(rd[:], rc[:], oh[:], ALU.mult))
                    v.tensor_scalar(r8[:, 4, :], r8[:, 4, :], float(CAP), DROP, ALU.is_ge, ALU.mult)
                    link2(v.reduce_sum(r8[:, 5, :], rd[:], AX))
                    v.tensor_tensor(slot_i[k][:], r8[:, 4, :], r8[:, 5, :], ALU.add).then_inc(s["slot_ready"], 1)

            passes(dve, one)

        @block.tensor
        def _(pe):
            mm = nc.tensor.matmul
            pe.wait_ge(s["w_loaded"], 16 * NW)
            pe.wait_ge(s["mask_ready"], 1)
            pe.wait_ge(s["wexp_ready"], 1)
            for kh in range(3):
                nc.tensor.transpose(work[:, 0, kh * U:(kh + 1) * U],
                                    wexp[:, 3 * kh:3 * kh + 2, :].rearrange("o a i -> o (a i)"), ident[0:U, 0:U])
                last = nc.tensor.transpose(work[0:U, 1, kh * U:(kh + 1) * U], wexp[:, 3 * kh + 2, :], ident[0:U, 0:U])
            last.then_inc(s["taps_psum"], 1)
            pe.wait_ge(s["taps_ready"], 1)

            def turn(src, done):
                for t in range(NT):
                    last = nc.tensor.transpose(workt[:, t, :], src(t), ident[:])
                last.then_inc(done, 1)

            def mx(b, k, c, n):
                qt = 4 * c + n // 2
                if not (isinstance(b, int) and b == 0 and c == 0 and n < 2):
                    pe.wait_ge(s["mx_read"], b * 16 + (c * 8 + n - 1))
                if c == 1 and n == 5 and not (isinstance(b, int) and b == B - 1):
                    pe.wait_ge(s["kmask_ready"], b + 2)
                mm(mxp[n % 2][:], qhi[k][0:U + 1, qt * P:(qt + 1) * P], khi[k][0:U + 1, (n % 2) * HALF:(n % 2 + 1) * HALF],
                   start=True, stop=True).then_inc(s["mx_done"], 1)

            def one(st, b, m, k):
                first = early(b, 1)
                if st == "x_turn":
                    pe.wait_ge(x_loaded[k], m * 16 + 16)
                    if not first:
                        pe.wait_ge(s["t1_ready"], b)
                    if not early(b, 4):
                        pe.wait_ge(s["u2T_ready"], b - 3)
                    turn(lambda t: xs[k][:, t * P:(t + 1) * P], s["x_turned"])
                if st == "xn_turn":
                    pe.wait_ge(s["xn_ready"], b + 1)
                    if not first:
                        pe.wait_ge(s["vz_ready"], b)
                    turn(lambda t: xn[:, t, :], s["xn_turned"])
                if st == "bcdt":
                    pe.wait_ge(s["xnT_ready"], b + 1)
                    for h in range(2):
                        last = mm(work[:, h, :], wbc[:].rearrange("p a u -> p (a u)"), xnT[:, h * HALF:(h + 1) * HALF],
                                  start=True, stop=True)
                    last.then_inc(s["bcdt_done"], 1)
                if isinstance(st, tuple) and st[0] == "conv":
                    h = st[1]
                    pe.wait_ge(s["img_ready"], b + 1)
                    r0 = h * (H // 2)
                    for kh in range(3):
                        mm(work[0:U, h, :], wtap2[:, kh, :], img[:, r0 + kh:r0 + kh + H // 2, 0:W],
                           start=(kh == 0), stop=False)
                        last = mm(work[0:U, h, :], wtap1[:, kh, :], img[0:U, r0 + kh:r0 + kh + H // 2, 2:2 + W],
                                  start=False, stop=(kh == 2))
                    last.then_inc(s["conv_done"], 1)
                if st == "cd_turn":
                    wait_apart(pe, s["cd_exp"], b + 1, passed["pe"])
                    for t in range(NT):
                        last = nc.tensor.transpose(work[:, 0, t * U:(t + 1) * U], cd[:, t * P:(t + 1) * P],
                                                   ident[0:U, 0:U])
                    last.then_inc(s["cd_turned"], 1)
                if st == "h":
                    pe.wait_ge(s["abT_ready"], b + 1)
                    for t in range(NT):
                        last = mm(work[:, 1, 0:S], xT[:, t, :], abT[:, t, :], start=(t == 0), stop=(t == NT - 1))
                    last.then_inc(s["h_done"], 1)
                if st == "g":
                    pe.wait_ge(s["h_ready"], b + 1)
                    mm(work[0:S, 0, 0:C], hs[:], wot[:], start=True, stop=True).then_inc(s["g_done"], 1)
                if st == "y":
                    pe.wait_ge(s["g_ready"], b + 1)
                    for t in range(NT):
                        last = mm(workt[:, t, :], cd[0:S, t * P:(t + 1) * P], gs[:], start=True, stop=True)
                    last.then_inc(s["y_done"], 1)
                if st == "u1_turn":
                    pe.wait_ge(s["u1_ready"], b + 1)
                    if not (isinstance(b, int) and b >= B - 1):
                        pe.wait_ge(s["xT_ready"], b + 2)
                    turn(lambda t: u1[k][:, t, :], s["u1_turned"])
                if st == "qk":
                    pe.wait_ge(s["u1T_ready"], b + 1)
                    for h in range(2):
                        last = mm(work[:, h, :], wqk_s[:], u1T[:, h * HALF:(h + 1) * HALF], start=True, stop=True)
                    last.then_inc(s["qk_done"], 1)
                if st == "mask":
                    pe.wait_ge(s["absu_ready"], b + 1)
                    if not first:
                        pe.wait_ge(s["mx_read"], b * 16 - 3)
                    for h in range(2):
                        last = mm(mxp[h][U:KA, :], onecol_bf[:], absu[:, h * HALF:(h + 1) * HALF], start=True, stop=True)
                    last.then_inc(s["mask_done"], 1)
                if st == "v":
                    pe.wait_ge(s["qkz_ready"], b + 1)
                    for t in range(NT):
                        last = mm(workt[:, t, :], u1T[:, t * P:(t + 1) * P], wv_s[:], start=True, stop=True)
                    last.then_inc(s["v_done"], 1)
                if isinstance(st, tuple) and st[0] == "st":
                    c, kt = st[1], st[2]
                    if kt == 0:
                        pe.wait_ge(s["mrow_ready"], b * 2 + (c + 1))
                    if kt == 0 and c == 0:
                        pe.wait_ge(s["parts_high"], b + 1)
                        pe.wait_ge(s["parts_low"], b * 2 + 2)
                    if not (first and c == 0 and kt < 2):
                        pe.wait_ge(s["exp_ready"], b * 16 + (c * 8 + kt - 1))
                    mm(stp[kt % 2][:], klh[k][:, kt * P:(kt + 1) * P], qhl[k][:, c * HALF:(c + 1) * HALF],
                       start=True, stop=False)
                    mm(stp[kt % 2][:], khi[k][:, kt * P:(kt + 1) * P], qhi[k][:, c * HALF:(c + 1) * HALF],
                       start=False, stop=True).then_inc(s["st_done"], 1)
                if isinstance(st, tuple) and st[0] == "mx":
                    if st[1] == 0 and st[2] == 0:
                        pe.wait_ge(s["qhi_ready"], b + 1)
                        pe.wait_ge(s["khi_ready"], b + 1)
                        pe.wait_ge(s["kmask_ready"], b + 1)
                    mx(b, k, st[1], st[2])
                if isinstance(st, tuple) and st[0] == "mrow":
                    c = st[1]
                    pe.wait_ge(s["negmax_ready"], b * 2 + (c + 1))
                    if not (first and c == 0):
                        pe.wait_ge(s["exp_ready"], b * 16 + c * 8)
                    for n in range(4):
                        qt = 4 * c + n
                        last = mm(stp[1][U:KA, n * P:(n + 1) * P], nmx[:, qt, :], ident[:], start=True, stop=True)
                    last.then_inc(s["mrow_done"], 1)
                if isinstance(st, tuple) and st[0] == "pv":
                    c, n = st[1], st[2]
                    qt = 4 * c + n
                    if n == 0:
                        pe.wait_ge(s["exp_ready"], b * 16 + (c * 8 + 8))
                    if n == 0 and c == 0:
                        pe.wait_ge(s["va_ready"], b + 1)
                    if not (first and qt < 2):
                        pe.wait_ge(s["o_ready"], b * 8 + (qt - 1))
                    if qt == 0 and not early(b, 2):
                        pe.wait_ge(s["gate_chain"], b * 13 - 15)
                    for kt in range(NT):
                        last = mm(pvp[qt % 2][:, 0:VA], pT[c][:, kt, n * P:(n + 1) * P], va[k][:, kt, :],
                                  start=(kt == 0), stop=(kt == NT - 1))
                    last.then_inc(s["pv_done"], 1)
                if st == "u2_turn":
                    pe.wait_ge(s["u2_ready"], b + 1)
                    if not (isinstance(b, int) and b >= B - 3):
                        pe.wait_ge(s["t1_ready"], b + 4)
                    turn(lambda t: u2[:, t, :], s["u2_turned"])
                if st == "gate":
                    pe.wait_ge(s["u2T_ready"], b + 1)
                    if not early(b, 1):
                        pe.wait_ge(s["gate_chain"], b * 13 - 2)
                    pe.wait_ge(s["o_ready"], B * 8 if isinstance(b, int) and b == B - 1 else b * 8 + 15)
                    for t in range(NT):
                        last = mm(pvp[0][:, GATE + t * E:GATE + (t + 1) * E], u2T[:, t * P:(t + 1) * P], gw_s[:], start=True, stop=True)
                    last.then_inc(s["gate_done"], 1)
                if st == "pos":
                    pe.wait_ge(s["ohb_ready"], b + 1)
                    ohf = oh_bf[:].rearrange("p t e -> p (t e)")
                    mm(pvp[0][:, PLACE:PLACE + NT * E], before_bf[:], ohf, start=True, stop=False, skip_group_check=True)
                    for d in range(NT):
                        last = mm(pvp[0][:, PLACE + (d + 1) * E:PLACE + (NT + 1) * E], ones_bf[:], ohf[:, 0:(NT - d) * E],
                                  start=False, stop=(d == NT - 1), skip_group_check=True)
                    last.then_inc(s["pos_done"], 1)

            passes(pe, one)



def expert_program(nc, slots, tokens, w1, b1, w2, b2, sems):
    with ExitStack() as ctx:
        def sb(name, shape, dt=F32):
            return ctx.enter_context(nc.sbuf_tensor(name, shape, dt))

        def sem(name):
            return sems.enter_context(nc.semaphore(name))

        ident = sb("e_ident", [P, P])
        zeros = sb("e_zeros", [P, G, C])
        w1s = [sb(f"w1s{k}", [P, F]) for k in range(2)]
        w1h = sb("w1h", [P, F])
        w1p = [sb(f"w1p{k}", [P, 2, F], F32R) for k in range(2)]
        uh = sb("e_uh", [P, BLK])
        up = [sb(f"e_up{k}", [P, 2, BLK], F32R) for k in range(2)]
        w2s = [sb(f"w2s{k}", [P, FC, C]) for k in range(2)]
        b1c = [sb(f"b1c{k}", [P, FC]) for k in range(2)]
        b2r = [sb(f"b2r{k}", [P, C]) for k in range(2)]
        rows = [sb(f"e_rows{k}", [P, G, ROW]) for k in range(2)]
        kept = [sb(f"kept{k}", [P, G, ROW]) for k in range(2)]
        u = sb("e_u", [P, G, C])
        uT = [sb(f"e_uT{k}", [P, BLK]) for k in range(2)]
        hid = [sb(f"hid{k}", [P, BLK]) for k in range(4)]
        yb = sb("yb", [P, G, C])
        z = sb("z", [P, G, C])
        isnan = sb("isnan", [P, G, C], I32)
        isfin = sb("isfin", [P, G, C], I32)
        ysafe = sb("ysafe", [P, G, C])
        res = [sb(f"res{k}", [P, G, ROW]) for k in range(2)]
        tp = [ctx.enter_context(nc.psum_tensor(f"e_tp{k}", [P, BLK], F32)) for k in range(2)]
        hp = [ctx.enter_context(nc.psum_tensor(f"e_hp{k}", [P, BLK], F32)) for k in range(FC)]
        yp = [ctx.enter_context(nc.psum_tensor(f"e_yp{k}", [P, G, C], F32)) for k in range(2)]

        names = """e_const e_ident_ready e_u_ready e_turned e_uT_ready e_kept e_w1_high e_w1_parts e_u_parts
        e_hid_done e_hid_ready e_y_done e_yb_ready e_guard e_res_ready""".split()
        s = {n: sem(n) for n in names}
        passed = {n: sem(f"e_passed_{n}") for n in ("sp", "pool", "dve", "pe")}
        w_loaded, rows_loaded, stored = ([sem(f"e_{n}{k}") for k in range(2)] for n in ("w_loaded", "rows_loaded", "stored"))
        NBLKS = E * NBLK

        def blocks(eng, one):
            def pair(e, par, j, at):
                one(e * NBLK + j * 2, 0, par, e, at)
                one(e * NBLK + j * 2 + 1, 1, par, e, None if at is None else at + 1)

            def expert(e, par):
                pair(e, par, 0, 0)
                pair(e, par, 1, 2)
                with eng.Fori(2, NBLK // 2 - 1) as j:
                    pair(e, par, j, None)
                pair(e, par, NBLK // 2 - 1, NBLK - 2)
            expert(0, 0)
            expert(1, 1)
            with eng.Fori(1, E // 2 - 1) as i:
                expert(i * 2, 0)
                expert(i * 2 + 1, 1)
            expert(E - 2, 0)
            expert(E - 1, 1)

        def is_last(n):
            return isinstance(n, int) and n == NBLKS - 1

        def wait_rows(eng, n, half):
            eng.wait_ge(rows_loaded[half], n * 8 + (16 if half == 0 else 8))

        block = ctx.enter_context(nc.Block())

        @block.sync
        def _(sp):
            def load_w(e, par):
                for dst, src in ((w1s[par][:], w1[bass.ds(e, 1)].rearrange("o d f -> (o d) f")),
                                 (w2s[par][:], w2[bass.ds(e, 1)].rearrange("o (c p) d -> p (o c) d", p=P)),
                                 (b1c[par][:], b1[bass.ds(e, 1)].rearrange("o p c -> (o p) c")),
                                 (b2r[par][:], b2[bass.ds(e, 1)].rearrange("o d -> (o d)").partition_broadcast(P))):
                    sp.dma_start(dst, src).then_inc(w_loaded[par], 16)

            def load_rows(n, half):
                sp.dma_start(rows[half][:].rearrange("p g d -> p (g d)"),
                             slots[bass.ds(n * BLK, BLK)].rearrange("(p g) d -> p (g d)", p=P)).then_inc(rows_loaded[half], 16)

            load_rows(0, 0)
            load_w(0, 0)

            def one(n, half, par, e, at):
                if not is_last(n):
                    if not early(n, 1):
                        wait_apart(sp, s["e_kept"], n, passed["sp"])
                    load_rows(n + 1, 1 - half)
                if at == 0 and not (isinstance(e, int) and e == E - 1):
                    if not early(n, 1):
                        wait_apart(sp, s["e_y_done"], n, passed["sp"])
                        wait_apart(sp, s["e_yb_ready"], n * 2, passed["sp"])
                    load_w(e + 1, 1 - par)

            blocks(sp, one)

        @block.gpsimd
        def _(pool):
            g = nc.gpsimd
            g.memset(ident[:], 0.0).then_inc(s["e_const"], 1)
            pool.wait_ge(s["e_const"], 1)
            g.memset(zeros[:], 0.0).then_inc(s["e_const"], 1)
            g.affine_select(out=ident[:], in_=ident[:], pattern=[[-1, P]], compare_op=ALU.not_equal, fill=1.0,
                            base=0, channel_multiplier=1).then_inc(s["e_ident_ready"], 1)

            def store(n, half):
                wait_apart(pool, s["e_res_ready"], n + 1, passed["pool"])
                for q in range(G):
                    g.indirect_dma_start(out=tokens, out_offset=bass.IndirectOffsetOnAxis(
                        ap=res[half][:, q, TOKEN:TOKEN + 1].bitcast(I32), axis=0), in_=res[half][:, q, 0:C], in_offset=None,
                        bounds_check=T - 1, oob_is_err=False).then_inc(stored[half], 16)

            def one(n, half, par, e, at):
                if not early(n, 1):
                    store(n - 1, 1 - half)

            blocks(pool, one)
            store(NBLKS - 1, 1)

        @block.scalar
        def _(act):
            a = nc.scalar

            def prep(n, half, q0):
                if q0 == 0:
                    wait_rows(act, n, half)
                    if not early(n, 1):
                        act.wait_ge(s["e_turned"], n)
                for q in range(q0, q0 + 2):
                    last = a.activation(u[:, q, :], rows[half][:, q, 0:C], ACT.Identity,
                                        bias=rows[half][:, q, SHIFT:SHIFT + 1], scale=rows[half][:, q, RSTD:RSTD + 1])
                if q0 == 2:
                    last.then_inc(s["e_u_ready"], 1)

            def keep(n, half):
                wait_rows(act, n, half)
                if not early(n, 2):
                    act.wait_ge(s["e_res_ready"], n - 1)
                a.copy(kept[half][:], rows[half][:]).then_inc(s["e_kept"], 1)

            def turned(n, half):
                act.wait_ge(s["e_turned"], n + 1)
                if not early(n, 2):
                    act.wait_ge(s["e_u_parts"], n * 3 - 3)
                a.copy(uT[half][:], tp[half][:]).then_inc(s["e_uT_ready"], 1)

            def relu(n, f, par):
                act.wait_ge(s["e_hid_done"], n * FC + (f + 1))
                a.activation(hid[f][:], hp[f][:], ACT.Relu, bias=b1c[par][:, f:f + 1], scale=1.0)\
                    .then_inc(s["e_hid_ready"], 1)

            def one(n, half, par, e, at):
                more = not (isinstance(n, int) and n >= NBLKS - 2)
                if not is_last(n):
                    nxt = 1 - par if at == NBLK - 1 else par
                    turned(n + 1, 1 - half)
                relu(n, 2, par)
                relu(n, 3, par)
                if more:
                    prep(n + 2, half, 0)
                if not is_last(n):
                    relu(n + 1, 0, nxt)
                if more:
                    prep(n + 2, half, 2)
                if not is_last(n):
                    relu(n + 1, 1, nxt)
                    keep(n + 1, 1 - half)

            prep(0, 0, 0)
            prep(0, 0, 2)
            turned(0, 0)
            relu(0, 0, 0)
            relu(0, 1, 0)
            prep(1, 1, 0)
            prep(1, 1, 2)
            keep(0, 0)
            blocks(act, one)

        @block.vector
        def _(dve):
            v = nc.vector

            def w1_parts(e, par):
                dve.wait_ge(w_loaded[par], (e * 32 + 64) if par == 0 else (e * 32 + 32))
                if not early(e, 2):
                    dve.wait_ge(s["e_hid_done"], (e - 1) * (NBLK * FC))
                if not early(e, 1):
                    dve.wait_ge(s["e_w1_parts"], e * 2)
                v.tensor_scalar(w1h[:].bitcast(I32), w1s[par][:].bitcast(I32), HIGH_BITS, None, ALU.bitwise_and)\
                    .then_inc(s["e_w1_high"], 1)
                dve.wait_ge(s["e_w1_high"], e + 1)
                v.tensor_copy(w1p[par][:, 0, :], w1h[:]).then_inc(s["e_w1_parts"], 1)
                v.tensor_tensor(w1p[par][:, 1, :], w1s[par][:], w1h[:], ALU.subtract).then_inc(s["e_w1_parts"], 1)

            def u_parts(n, half):
                dve.wait_ge(s["e_uT_ready"], n + 1)
                if not early(n, 1):
                    dve.wait_ge(s["e_u_parts"], n * 3)
                v.tensor_scalar(uh[:].bitcast(I32), uT[half][:].bitcast(I32), HIGH_BITS, None, ALU.bitwise_and)\
                    .then_inc(s["e_u_parts"], 1)
                dve.wait_ge(s["e_u_parts"], n * 3 + 1)
                if not early(n, 2):
                    dve.wait_ge(s["e_hid_done"], n * FC - FC)
                v.tensor_copy(up[half][:, 0, :], uh[:]).then_inc(s["e_u_parts"], 1)
                v.tensor_tensor(up[half][:, 1, :], uT[half][:], uh[:], ALU.subtract).then_inc(s["e_u_parts"], 1)

            def result(n, half, par, between=None):
                dve.wait_ge(s["e_kept"], n + 1)
                dve.wait_ge(s["e_y_done"], n + 1)
                v.tensor_tensor(yb[:], yp[half][:], b2r[par][:].unsqueeze(1).to_broadcast([P, G, C]), ALU.add)\
                    .then_inc(s["e_yb_ready"], 1)
                dve.wait_ge(s["e_yb_ready"], n * 2 + 1)
                v.tensor_tensor(z[:], yb[:], kept[half][:, :, PROB:PROB + 1].to_broadcast([P, G, C]), ALU.mult)\
                    .then_inc(s["e_yb_ready"], 1)
                dve.wait_ge(s["e_yb_ready"], n * 2 + 2)
                v.tensor_scalar(ysafe[:], z[:], -NAN_CLIP, NAN_CLIP, ALU.max, ALU.min)
                v.tensor_tensor(isnan[:], z[:], z[:], ALU.not_equal)
                v.tensor_scalar(isfin[:], z[:], 0.0, 0.0, ALU.mult, ALU.is_equal).then_inc(s["e_guard"], 1)
                if between:
                    between()
                wait_apart(dve, s["e_guard"], n * 3 + 1, passed["dve"])
                v.copy_predicated(ysafe[:], isnan[:], zeros[:]).then_inc(s["e_guard"], 1)
                wait_apart(dve, s["e_guard"], n * 3 + 2, passed["dve"])
                v.copy_predicated(ysafe[:], isfin[:], z[:]).then_inc(s["e_guard"], 1)
                dve.wait_ge(s["e_guard"], n * 3 + 3)
                if not early(n, 2):
                    dve.wait_ge(stored[half], (n - half) * 32)
                v.tensor_copy(res[half][:, :, TOKEN:TOKEN + 1].bitcast(I32), kept[half][:, :, TOKEN:TOKEN + 1].bitcast(I32))
                v.tensor_tensor(res[half][:, :, 0:C], ysafe[:], kept[half][:, :, 0:C], ALU.add)\
                    .then_inc(s["e_res_ready"], 1)

            def one(n, half, par, e, at):
                def between():
                    if not is_last(n):
                        u_parts(n + 1, 1 - half)
                if early(n, 1):
                    between()
                else:
                    result(n - 1, 1 - half, 1 - par if at == 0 else par, between)
                if at == NBLK - 2 and not (isinstance(e, int) and e == E - 1):
                    w1_parts(e + 1, 1 - par)

            dve.wait_ge(s["e_ident_ready"], 1)
            w1_parts(0, 0)
            u_parts(0, 0)
            blocks(dve, one)
            result(NBLKS - 1, 1, 1)

        @block.tensor
        def _(pe):
            mm = nc.tensor.matmul
            pe.wait_ge(s["e_ident_ready"], 1)

            def turn(n, half):
                pe.wait_ge(s["e_u_ready"], n + 1)
                for q in range(G):
                    last = nc.tensor.transpose(tp[half][:, q * P:(q + 1) * P], u[:, q, :], ident[:])
                last.then_inc(s["e_turned"], 1)

            def layer1(n, half, par, f):
                if f == 0:
                    pe.wait_ge(s["e_u_parts"], n * 3 + 3)
                if not early(n, 1):
                    pe.wait_ge(s["e_hid_ready"], n * FC + (f + 1 - FC))
                wh, wl = (w1p[par][:, part, f * P:(f + 1) * P] for part in range(2))
                mm(hp[f][:], wh, up[half][:, 0, :], start=True, stop=False)
                mm(hp[f][:], wh, up[half][:, 1, :], start=False, stop=False)
                mm(hp[f][:], wl, up[half][:, 0, :], start=False, stop=True).then_inc(s["e_hid_done"], 1)

            def layer2(n, half, par, f):
                pe.wait_ge(s["e_hid_ready"], n * FC + (f + 1))
                if f == 0 and not early(n, 2):
                    pe.wait_ge(s["e_yb_ready"], n * 2 - 3)
                for q in range(G):
                    last = mm(yp[half][:, q, :], hid[f][:, q * P:(q + 1) * P], w2s[par][:, f, :],
                              start=(f == 0 and q == 0), stop=(f == FC - 1), skip_group_check=True)
                if f == FC - 1:
                    last.then_inc(s["e_y_done"], 1)

            def weights(e, par):
                pe.wait_ge(w_loaded[par], (e * 32 + 64) if par == 0 else (e * 32 + 32))
                pe.wait_ge(s["e_w1_parts"], e * 2 + 2)

            def one(n, half, par, e, at):
                layer2(n, half, par, 0)
                if not is_last(n):
                    turn(n + 1, 1 - half)
                layer1(n, half, par, 2)
                layer2(n, half, par, 1)
                layer1(n, half, par, 3)
                layer2(n, half, par, 2)
                nxt = 1 - par if at == NBLK - 1 else par
                if at == NBLK - 1 and not is_last(n):
                    weights(e + 1, nxt)
                if not is_last(n):
                    layer1(n + 1, 1 - half, nxt, 0)
                layer2(n, half, par, 3)
                if not is_last(n):
                    layer1(n + 1, 1 - half, nxt, 1)

            turn(0, 0)
            weights(0, 0)
            layer1(0, 0, 0, 0)
            layer1(0, 0, 0, 1)
            blocks(pe, one)

        @block.sync
        def _(sp):
            for k in range(2):
                sp.wait_ge(stored[k], NBLKS // 2 * G * 16)


def output_program(nc, tokens, out, sems):
    with ExitStack() as ctx:
        def sem(name):
            return sems.enter_context(nc.semaphore(name))

        ident = ctx.enter_context(nc.sbuf_tensor("f_ident", [P, P], F32))
        rows = [ctx.enter_context(nc.sbuf_tensor(f"f_rows{k}", [P, NT, C], F32)) for k in range(4)]
        cols = [ctx.enter_context(nc.sbuf_tensor(f"f_cols{k}", [P, N], F32)) for k in range(2)]
        ps = [ctx.enter_context(nc.psum_tensor(f"f_ps{k}", [P, 2, HALF], F32)) for k in range(2)]
        ident_set, ident_ready, turned, lo_ready, hi_ready = (sem(f"f_{n}") for n in
                                                              ("ident_set", "ident_ready", "turned", "lo_ready", "hi_ready"))
        loaded = [sem(f"f_loaded{k}") for k in range(4)]
        stored = [sem(f"f_stored{k}") for k in range(2)]
        passed = {"sp": sem("f_passed_sp")}
        R = 4
        block = ctx.enter_context(nc.Block())

        @block.sync
        def _(sp):
            def load(b, r):
                sp.dma_start(rows[r][:], tokens[bass.ds(b * N, N)].rearrange("(t p) c -> p t c", p=P)).then_inc(loaded[r], 16)
            for r in range(R):
                load(r, r)
            with sp.Fori(1, B // R) as i:
                for r in range(R):
                    wait_apart(sp, turned, i * R + (r + 1 - R), passed["sp"])
                    load(i * R + r, r)

        @block.gpsimd
        def _(pool):
            nc.gpsimd.memset(ident[:], 0.0).then_inc(ident_set, 1)
            pool.wait_ge(ident_set, 1)
            nc.gpsimd.affine_select(out=ident[:], in_=ident[:], pattern=[[-1, P]], compare_op=ALU.not_equal, fill=1.0,
                                    base=0, channel_multiplier=1).then_inc(ident_ready, 1)

        @block.tensor
        def _(pe):
            pe.wait_ge(ident_ready, 1)

            def one(i, r):
                pe.wait_ge(loaded[r], i * 16 + 16)
                if not (isinstance(i, int) and r < 2):
                    pe.wait_ge(lo_ready, i * R + (r - 1))
                    pe.wait_ge(hi_ready, i * R + (r - 1))
                for t in range(NT):
                    last = nc.tensor.transpose(ps[r % 2][:, t // 4, (t % 4) * P:(t % 4 + 1) * P], rows[r][:, t, :], ident[:])
                last.then_inc(turned, 1)
            for r in range(R):
                one(0, r)
            with pe.Fori(1, B // R) as i:
                for r in range(R):
                    one(i, r)

        @block.scalar
        def _(act):
            def one(i, r):
                act.wait_ge(turned, i * R + (r + 1))
                if not (isinstance(i, int) and r < 2):
                    act.wait_ge(stored[r % 2], i * 32 + (r // 2) * 16)
                nc.scalar.copy(cols[r % 2][:, 0:HALF], ps[r % 2][:, 0, :]).then_inc(lo_ready, 1)
                act.wait_ge(lo_ready, i * R + (r + 1))
                act.wait_ge(hi_ready, i * R + (r + 1))
                act.dma_start(out[bass.ds(i * R + r, 1)].rearrange("o c n -> (o c) n"), cols[r % 2][:]).then_inc(stored[r % 2], 16)
            for r in range(R):
                one(0, r)
            with act.Fori(1, B // R) as i:
                for r in range(R):
                    one(i, r)
            for k in range(2):
                act.wait_ge(stored[k], B // 2 * 16)

        @block.vector
        def _(dve):
            def one(i, r):
                dve.wait_ge(turned, i * R + (r + 1))
                if not (isinstance(i, int) and r < 2):
                    dve.wait_ge(stored[r % 2], i * 32 + (r // 2) * 16)
                nc.vector.tensor_copy(cols[r % 2][:, HALF:N], ps[r % 2][:, 1, :]).then_inc(hi_ready, 1)
            for r in range(R):
                one(0, r)
            with dve.Fori(1, B // R) as i:
                for r in range(R):
                    one(i, r)


def program(nc, a, out):
    slots = nc.dram_tensor("expert_slots", [E * CAP, ROW], F32, kind="Internal").ap()
    tokens = nc.dram_tensor("token_rows", [T, C], F32, kind="Internal").ap()
    with ExitStack() as sems:
        token_program(nc, a["x"], a["ln_w"], a["ln_b"], a["w_bcdt_t"], a["w_gw"], a["w_out_t"], a["A"], a["Wq"], a["bq"],
                      a["Wk"], a["bk"], a["Wv"], a["bv"], a["gamma"], a["beta"], a["gate_w"], a["gate_b"],
                      slots, tokens, sems)
        expert_program(nc, slots, tokens, a["w1"], a["b1"], a["w2"], a["b2"], sems)
        output_program(nc, tokens, out, sems)


def kernel(**inputs):
    import numpy as np
    import concourse.bacc as bacc
    from concourse.bass_utils import run_bass_kernel_spmd

    def get(name):
        return np.asarray(inputs[name])

    lay = {
        "x": get("x").reshape(B, C, N),
        "ln_w": get("L0_conv_ln_w").reshape(C, 1), "ln_b": get("L0_conv_ln_b").reshape(C, 1),
        "w_bcdt_t": get("L0_conv_w_bcdt").reshape(U, C).T, "w_gw": get("L0_conv_w_gw").reshape(U, 2, 9),
        "w_out_t": get("L0_conv_w_out").reshape(C, C).T, "A": get("L0_conv_A"),
        "Wq": get("L1_attn_Wq"), "bq": get("L1_attn_bq"), "Wk": get("L1_attn_Wk"), "bk": get("L1_attn_bk"),
        "Wv": get("L1_attn_Wv"), "bv": get("L1_attn_bv"), "gamma": get("L1_attn_gamma"), "beta": get("L1_attn_beta"),
        "gate_w": get("L1_ffn_gate_w"), "gate_b": get("L1_ffn_gate_b"), "w1": get("L1_ffn_w1"),
        "b1": get("L1_ffn_b1").reshape(E, FC, P).transpose(0, 2, 1),
        "w2": get("L1_ffn_w2"), "b2": get("L1_ffn_b2"),
    }
    nc = bacc.Bacc("TRN2", target_bir_lowering=False, num_devices=1)
    arrays = {f"in_{n}": np.ascontiguousarray(v) for n, v in lay.items()}
    args = {n: nc.dram_tensor(f"in_{n}", arrays[f"in_{n}"].shape, mybir.dt.from_np(arrays[f"in_{n}"].dtype),
                              kind="ExternalInput").ap() for n in lay}
    out = nc.dram_tensor("out", [B, C, N], F32, kind="ExternalOutput").ap()
    program(nc, args, out)
    r = run_bass_kernel_spmd(nc, [arrays], core_ids=[0])
    return r.results[0]["out"].reshape(B, C, H, W)
```
